# Optimizing a Trainium2 kernel written in Bass

```python
import numpy as np
import jax
import jax.numpy as jnp

def _softmax(x, axis=-1):
    return jax.nn.softmax(x, axis=axis)

def _gelu(x):
    return jax.nn.gelu(x, approximate=True)

def _silu(x):
    return jax.nn.silu(x)

def _sigmoid(x):
    return jax.nn.sigmoid(x)

def _layernorm(x, axis=-1, eps=1e-05):
    m = jnp.mean(x, axis=axis, keepdims=True)
    v = jnp.var(x, axis=axis, keepdims=True)
    return (x - m) / jnp.sqrt(v + eps)

def _scatter_add(tgt, idx, src, axis=0):
    return tgt.at[idx].add(src)

def _segment_sum(src, seg, n):
    return jax.ops.segment_sum(src, seg, n)
kernel_name = 'mk_gnn_preln_d4_gnn_r32_c55cc4'

def setup_inputs(seed: int=0):
    np.random.seed(seed)
    _w = jnp.asarray

    def _rec_inputs():
        import jax
        import jax.numpy as jnp
        _gk = jax.random.key(seed)
        x = -0.0003713 + 1 * jax.random.normal(jax.random.fold_in(_gk, 1), (3125, 128), jnp.float32)
        src = jax.random.randint(jax.random.fold_in(_gk, 2), (100000,), 0, 3125, jnp.int32)
        dst = jax.random.randint(jax.random.fold_in(_gk, 3), (100000,), 0, 3125, jnp.int32)
        _o = jnp.argsort(dst, stable=True)
        src = src[_o]
        dst = dst[_o]
        edge_type_5 = jax.random.randint(jax.random.fold_in(_gk, 12), (100000,), 0, 5, jnp.int32)
        return (x, src, dst, edge_type_5)
    x, src, dst, edge_type_5 = _rec_inputs()

    def _L0_gnn_setup():
        import jax, jax.numpy as jnp
        import numpy as np
        N_NODES = 3125
        N_EDGES = 50000
        D = 128
        R = 5
        L = 3

        def _rgcn_conv(h, src, dst, edge_types, W, root, bias):
            seg = dst * R + edge_types
            msg = h[src]
            sums = jax.ops.segment_sum(msg, seg, num_segments=N_NODES * R)
            sums = sums.reshape(N_NODES, R, -1)
            cnt = jax.ops.segment_sum(jnp.ones((src.shape[0],), h.dtype), seg, num_segments=N_NODES * R).reshape(N_NODES, R, 1)
            mean = sums / jnp.maximum(cnt, 1.0)
            return jnp.einsum('nrd,rde->ne', mean, W) + h @ root + bias
        key = jax.random.key(seed)
        ks = jax.random.split(key, 6)
        x = jax.random.normal(ks[0], (N_NODES, D), dtype=jnp.float32)
        edge_index = jax.random.randint(ks[1], (2, N_EDGES), 0, N_NODES, dtype=jnp.int32)
        edge_types = jax.random.randint(ks[2], (N_EDGES,), 0, R, dtype=jnp.int32)
        scale = 1.0 / np.sqrt(D).astype(np.float32)
        weights = jax.random.normal(ks[3], (L, R, D, D), dtype=jnp.float32) * scale
        roots = jax.random.normal(ks[4], (L, D, D), dtype=jnp.float32) * scale
        biases = jnp.zeros((L, D), dtype=jnp.float32)
        return {'x': x, 'edge_index': edge_index, 'edge_types': edge_types, 'weights': weights, 'roots': roots, 'biases': biases}
    _L0_gnn_all = _L0_gnn_setup()
    _L0_gnn_in = {k: v for k, v in _L0_gnn_all.items() if k in ('weights', 'roots', 'biases')}
    del _L0_gnn_all

    def _L1_gnn_setup():
        import jax, jax.numpy as jnp
        import numpy as np
        N_NODES = 50000
        N_EDGES = 25000
        D_IN = 128
        D_OUT = 128
        key = jax.random.key(seed)
        k1, k2, k3, k4, k5, k6 = jax.random.split(key, 6)
        curr_fea = jax.random.normal(k1, (N_NODES, D_IN), dtype=jnp.float32)
        edge_index = jax.random.randint(k2, (2, N_EDGES), 0, N_NODES, dtype=jnp.int64)
        s = 1.0 / np.sqrt(D_IN)
        W_self = jax.random.uniform(k3, (D_OUT, D_IN), jnp.float32, -s, s)
        b_self = jax.random.uniform(k4, (D_OUT,), jnp.float32, -s, s)
        W_neig = jax.random.uniform(k5, (D_OUT, D_IN), jnp.float32, -s, s)
        b_neig = jax.random.uniform(k6, (D_OUT,), jnp.float32, -s, s)
        return {'curr_fea': curr_fea, 'edge_index': edge_index, 'W_self': W_self, 'b_self': b_self, 'W_neig': W_neig, 'b_neig': b_neig}
    _L1_gnn_all = _L1_gnn_setup()
    _L1_gnn_in = {k: v for k, v in _L1_gnn_all.items() if k in ('W_self', 'b_self', 'W_neig', 'b_neig')}
    del _L1_gnn_all

    def _L2_gnn_setup():
        import jax, jax.numpy as jnp
        import numpy as np

        def _sage_conv(x, src, dst, W_l, b_l, W_r, num_nodes):
            msg = x[src]
            agg = jax.ops.segment_sum(msg, dst, num_segments=num_nodes)
            deg = jax.ops.segment_sum(jnp.ones_like(dst, dtype=x.dtype), dst, num_segments=num_nodes)
            mean = agg / jnp.maximum(deg, 1.0)[:, None]
            return mean @ W_l + b_l + x @ W_r
        key = jax.random.key(seed)
        ks = jax.random.split(key, 8)
        N, E, D = (50000, 20000, 128)
        s = 1.0 / np.sqrt(D)
        return {'x': jax.random.normal(ks[0], (N, D), dtype=jnp.float32), 'edge_index': jax.random.randint(ks[1], (2, E), 0, N, dtype=jnp.int64), 'W1_l': jax.random.normal(ks[2], (D, D), dtype=jnp.float32) * s, 'b1_l': jnp.zeros((D,), dtype=jnp.float32), 'W1_r': jax.random.normal(ks[3], (D, D), dtype=jnp.float32) * s, 'W2_l': jax.random.normal(ks[4], (D, D), dtype=jnp.float32) * s, 'b2_l': jnp.zeros((D,), dtype=jnp.float32), 'W2_r': jax.random.normal(ks[5], (D, D), dtype=jnp.float32) * s}
    _L2_gnn_all = _L2_gnn_setup()
    _L2_gnn_in = {k: v for k, v in _L2_gnn_all.items() if k in ('W1_l', 'b1_l', 'W1_r', 'W2_l', 'b2_l', 'W2_r')}
    del _L2_gnn_all

    def _L3_gnn_setup():
        import jax, jax.numpy as jnp
        import numpy as np
        EPS = 1e-07
        N_NODES, N_EDGES, D = (10000, 5000, 128)

        def mobius_add(x, y):
            x2 = jnp.sum(x * x, axis=-1, keepdims=True)
            y2 = jnp.sum(y * y, axis=-1, keepdims=True)
            xy = jnp.sum(x * y, axis=-1, keepdims=True)
            num = (1.0 + 2.0 * xy + y2) * x + (1.0 - x2) * y
            den = 1.0 + 2.0 * xy + x2 * y2
            return num / jnp.maximum(den, EPS)

        def mobius_scalar_mul(r, x):
            nrm = jnp.sqrt(jnp.sum(x * x, axis=-1, keepdims=True))
            nrm_c = jnp.clip(nrm, EPS, 1.0 - EPS)
            scaled = jnp.tanh(r * jnp.arctanh(nrm_c)) * (x / nrm_c)
            return jnp.where(nrm > EPS, scaled, jnp.zeros_like(x))
        key = jax.random.key(seed)
        kx, ke = jax.random.split(key)
        raw = jax.random.normal(kx, (N_NODES, D), dtype=jnp.float32)
        x = 0.4 * raw / (1.0 + jnp.linalg.norm(raw, axis=-1, keepdims=True))
        edge_index = jax.random.randint(ke, (2, N_EDGES), 0, N_NODES, dtype=jnp.int64)
        return {'x': x, 'edge_index': edge_index}
    _L3_gnn_all = _L3_gnn_setup()
    _L3_gnn_in = {k: v for k, v in _L3_gnn_all.items() if k in ()}
    del _L3_gnn_all
    return {'x': x, 'src': src, 'dst': dst, 'edge_type_5': edge_type_5, 'L0_gnn_weights': _L0_gnn_in['weights'], 'L0_gnn_roots': _L0_gnn_in['roots'], 'L0_gnn_biases': _L0_gnn_in['biases'], 'L1_gnn_W_self': _L1_gnn_in['W_self'], 'L1_gnn_b_self': _L1_gnn_in['b_self'], 'L1_gnn_W_neig': _L1_gnn_in['W_neig'], 'L1_gnn_b_neig': _L1_gnn_in['b_neig'], 'L2_gnn_W1_l': _L2_gnn_in['W1_l'], 'L2_gnn_b1_l': _L2_gnn_in['b1_l'], 'L2_gnn_W1_r': _L2_gnn_in['W1_r'], 'L2_gnn_W2_l': _L2_gnn_in['W2_l'], 'L2_gnn_b2_l': _L2_gnn_in['b2_l'], 'L2_gnn_W2_r': _L2_gnn_in['W2_r']}

def reference(x, src, dst, edge_type_5, L0_gnn_weights, L0_gnn_roots, L0_gnn_biases, L1_gnn_W_self, L1_gnn_b_self, L1_gnn_W_neig, L1_gnn_b_neig, L2_gnn_W1_l, L2_gnn_b1_l, L2_gnn_W1_r, L2_gnn_W2_l, L2_gnn_b2_l, L2_gnn_W2_r):
    import jax
    import jax.numpy as jnp

    def _L0_gnn_ref(x, edge_index, edge_types, weights, roots, biases):
        import jax, jax.numpy as jnp
        import numpy as np
        N_NODES = 3125
        N_EDGES = 50000
        D = 128
        R = 5
        L = 3

        def _rgcn_conv(h, src, dst, edge_types, W, root, bias):
            seg = dst * R + edge_types
            msg = h[src]
            sums = jax.ops.segment_sum(msg, seg, num_segments=N_NODES * R)
            sums = sums.reshape(N_NODES, R, -1)
            cnt = jax.ops.segment_sum(jnp.ones((src.shape[0],), h.dtype), seg, num_segments=N_NODES * R).reshape(N_NODES, R, 1)
            mean = sums / jnp.maximum(cnt, 1.0)
            return jnp.einsum('nrd,rde->ne', mean, W) + h @ root + bias
        src, dst = (edge_index[0], edge_index[1])
        h = x
        for l in range(L):
            h = _rgcn_conv(h, src, dst, edge_types, weights[l], roots[l], biases[l])
            if l < L - 1:
                h = jax.nn.relu(h)
        return h

    def _L1_gnn_ref(curr_fea, edge_index, W_self, b_self, W_neig, b_neig):
        import jax, jax.numpy as jnp
        import numpy as np
        N_NODES = 50000
        N_EDGES = 25000
        D_IN = 128
        D_OUT = 128
        num_nodes = curr_fea.shape[0]
        src, dst = (edge_index[0], edge_index[1])
        src_all = jnp.concatenate([src, dst], axis=0)
        dst_all = jnp.concatenate([dst, src], axis=0)
        nei_sum = jax.ops.segment_sum(curr_fea[src_all], dst_all, num_segments=num_nodes)
        out = curr_fea @ W_self.T + b_self + (nei_sum @ W_neig.T + b_neig)
        return out

    def _L2_gnn_ref(x, edge_index, W1_l, b1_l, W1_r, W2_l, b2_l, W2_r):
        import jax, jax.numpy as jnp
        import numpy as np

        def _sage_conv(x, src, dst, W_l, b_l, W_r, num_nodes):
            msg = x[src]
            agg = jax.ops.segment_sum(msg, dst, num_segments=num_nodes)
            deg = jax.ops.segment_sum(jnp.ones_like(dst, dtype=x.dtype), dst, num_segments=num_nodes)
            mean = agg / jnp.maximum(deg, 1.0)[:, None]
            return mean @ W_l + b_l + x @ W_r
        N = x.shape[0]
        src, dst = (edge_index[0], edge_index[1])
        h = jax.nn.relu(_sage_conv(x, src, dst, W1_l, b1_l, W1_r, N))
        z = _sage_conv(h, src, dst, W2_l, b2_l, W2_r, N)
        return z

    def _L3_gnn_ref(x, edge_index):
        import jax, jax.numpy as jnp
        import numpy as np
        EPS = 1e-07
        N_NODES, N_EDGES, D = (10000, 5000, 128)

        def mobius_add(x, y):
            x2 = jnp.sum(x * x, axis=-1, keepdims=True)
            y2 = jnp.sum(y * y, axis=-1, keepdims=True)
            xy = jnp.sum(x * y, axis=-1, keepdims=True)
            num = (1.0 + 2.0 * xy + y2) * x + (1.0 - x2) * y
            den = 1.0 + 2.0 * xy + x2 * y2
            return num / jnp.maximum(den, EPS)

        def mobius_scalar_mul(r, x):
            nrm = jnp.sqrt(jnp.sum(x * x, axis=-1, keepdims=True))
            nrm_c = jnp.clip(nrm, EPS, 1.0 - EPS)
            scaled = jnp.tanh(r * jnp.arctanh(nrm_c)) * (x / nrm_c)
            return jnp.where(nrm > EPS, scaled, jnp.zeros_like(x))
        src, dst = (edge_index[0], edge_index[1])
        n, d = x.shape
        messages = mobius_add(x[src], -x[dst])

        def body(out, em):
            m, idx = em
            return (out.at[idx].set(mobius_add(out[idx], m)), None)
        out0 = jnp.zeros((n, d), dtype=x.dtype)
        total, _ = jax.lax.scan(body, out0, (messages, dst))
        count = jnp.zeros((n,), dtype=x.dtype).at[dst].add(1.0)
        scale = 1.0 / jnp.maximum(count, 1.0)
        aggr = mobius_scalar_mul(scale[:, None], total)
        return mobius_add(x, aggr)
    edge_index = jnp.stack([src, dst])
    h = jnp.maximum(_layernorm(x, axis=-1), 0.0)
    x = x + _L0_gnn_ref(h, edge_index, edge_type_5, L0_gnn_weights, L0_gnn_roots, L0_gnn_biases)
    h = jnp.maximum(_layernorm(x, axis=-1), 0.0)
    x = x + _L1_gnn_ref(h, edge_index, L1_gnn_W_self, L1_gnn_b_self, L1_gnn_W_neig, L1_gnn_b_neig)
    h = jnp.maximum(_layernorm(x, axis=-1), 0.0)
    x = x + _L2_gnn_ref(h, edge_index, L2_gnn_W1_l, L2_gnn_b1_l, L2_gnn_W1_r, L2_gnn_W2_l, L2_gnn_b2_l, L2_gnn_W2_r)
    h = jnp.maximum(_layernorm(x, axis=-1), 0.0)
    x = x + _L3_gnn_ref(h, edge_index)
    return x

_drawn_inputs = setup_inputs


def setup_inputs(seed=0):
    import zlib

    import numpy as np

    out = dict(_drawn_inputs(seed))
    spreads = {'L0_gnn_biases': (0.0, 0.1), 'L2_gnn_b1_l': (0.0, 2.0), 'L2_gnn_b2_l': (0.0, 2.0)}
    factors = {'L1_gnn_W_self': 4.089, 'L1_gnn_b_self': 30.414, 'L1_gnn_b_neig': 26.494}
    for name, (base, spread) in spreads.items():
        noise = np.random.default_rng([zlib.crc32(name.encode()), seed]).standard_normal(out[name].shape)
        drawn = base * np.exp(spread * noise) if base else spread * noise
        out[name] = jnp.asarray(drawn.astype(out[name].dtype))
    for name, factor in factors.items():
        out[name] = (out[name] * factor).astype(out[name].dtype)
    return out
```

```python
from contextlib import ExitStack, contextmanager

import concourse.bass as bass
import numpy as np
from concourse import mybir

N = 3125
E = 100000
D = 128
R = 5
P = 128
T = -(-N // P)
LAST = N - (T - 1) * P
EP = 125
EC = E // EP
KB = 64
HC = 20
NB = 64
SB = (T + 1) // 2
C = R * T
BATCHES = 2 * T - 1
GN = 512
GB = GN // NB
GROUPS = -(-N // GN)
OH = 32
TYPE_BITS = 3
TW = D + 4
STEPS = 4
TILE_GROUPS = ((0, 13), (13, T))
EPS = 1e-5
BALL_EPS = 1e-7

DT = mybir.dt
FP, BF, I32 = DT.float32, DT.bfloat16, DT.int32
ALU = mybir.AluOpType
ACT = mybir.ActivationFunctionType
AX = mybir.AxisListType


@contextmanager
def stage(nc, prefix):
    sems = []
    with ExitStack() as ctx:
        def sb(name, shape, dtype):
            return ctx.enter_context(nc.sbuf_tensor(prefix + name, shape, dtype))

        def sem(name):
            sems.append(nc.alloc_semaphore(prefix + name))
            return sems[-1]

        yield sb, sem
    nc.clear_and_free_semaphores(sems)
    nc.all_engine_barrier()


def wait_apart(eng, sem, value):
    eng.wait_ge(sem, value)
    if not isinstance(value, int):
        eng.sem_inc(APART[0], 1)


APART = [None]


class Tally:

    def __init__(self, engine, sem, at=0):
        self.engine, self.sem, self.at, self.n = engine, sem, at, 0

    def __call__(self, instruction):
        self.at, self.n = self.at + 1, self.n + 1
        instruction.then_inc(self.sem, 1)
        return self.at

    def settle(self, at=None):
        self.engine.wait_ge(self.sem, self.at if at is None else at)

    def chain(self, instruction):
        self(instruction)
        self.settle()


def build(nc, A, upto=99):
    ctx = ExitStack()
    with ctx:
        def sb(name, shape, dtype):
            return ctx.enter_context(nc.sbuf_tensor(name, shape, dtype))

        def sem(name):
            return ctx.enter_context(nc.semaphore(name))

        def dram(name, shape, dtype):
            return nc.dram_tensor(name, shape, dtype, kind="Internal").ap()

        psum = [ctx.enter_context(nc.psum_tensor(f"bank{i}", [P, 512], FP)) for i in range(8)]

        edge_code = dram("edge_code", (E + KB, 1), I32)
        adj = dram("adj", (BATCHES * P, C * NB), BF)
        sum_adj = dram("sum_adj", (BATCHES * P, T * NB), BF)
        sum_adj_t = dram("sum_adj_t", (BATCHES * P, T * NB), BF)

        table = dram("table", (N, TW), FP)

        ident = sb("ident", [P, P], FP)
        ident_bf = sb("ident_bf", [P, P], BF)
        below = sb("below", [P, P], FP)
        ones = sb("ones", [P, P], FP)
        cnt = sb("cnt", [P, T, R], FP)
        deg = sb("deg", [P, T + 1], FP)
        rcnt = sb("rcnt", [P, T, R], FP)
        rdeg = sb("rdeg", [P, T], FP)
        first_edge = sb("first_edge", [P, T], I32)
        first_f = sb("first_f", [P, T], FP)

        APART[0] = nc.alloc_semaphore("waits_apart")
        preprocess(nc, A, locals())
        if upto >= 1:
            build_adjacency(nc, A, locals())

        x_sb = sb("x_sb", [P, T, D], FP)
        base = sb("base", [P, T, D], FP)
        parts = [sb(f"parts{i}", [P, T, 3, D], BF) for i in range(2)]
        one_col = sb("one_col", [P, T, 1], FP)
        w_rel = sb("w_rel", [P, 3 * R, D], FP)
        w_root = sb("w_root", [P, 3, D], FP)
        w_two = sb("w_two", [P, 4, D], FP)
        w_turned = sb("w_turned", [P, 2, D], FP)
        bias_0 = sb("bias_0", [P, 3, D], FP)
        bias_1 = sb("bias_1", [P, 2, D], FP)
        bias_2 = sb("bias_2", [P, 2, D], FP)

        m = locals()
        if upto >= 2:
            start_features(nc, A, m)
        layers = [
            dict(rels=R, streams=[adj], scale=rcnt, w=w_rel[:, 0:R], root=w_root[:, 1], bias=bias_0[:, 1], make_sum=True),
            dict(rels=R, streams=[adj], scale=rcnt, w=w_rel[:, R:2 * R], root=w_root[:, 2], bias=bias_0[:, 2]),
            dict(rels=R, streams=[adj], scale=rcnt, w=w_rel[:, 2 * R:3 * R], root=w_turned[:, 0], bias=bias_1[:, 0], norm=True),
            dict(rels=1, streams=[sum_adj, sum_adj_t], scale=one_col, w=w_turned[:, 1:2], root=w_two[:, 1], bias=bias_2[:, 0], norm=True),
            dict(rels=1, streams=[sum_adj], scale=rdeg, w=w_two[:, 0:1], root=w_two[:, 3], bias=bias_2[:, 1]),
            dict(rels=1, streams=[sum_adj], scale=rdeg, w=w_two[:, 2:3], root=None, bias=None, norm=True),
        ]
        for n, layer in enumerate(layers):
            if n == 5:
                table_sb = sb("table_sb", [P, T, TW], FP)
                m["table_sb"] = table_sb
            if upto >= 3 + n:
                conv_layer(nc, m, n, **layer)
            if n == 2 and upto >= 3 + n:
                transpose_sum(nc, m)
        if upto >= 9:
            gyro_sum(nc, A, m)


def preprocess(nc, A, m):
    psum, cnt, deg, rcnt, rdeg = m["psum"], m["cnt"], m["deg"], m["rcnt"], m["rdeg"]
    first_edge, first_f = m["first_edge"], m["first_f"]
    ident, ident_bf, below, ones = m["ident"], m["ident_bf"], m["below"], m["ones"]
    edge_code = m["edge_code"]
    with stage(nc, "p_") as (sb, sem):

        dst_e = sb("dst_e", [EP, EC], I32)
        src_e = sb("src_e", [EP, EC], I32)
        typ_e = sb("typ_e", [EP, EC], I32)
        low_i = sb("low_i", [EP, EC], I32)
        tile_i = sb("tile_i", [EP, EC], I32)
        code_i = sb("code_i", [EP, EC], I32)
        low_b = sb("low_bf", [EP, EC], BF)
        code_b = sb("code_b", [EP, EC], BF)
        zero_i = sb("zero_i", [1, KB], I32)
        count_to = sb("count_to", [EP, P, HC], BF)
        hot_low = sb("hot_low", [EP, 2, P, HC], BF)
        hot_code = sb("hot_code", [EP, 2, C, HC], BF)
        tot = sb("tot", [P, T], FP)
        upto_tile = sb("upto_tile", [P, T], FP)

        made, loaded, coded, stored = sem("made"), sem("loaded"), sem("coded"), sem("stored")
        hot, used = sem("hot"), sem("used")
        vec, deg_ready, prefix = sem("vec"), sem("deg"), sem("prefix")
        hist = psum[0][:, 0:C]
        total, lower = psum[1][:, 0:T], psum[2][:, 0:T]

        with nc.Block() as block:
            @block.sync
            def _(sync):
                sync.dma_start(dst_e[:, :], A["dst"].rearrange("(p c) -> p c", c=EC)).then_inc(loaded, 16)
                sync.dma_start(typ_e[:, :], A["edge_type_5"].rearrange("(p c) -> p c", c=EC)).then_inc(loaded, 16)
                sync.dma_start(src_e[:, :], A["src"].rearrange("(p c) -> p c", c=EC)).then_inc(loaded, 16)
                sync.wait_ge(coded, 1)
                sync.dma_start(edge_code[0:E, :].rearrange("(p c) o -> p (c o)", c=EC), src_e[:, :]).then_inc(stored, 16)
                sync.dma_start(edge_code[E:E + KB, :].rearrange("(a c) o -> a (c o)", a=1), zero_i[:, :]).then_inc(stored, 16)
                sync.wait_ge(stored, 32)

            @block.gpsimd
            def _(pool):
                pool.iota(count_to[:, :, :], [[1, P], [0, HC]], base=0, channel_multiplier=0,
                          allow_small_or_imprecise_dtypes=True).then_inc(made, 1)
                pool.memset(zero_i[:, :], 0).then_inc(made, 1)
                pool.memset(ident[:, :], 0.0).then_inc(made, 1)
                pool.memset(ident_bf[:, :], 0.0).then_inc(made, 1)
                pool.memset(below[:, :], 0.0).then_inc(made, 1)
                pool.memset(ones[:, :], 1.0).then_inc(made, 1)
                pool.memset(deg[:, T:T + 1], 0.0).then_inc(made, 1)
                pool.wait_ge(made, 7)
                for x in (ident, ident_bf):
                    pool.affine_select(out=x[:, :], in_=x[:, :], compare_op=ALU.not_equal, fill=1.0,
                                       base=0, pattern=[[-1, P]], channel_multiplier=1).then_inc(made, 1)
                pool.affine_select(out=below[:, :], in_=below[:, :], compare_op=ALU.is_ge, fill=1.0,
                                   base=0, pattern=[[-1, P]], channel_multiplier=1).then_inc(made, 1)

            @block.vector
            def _(dve):
                v = Tally(dve, vec)
                dve.wait_ge(loaded, 48)
                v(dve.tensor_scalar(low_i[:, :], dst_e[:, :], P - 1, None, ALU.bitwise_and))
                v(dve.tensor_scalar(tile_i[:, :], dst_e[:, :], 7, None, ALU.logical_shift_right))
                v.settle()
                v(dve.tensor_copy(low_b[:, :], low_i[:, :]))
                v(dve.scalar_tensor_tensor(code_b[:, :], tile_i[:, :], float(R), typ_e[:, :], ALU.mult, ALU.add))
                v.chain(dve.scalar_tensor_tensor(code_i[:, :], src_e[:, :], float(1 << TYPE_BITS), typ_e[:, :],
                                                 ALU.mult, ALU.add))
                dve.wait_ge(made, 2)
                dve.tensor_copy(src_e[:, :], code_i[:, :]).then_inc(coded, 1)

                def make_hot(col, step, slot, wait):
                    if wait:
                        dve.wait_ge(used, step - 1)
                    dve.tensor_tensor(hot_low[:, slot], count_to[:, :, :],
                                      low_b[:, bass.ds(col, HC)].unsqueeze(1).broadcast_to([EP, P, HC]),
                                      ALU.is_equal).then_inc(hot, 1)
                    dve.tensor_tensor(hot_code[:, slot], count_to[:, 0:C, :],
                                      code_b[:, bass.ds(col, HC)].unsqueeze(1).broadcast_to([EP, C, HC]),
                                      ALU.is_equal).then_inc(hot, 1)

                make_hot(0, 0, 0, False)
                make_hot(HC, 1, 1, False)
                with dve.Fori(1, EC // HC // 2) as i:
                    make_hot(i * (2 * HC), i * 2, 0, True)
                    make_hot(i * (2 * HC) + HC, i * 2 + 1, 1, True)
                dve.wait_ge(used, EC // HC)
                v(dve.tensor_copy(cnt[:, :, :], hist.rearrange("p (t r) -> p t r", r=R)))
                v.chain(dve.tensor_reduce(deg[:, 0:T], hist.rearrange("p (t r) -> p t r", r=R), AX.X, ALU.add))
                dve.wait_ge(vec, v.at)
                v(dve.tensor_scalar(rcnt[:, :, :], cnt[:, :, :], 1.0, None, ALU.max))
                v(dve.tensor_scalar(rdeg[:, :], deg[:, 0:T], 1.0, None, ALU.max))
                dve.tensor_copy(upto_tile[:, :], deg[:, 0:T]).then_inc(deg_ready, 1)
                v.settle()
                v(dve.reciprocal(rcnt[:, :, :], rcnt[:, :, :]))
                v(dve.reciprocal(rdeg[:, :], rdeg[:, :]))
                dve.wait_ge(prefix, 2)
                v.chain(dve.tensor_copy(tot[:, :], total))
                v.chain(dve.tensor_tensor_scan(upto_tile[:, :], ones[:, 0:T], tot[:, :], 0.0, ALU.mult, ALU.add))
                v.chain(dve.tensor_tensor(upto_tile[:, :], upto_tile[:, :], tot[:, :], ALU.subtract))
                v.chain(dve.tensor_tensor(first_f[:, :], upto_tile[:, :], lower, ALU.add))
                v.chain(dve.tensor_copy(first_edge[:, :], first_f[:, :]))

            @block.tensor
            def _(pe):
                def count(step, slot, begin=False, end=False):
                    pe.wait_ge(hot, step * 2 + 2)
                    for c in range(HC):
                        last = pe.matmul(hist, hot_low[:, slot, :, c], hot_code[:, slot, :, c],
                                         start=begin and c == 0, stop=end and c == HC - 1)
                    last.then_inc(used, 1)

                count(0, 0, begin=True)
                count(1, 1)
                with pe.Fori(1, EC // HC // 2 - 1) as i:
                    count(i * 2, 0)
                    count(i * 2 + 1, 1)
                count(EC // HC - 2, 0)
                count(EC // HC - 1, 1, end=True)
                pe.wait_ge(made, 10)
                pe.wait_ge(deg_ready, 1)
                pe.matmul(total, ones[:, :], upto_tile[:, :], start=True, stop=True).then_inc(prefix, 1)
                pe.matmul(lower, below[:, :], upto_tile[:, :], start=True, stop=True).then_inc(prefix, 1)


def build_adjacency(nc, A, m):
    psum, deg, first_edge, edge_code, adj = m["psum"], m["deg"], m["first_edge"], m["edge_code"], m["adj"]
    ident_bf = m["ident_bf"]
    with stage(nc, "b_") as (sb, sem):

        lists = sb("lists", [P, 2 * SB, KB], I32)
        low_l = sb("low_l", [P, 2 * SB, KB], I32)
        tile_l = sb("tile_l", [P, 2 * SB, KB], I32)
        rel_l = sb("rel_l", [P, 2 * SB, KB], I32)
        valid = sb("valid", [P, 2 * SB, KB], FP)
        slot_no = sb("slot_no", [P, KB], FP)
        low_n = sb("low_n", [P, 2 * SB, KB], BF)
        code_f = sb("code_f", [P, 2 * SB, KB], FP)
        code_n = sb("code_n", [P, 2 * SB, KB], BF)
        low_t = sb("low_t", [P, SB, P], BF)
        code_t = sb("code_t", [P, SB, P], BF)
        count_to = sb("count_to_b", [P, P, OH], BF)
        hot_low = sb("hot_low_b", [P, 2, P, OH], BF)
        hot_code = sb("hot_code_b", [P, 2, C, OH], BF)
        batch = sb("batch", [P, 2, 2, C, NB], BF)

        made, fetched, turned = sem("made"), sem("fetched"), sem("turned")
        turned_sb, hot, used = sem("turned_sb"), sem("hot"), sem("used")
        vec, by_act, by_dve = sem("vec"), sem("by_act"), sem("by_dve")
        store = [sem(f"store{h}") for h in range(2)]
        UNITS = 2 * OH // 4
        DVE_UNITS = (3, 8, 13)
        ACT_UNITS = tuple(u for u in range(UNITS) if u not in DVE_UNITS)
        LAST_DVE_UNITS = tuple(u for u in DVE_UNITS if u < 8)
        LAST_ACT_UNITS = tuple(u for u in ACT_UNITS if u < 8)
        turn_go, copied = sem("turn_go"), sem("copied")

        def evacuate(eng, s, k, units, first=False):
            q, h = k // 2, k % 2
            if h == 0 and not first:
                eng.wait_ge(store[q], s * 32)
            for u in units:
                before = s * 4 * UNITS + (k * UNITS if not (isinstance(s, int) and s == SB - 1) else k * (UNITS // 2))
                eng.wait_ge(used, before + (u + 1))
                at = h * OH + u % 8 * 4
                to = batch[:, q, u // 8, :, at:at + 4].rearrange("p c n -> p n c")
                of = psum[u % 8][:, 0:4 * C].rearrange("p (n c) -> p n c", c=C)
                if eng.engine == mybir.EngineType.DVE:
                    eng.tensor_copy(to, of).then_inc(by_dve, 1)
                else:
                    eng.activation(to, of, ACT.Copy).then_inc(by_act, 1)

        with nc.Block() as block:
            @block.gpsimd
            def _(pool):
                pool.iota(slot_no[:, :], [[1, KB]], base=0, channel_multiplier=0,
                          allow_small_or_imprecise_dtypes=True).then_inc(made, 1)
                pool.iota(count_to[:, :, :], [[1, P], [0, OH]], base=0, channel_multiplier=0,
                          allow_small_or_imprecise_dtypes=True).then_inc(made, 1)
                pool.memset(lists[:, T, :], 0).then_inc(made, 1)
                for t in range(T):
                    pool.indirect_dma_start(lists[:, t, :], None, edge_code,
                                            bass.IndirectOffsetOnAxis(first_edge[:, t:t + 1], 0)).then_inc(fetched, 16)

            @block.vector
            def _(dve):
                v = Tally(dve, vec)
                dve.wait_ge(made, 3)
                dve.wait_ge(fetched, 16 * T)
                v(dve.tensor_scalar(tile_l[:, :, :], lists[:, :, :], TYPE_BITS + 7, None, ALU.logical_shift_right))
                v(dve.tensor_scalar(rel_l[:, :, :], lists[:, :, :], (1 << TYPE_BITS) - 1, None, ALU.bitwise_and))
                v(dve.tensor_scalar(low_l[:, :, :], lists[:, :, :], TYPE_BITS, P - 1, ALU.logical_shift_right, ALU.bitwise_and))
                v(dve.tensor_tensor(valid[:, :, :], slot_no[:, :].unsqueeze(1).broadcast_to([P, 2 * SB, KB]),
                                    deg[:, :].unsqueeze(2).broadcast_to([P, 2 * SB, KB]), ALU.is_lt))
                v.settle()
                v(dve.scalar_tensor_tensor(code_f[:, :, :], rel_l[:, :, :], float(T), tile_l[:, :, :], ALU.mult, ALU.add))
                v(dve.tensor_copy(low_n[:, :, :], low_l[:, :, :]))
                v.settle()
                v.chain(dve.scalar_tensor_tensor(code_f[:, :, :], code_f[:, :, :], 1.0, valid[:, :, :], ALU.add, ALU.mult))
                v.chain(dve.tensor_scalar(code_n[:, :, :], code_f[:, :, :], -1.0, None, ALU.add))
                coded = v.at
                dve.nop().then_inc(turn_go, 1)
                for s in range(SB):
                    dve.wait_ge(turned, 2 * s + 2)
                    v(dve.tensor_copy(low_t[:, s, :], psum[2 * s % 8][:, 0:P // 2].bitcast(BF)))
                    dve.tensor_copy(code_t[:, s, :], psum[(2 * s + 1) % 8][:, 0:P // 2].bitcast(BF)).then_inc(copied, 1)
                v.settle()
                dve.wait_ge(copied, SB)

                def make_hot(step, s, k):
                    if not (isinstance(step, int) and step < 2):
                        dve.wait_ge(used, step * UNITS - UNITS)
                    at = k // 2 * NB + k % 2 * OH
                    for to, codes, n in ((hot_low, low_t, P), (hot_code, code_t, C)):
                        dve.tensor_tensor(to[:, k % 2], count_to[:, 0:n, :],
                                          codes[:, bass.ds(s, 1), at:at + OH].broadcast_to([P, n, OH]),
                                          ALU.is_equal).then_inc(hot, 1)

                def four_steps(s, first=False):
                    for k in range(4):
                        make_hot(s * 4 + (k + 1), s + (k + 1) // 4, (k + 1) % 4)
                        evacuate(dve, s, k, DVE_UNITS, first)

                make_hot(0, 0, 0)
                four_steps(0, True)
                with dve.Fori(1, SB - 1) as s:
                    four_steps(s)
                make_hot((SB - 1) * 4 + 1, SB - 1, 1)
                for k in range(2):
                    evacuate(dve, SB - 1, k, LAST_DVE_UNITS)

            @block.scalar
            def _(act):
                for k in range(4):
                    evacuate(act, 0, k, ACT_UNITS, True)
                with act.Fori(1, SB - 1) as s:
                    for k in range(4):
                        evacuate(act, s, k, ACT_UNITS)
                for k in range(2):
                    evacuate(act, SB - 1, k, LAST_ACT_UNITS)

            @block.tensor
            def _(pe):
                pe.wait_ge(turn_go, 1)
                for s in range(SB):
                    if s >= 4:
                        pe.wait_ge(copied, s - 3)
                    for n, x in enumerate((low_n, code_n)):
                        pe.transpose(psum[(2 * s + n) % 8][:, 0:P // 2].bitcast(BF),
                                     x[:, 2 * s:2 * s + 2, :].rearrange("p t k -> p (t k)"),
                                     ident_bf[:, :]).then_inc(turned, 1)
                pe.wait_ge(copied, SB)

                def count(s, k, units, first=False):
                    step = s * 4 + k
                    pe.wait_ge(hot, step * 2 + 2)
                    for u in range(units):
                        if not (first and k == 0 and u < 8):
                            if u < 8:
                                last_u = u + 8 if not (isinstance(s, int) and s == SB - 1 and k == 1) else u
                                short = isinstance(s, int) and s == SB - 1 and k == 1
                                done = ((LAST_DVE_UNITS, LAST_ACT_UNITS) if short else (DVE_UNITS, ACT_UNITS))
                                dve_one = last_u in done[0]
                                sem_, mine, per = (by_dve, done[0], len(DVE_UNITS)) if dve_one else (by_act, done[1], len(ACT_UNITS))
                                pe.wait_ge(sem_, (step - 1) * per + (mine.index(last_u) + 1))
                            else:
                                last_u = u - 8
                                sem_, mine = (by_dve, DVE_UNITS) if last_u in DVE_UNITS else (by_act, ACT_UNITS)
                                pe.wait_ge(sem_, step * len(mine) + (mine.index(last_u) + 1))
                        j = u // 8
                        rows = slice(j * KB, j * KB + KB)
                        for n in range(4):
                            i = u % 8 * 4 + n
                            last = pe.matmul(psum[u % 8][:, n * C:n * C + C], hot_low[rows, k % 2, :, i],
                                             hot_code[rows, k % 2, :, i], start=True, stop=True)
                        last.then_inc(used, 1)

                for k in range(4):
                    count(0, k, UNITS, True)
                with pe.Fori(1, SB - 1) as s:
                    for k in range(4):
                        count(s, k, UNITS)
                for k in range(2):
                    count(SB - 1, k, UNITS // 2)

            @block.sync
            def _(sync):
                def put(s, q, tiles=2):
                    step = s * 4 + (q * 2 + 2)
                    if tiles == 2:
                        wait_apart(sync, by_dve, step * len(DVE_UNITS))
                        wait_apart(sync, by_act, step * len(ACT_UNITS))
                    else:
                        sync.wait_ge(by_dve, (SB - 1) * 4 * len(DVE_UNITS) + 2 * len(LAST_DVE_UNITS))
                        sync.wait_ge(by_act, (SB - 1) * 4 * len(ACT_UNITS) + 2 * len(LAST_ACT_UNITS))
                    for j in range(tiles):
                        sync.dma_start(adj[bass.ds(s * (4 * P) + (2 * j + q) * P, P), :],
                                       batch[:, q, j].rearrange("p c n -> p (c n)")).then_inc(store[q], 16)

                with sync.Fori(0, SB - 1) as s:
                    for q in range(2):
                        put(s, q)
                put(SB - 1, 0, 1)
                sync.wait_ge(store[0], 32 * (SB - 1) + 16)
                sync.wait_ge(store[1], 32 * (SB - 1))


def layer_norm(dve, v, x, stats, mean_var, tiles):
    for t in range(tiles):
        v(dve.bn_stats(stats[:, t, :], x[:, t, :]))
    wait_apart(dve, v.sem, v.at)
    for t in range(tiles):
        v(dve.bn_aggr(mean_var[:, t, :], stats[:, t, :]))
    v.settle()


def split(dve, v, parts, h, rest):
    v.chain(dve.tensor_copy(parts[:, :, 0, :], h))
    v.chain(dve.tensor_tensor(rest, h, parts[:, :, 0, :], ALU.subtract))
    v.chain(dve.tensor_copy(parts[:, :, 1, :], rest))
    v.chain(dve.tensor_tensor(parts[:, :, 2, :], rest, parts[:, :, 1, :], ALU.subtract))


def start_features(nc, A, m):
    x_sb, base, parts, psum, ident = m["x_sb"], m["base"], m["parts"], m["psum"], m["ident"]
    with stage(nc, "f_") as (sb, sem):

        stats = sb("stats", [P, T, 6], FP)
        mean_var = sb("mean_var", [P, T, 2], FP)
        deviation = sb("deviation", [P, T], FP)
        rstd = sb("rstd", [P, T], FP)
        shift = sb("shift", [P, T], FP)
        h = sb("h", [P, T, D], FP)
        rest = sb("rest", [P, T, D], FP)
        h_t = sb("h_t", [P, T, P], FP)
        w_pair = sb("w_pair", [P, 2, D], FP)
        xs, ws, vec, dev, scaled, normed = (sem(f"{n}") for n in ("xs", "ws", "vec", "dev", "scaled", "normed"))
        turned, copied, rooted, added = (sem(f"{n}") for n in ("turned", "copied", "rooted", "added"))
        cleared, w_turns, w_copied = sem("cleared"), sem("w_turns"), sem("w_copied")
        QUADS = -(-T // 4)

        with nc.Block() as block:
            @block.sync
            def _(sync):
                x = A["x"]
                full = (T - 1) * P
                for q in range(2):
                    sync.dma_start(x_sb[:, 12 * q:12 * q + 12, :],
                                   x[12 * P * q:12 * P * (q + 1), :].rearrange("(t p) d -> p t d", p=P)).then_inc(xs, 16)
                sync.wait_ge(cleared, 1)
                sync.dma_start(x_sb[0:LAST, T - 1, :], x[full:N, :]).then_inc(xs, 16)
                sync.dma_start(m["w_root"][:, :, :], A["L0_gnn_roots"].rearrange("l d e -> d l e")).then_inc(ws, 16)
                sync.dma_start(m["w_rel"][:, :, :], A["L0_gnn_weights"].rearrange("l r d e -> d (l r) e")).then_inc(ws, 16)
                sync.wait_ge(ws, 16 * 13)

            @block.scalar
            def _(act):
                act.dma_start(m["bias_0"][:, :, :], A["L0_gnn_biases"].unsqueeze(0).broadcast_to([P, 3, D])).then_inc(ws, 16)
                for n, name in enumerate(("L1_gnn_W_self", "L1_gnn_W_neig")):
                    act.dma_start(w_pair[:, n, :], A[name]).then_inc(ws, 16)
                for n, name in enumerate(("L2_gnn_W1_l", "L2_gnn_W1_r", "L2_gnn_W2_l", "L2_gnn_W2_r")):
                    act.dma_start(m["w_two"][:, n, :], A[name]).then_inc(ws, 16)
                for to, name in ((m["bias_1"][:, 0], "L1_gnn_b_self"), (m["bias_1"][:, 1], "L1_gnn_b_neig"),
                                 (m["bias_2"][:, 0], "L2_gnn_b1_l"), (m["bias_2"][:, 1], "L2_gnn_b2_l")):
                    act.dma_start(to, A[name].unsqueeze(0).broadcast_to([P, D])).then_inc(ws, 16)
                act.wait_ge(dev, 1)
                act.activation(deviation[:, :], deviation[:, :], ACT.Sqrt).then_inc(dev, 1)
                act.wait_ge(scaled, 1)
                for t in range(T):
                    act.activation(h[:, t, :], x_sb[:, t, :], ACT.Relu, scale=rstd[:, t:t + 1],
                                   bias=shift[:, t:t + 1]).then_inc(normed, 1)
                for q in range(QUADS):
                    n = min(4, T - 4 * q)
                    act.wait_ge(turned, q + 1)
                    act.activation(h_t[:, 4 * q:4 * q + n, :], psum[q % 4][:, 0:n * P].rearrange("p (t n) -> p t n", n=P),
                                   ACT.Copy).then_inc(copied, 1)
                act.wait_ge(w_turns, 2)
                act.activation(m["w_turned"][:, :, :], psum[7][:, 0:2 * P].rearrange("p (t n) -> p t n", n=P),
                               ACT.Copy).then_inc(w_copied, 1)

            @block.vector
            def _(dve):
                v = Tally(dve, vec)
                dve.memset(x_sb[:, T - 1, :], 0.0).then_inc(cleared, 1)
                v(dve.memset(m["one_col"][:, :, :], 1.0))
                dve.wait_ge(xs, 48)
                layer_norm(dve, v, x_sb, stats, mean_var, T)
                dve.tensor_scalar(deviation[:, :], mean_var[:, :, 1], EPS, None, ALU.add).then_inc(dev, 1)
                dve.wait_ge(dev, 2)
                v.chain(dve.reciprocal(rstd[:, :], deviation[:, :]))
                dve.scalar_tensor_tensor(shift[:, :], mean_var[:, :, 0], -1.0, rstd[:, :], ALU.mult, ALU.mult).then_inc(scaled, 1)
                dve.wait_ge(normed, T)
                split(dve, v, parts[0][:, :, :, :], h[:, :, :], rest[:, :, :])
                dve.wait_ge(ws, 16 * 13)
                for q in range(QUADS):
                    n = min(4, T - 4 * q)
                    dve.wait_ge(rooted, q + 1)
                    dve.tensor_tensor(base[:, 4 * q:4 * q + n, :],
                                      psum[4 + q % 2][:, 0:n * D].rearrange("p (t n) -> p t n", n=D),
                                      m["bias_0"][:, 0:1, :].broadcast_to([P, n, D]), ALU.add).then_inc(added, 1)
                v(dve.tensor_tensor(m["bias_1"][:, 0], m["bias_1"][:, 0], m["bias_1"][:, 1], ALU.add))

            @block.tensor
            def _(pe):
                pe.wait_ge(normed, T)
                for q in range(QUADS):
                    n = min(4, T - 4 * q)
                    if q >= 4:
                        pe.wait_ge(copied, q - 3)
                    for t in range(n):
                        last = pe.transpose(psum[q % 4][:, t * P:t * P + P], h[:, 4 * q + t, :], ident[:, :])
                    last.then_inc(turned, 1)
                pe.wait_ge(ws, 16 * 13)
                for n in range(2):
                    pe.transpose(psum[7][:, n * P:n * P + P], w_pair[:, n, :], ident[:, :]).then_inc(w_turns, 1)
                for q in range(QUADS):
                    n = min(4, T - 4 * q)
                    pe.wait_ge(copied, q + 1)
                    if q >= 2:
                        pe.wait_ge(added, q - 1)
                    for t in range(n):
                        last = pe.matmul(psum[4 + q % 2][:, t * D:t * D + D], h_t[:, 4 * q + t, :],
                                         m["w_root"][:, 0, :], start=True, stop=True)
                    last.then_inc(rooted, 1)


HALVES = ((0, 13), (13, T))
HW = 13


def conv_layer(nc, m, number, rels, streams, scale, w, root, bias, norm=False, make_sum=False):
    psum, ident, base, x_sb = m["psum"], m["ident"], m["base"], m["x_sb"]
    now, then = m["parts"][number % 2], m["parts"][1 - number % 2]
    per_body = 1 if rels > 1 else 2
    spb = per_body * rels
    BANK, BACK = ((0, 1, 0, 1, 2), (3, 3, 2, 2, 5)) if rels == 5 else ((0, 1), (2, 2))
    S = len(streams)
    halves = 2 * S
    slots = 5 if rels == 5 else 4
    with stage(nc, f"l{number}_") as (sb, sem):

        slot = [sb(f"slot{i}", [P, GB, HW * NB], BF) for i in range(slots)]
        sums = [sb(f"sums{i}", [P, GN], FP) for i in range(3)]
        acc = sb("acc", [P, 4, D], FP)
        hbuf = [sb(f"h{i}", [P, 4, D], FP) for i in range(2)]
        rest = sb("rest", [P, 4, D], FP)
        h_t = sb("h_t", [P, GN], FP)
        stats = sb("stats", [P, 4, 6], FP)
        mean_var = sb("mean_var", [P, 4, 2], FP)
        deviation = sb("deviation", [P, 4], FP)
        rstd = sb("rstd", [P, 4], FP)
        shift = sb("shift", [P, 4], FP)
        total = [sb(f"total{i}", [P, GB, HW * NB], BF) for i in range(2)] if make_sum else None

        arrived = [sem(f"arrived{i}") for i in range(slots)]
        half_done, sums_copied, w_done, acc_done = sem("half_done"), sem("sums_copied"), sem("w_done"), sem("acc_done")
        h_done, turned, h_copied, based, base_added = (sem(n) for n in ("h_done", "turned", "h_copied", "based", "base_added"))
        vec, var_done, dev_done, scaled, summed, total_out = (
            sem(n) for n in ("vec", "var_done", "dev_done", "scaled", "summed", "total_out"))

        act_norm, acc_read = sem("act_norm"), sem("acc_read")
        if norm:
            h_done_of = lambda g: (act_norm, g * 4 + size(g)[1])
        else:
            h_done_of = lambda g: (acc_read, g + 1)

        def added(seq):
            full = (GROUPS - 1) * rels
            return full * 4 + seq - full if isinstance(seq, int) and seq > full else seq * 4

        def is_past(value):
            return not isinstance(value, int) or value > 0

        def wait(eng, s, value):
            if is_past(value):
                eng.wait_ge(s, value)

        def size(g):
            return (1, 1) if isinstance(g, int) and g == GROUPS - 1 else (GB, 4)

        def bodies(eng, body):
            body(0, False)
            if rels > 1:
                with eng.Fori(1, GROUPS - 1) as i:
                    body(i, False)
            else:
                body(1, False)
                body(2, False)
            body((GROUPS - 1) // per_body, True)

        def products(i, last):
            for b in range(rels if last else spb):
                yield i * spb + b, b, i * per_body + b // rels, b % rels

        def tiles_of(g, k):
            return bass.ds(g * 4, k)

        def slot_of(g):
            return slot_by_group[0]

        slot_by_group = [0]

        def schedule(eng, at_seq, after_seq, turn, root_product):
            def behind(i, b, back):
                q = b - back
                body_i = i
                while q < 0:
                    q, body_i = q + spb, body_i - 1
                if isinstance(i, int) and body_i < 0:
                    return None
                return body_i * spb + q, q, body_i * per_body + q // rels, q % rels

            def ended(i, b, back):
                p = behind(i, b, back)
                if p is None or p[3] != rels - 1:
                    return None
                slot_by_group[0] = p[1] // rels
                return p[2]

            def body(i, last):
                for seq, b, g, r in products(i, last):
                    at_seq(i, seq, b, g)
                    p = behind(i, b, 1)
                    if p is not None:
                        after_seq(*p)
                    if root is not None:
                        g2 = ended(i, b, 2)
                        if g2 is not None:
                            turn(g2)
                        g3 = ended(i, b, 3)
                        if g3 is not None:
                            root_product(g3)
                if last:
                    end = rels
                    for b in range(end, end + 3):
                        if b == end:
                            after_seq(*behind(i, b, 1))
                        if root is not None:
                            for back, what in ((2, turn), (3, root_product)):
                                if b - back < end:
                                    gx = ended(i, b, back)
                                    if gx is not None:
                                        what(gx)
            bodies(eng, body)

        with nc.Block() as block:
            @block.sync
            def _(sync):
                def body(i, last):
                    for seq, b, g, r in products(i, last):
                        n, _ = size(g)
                        for k in range(halves):
                            hb = b * halves + k
                            here = i * (spb * halves) + hb
                            if is_past(here - slots + 1):
                                wait_apart(sync, half_done, here - slots + 1)
                                if make_sum:
                                    wait_apart(sync, summed, here - slots + 1)
                            a0, a1 = HALVES[k % 2]
                            of = streams[k // 2].rearrange("(b p) c -> p b c", p=P)
                            sync.dma_start(slot[hb % slots][:, 0:n, 0:(a1 - a0) * NB],
                                           of[:, bass.ds(g * GB, n), (r * T + a0) * NB:(r * T + a1) * NB]) \
                                .then_inc(arrived[hb % slots], 16)
                bodies(sync, body)

            @block.tensor
            def _(pe):
                def aggregate(i, seq, b, g):
                    n, _ = size(g)
                    bank = psum[BANK[b]][:, 0:n * NB].rearrange("p (b n) -> p b n", n=NB)
                    wait(pe, sums_copied, seq - BACK[b] + 1)
                    for k in range(halves):
                        hb = b * halves + k
                        pe.wait_ge(arrived[hb % slots],
                                   i * (spb * halves // slots * 16) + (hb // slots + 1) * 16)
                        a0, a1 = HALVES[k % 2]
                        for a in range(a0, a1):
                            for part in range(3):
                                one = pe.matmul(bank, now[:, a, part, :],
                                                slot[hb % slots][:, 0:n, (a - a0) * NB:(a - a0 + 1) * NB],
                                                start=(k == 0 and a == 0 and part == 0),
                                                stop=(k == halves - 1 and a == T - 1 and part == 2))
                        one.then_inc(half_done, 1)

                def weigh(seq, b, g, r):
                    _, k = size(g)
                    pe.wait_ge(sums_copied, seq + 1)
                    wait(pe, acc_done, added(seq - BACK[b] + 1))
                    for t in range(k):
                        one = pe.matmul(psum[3 + BANK[b]][:, t * D:t * D + D], sums[BANK[b]][:, t * P:t * P + P],
                                        w[:, r, :], start=True, stop=True)
                    one.then_inc(w_done, 1)

                def turn(g):
                    _, k = size(g)
                    pe.wait_ge(*h_done_of(g))
                    wait(pe, h_copied, g)
                    for t in range(k):
                        one = pe.transpose(psum[6][:, t * P:t * P + P], hbuf[slot_of(g)][:, t, :], ident[:, :])
                    one.then_inc(turned, 1)

                def root_product(g):
                    _, k = size(g)
                    pe.wait_ge(h_copied, g + 1)
                    wait(pe, base_added, g)
                    for t in range(k):
                        one = pe.matmul(psum[7][:, t * D:t * D + D], h_t[:, t * P:t * P + P], root,
                                        start=True, stop=True)
                    one.then_inc(based, 1)

                schedule(pe, aggregate, weigh, turn, root_product)

            @block.scalar
            def _(act):
                def copy_sums(i, seq, b, g):
                    n, k = size(g)
                    act.wait_ge(half_done, (seq + 1) * halves)
                    wait(act, w_done, seq - BACK[b] + 1)
                    act.activation(sums[BANK[b]][:, 0:n * NB], psum[BANK[b]][:, 0:n * NB], ACT.Copy) \
                        .then_inc(sums_copied, 1)

                def normalise(seq, b, g, r):
                    if not norm or r != rels - 1:
                        return
                    _, k = size(g)
                    act.wait_ge(var_done, g + 1)
                    act.activation(deviation[:, 0:k], deviation[:, 0:k], ACT.Sqrt).then_inc(dev_done, 1)
                    act.wait_ge(scaled, g + 1)
                    for t in range(k):
                        act.activation(m["table_sb"][:, tiles_of(g, k), 0:D][:, t, :] if root is None else hbuf[b // rels][:, t, :],
                                       x_sb[:, tiles_of(g, k), :][:, t, :], ACT.Relu, scale=rstd[:, t:t + 1],
                                       bias=shift[:, t:t + 1]).then_inc(act_norm, 1)

                def copy_turned(g):
                    _, k = size(g)
                    act.wait_ge(turned, g + 1)
                    wait(act, based, g)
                    act.activation(h_t[:, 0:k * P], psum[6][:, 0:k * P], ACT.Copy).then_inc(h_copied, 1)

                schedule(act, copy_sums, normalise, copy_turned, lambda g: None)

            @block.vector
            def _(dve):
                per_step = (9 if norm else 0) + (4 if root is not None else 0)

                def begin(i, seq, b, g):
                    if not make_sum:
                        return
                    r = b
                    n, _ = size(g)
                    for k in range(halves):
                        hb = b * halves + k
                        dve.wait_ge(arrived[hb % slots],
                                    i * (spb * halves // slots * 16) + (hb // slots + 1) * 16)
                        a0, a1 = HALVES[k]
                        to, of = total[k][:, 0:n, 0:(a1 - a0) * NB], slot[hb % slots][:, 0:n, 0:(a1 - a0) * NB]
                        if r == 0:
                            wait(dve, total_out, g * 32)
                            dve.tensor_copy(to, of).then_inc(summed, 1)
                        else:
                            dve.wait_ge(summed, i * (spb * halves) + hb - 1)
                            dve.tensor_tensor(to, to, of, ALU.add).then_inc(summed, 1)

                def add(seq, b, g, r):
                    _, k = size(g)
                    dve.wait_ge(w_done, seq + 1)
                    if r:
                        dve.wait_ge(acc_done, added(seq))
                    else:
                        wait(dve, acc_read, g)
                    for t in range(k):
                        dve.scalar_tensor_tensor(
                            acc[:, t, :], psum[3 + BANK[b]][:, t * D:t * D + D],
                            scale[:, tiles_of(g, k), r][:, t:t + 1] if len(scale.shape) == 3 else scale[:, tiles_of(g, k)][:, t:t + 1],
                            acc[:, t, :] if r else base[:, tiles_of(g, k), :][:, t, :],
                            ALU.mult, ALU.add).then_inc(acc_done, 1)
                    if r != rels - 1:
                        return
                    dve.wait_ge(acc_done, added(seq + 1))
                    mine = hbuf[b // rels]
                    if root is not None:
                        wait(dve, turned, g - per_body + 1)
                    v = Tally(dve, vec, g * per_step)
                    start = v.at
                    if norm:
                        xs = x_sb[:, tiles_of(g, k), :]
                        dve.tensor_tensor(xs, xs, acc[:, 0:k, :], ALU.add).then_inc(acc_read, 1)
                        wait_apart(dve, acc_read, g + 1)
                        layer_norm(dve, v, xs, stats, mean_var, k)
                        dve.tensor_scalar(deviation[:, 0:k], mean_var[:, 0:k, 1], EPS, None, ALU.add).then_inc(var_done, 1)
                        dve.wait_ge(dev_done, g + 1)
                        v.chain(dve.reciprocal(rstd[:, 0:k], deviation[:, 0:k]))
                        dve.scalar_tensor_tensor(shift[:, 0:k], mean_var[:, 0:k, 0], -1.0, rstd[:, 0:k],
                                                 ALU.mult, ALU.mult).then_inc(scaled, 1)
                        dve.wait_ge(act_norm, g * 4 + k)
                    else:
                        dve.tensor_scalar(mine[:, 0:k, :], acc[:, 0:k, :], 0.0, None, ALU.max).then_inc(acc_read, 1)
                        dve.wait_ge(acc_read, g + 1)
                    if root is not None:
                        v.chain(dve.tensor_copy(then[:, tiles_of(g, k), 0, :], mine[:, 0:k, :]))
                        v.chain(dve.tensor_tensor(rest[:, 0:k, :], mine[:, 0:k, :], then[:, tiles_of(g, k), 0, :], ALU.subtract))
                        v.chain(dve.tensor_copy(then[:, tiles_of(g, k), 1, :], rest[:, 0:k, :]))
                        v.chain(dve.tensor_tensor(then[:, tiles_of(g, k), 2, :], rest[:, 0:k, :],
                                                  then[:, tiles_of(g, k), 1, :], ALU.subtract))
                    if k == 4 and isinstance(start, int):
                        assert v.at - start == per_step

                def add_base(g):
                    _, k = size(g)
                    dve.wait_ge(based, g + 1)
                    dve.tensor_tensor(base[:, tiles_of(g, k), :],
                                      psum[7][:, 0:k * D].rearrange("p (t d) -> p t d", d=D),
                                      bias.unsqueeze(1).broadcast_to([P, k, D]), ALU.add).then_inc(base_added, 1)

                schedule(dve, begin, add, lambda g: None, add_base)

            if make_sum:
                @block.gpsimd
                def _(pool):
                    def body(i, last):
                        n, _ = size(i)
                        pool.wait_ge(summed, i * 10 + 10)
                        for k, (a0, a1) in enumerate(HALVES):
                            pool.dma_start(m["sum_adj"].rearrange("(b p) c -> p b c", p=P)
                                           [:, bass.ds(i * GB, n), a0 * NB:a1 * NB],
                                           total[k][:, 0:n, 0:(a1 - a0) * NB]).then_inc(total_out, 16)
                    bodies(pool, body)
                    pool.wait_ge(total_out, 32 * GROUPS)


def transpose_sum(nc, m):
    psum, ident_bf = m["psum"], m["ident_bf"]
    CUT = 12
    UNITS = -(-T // 2)
    with stage(nc, "t_") as (sb, sem):

        part = [sb(f"in{i}", [P, GB, (T - CUT) * NB], BF) for i in range(2)]
        out = [sb(f"out{i}", [P, 2 * T, 4, NB], BF) for i in range(2)]
        loaded = [sem(f"loaded{i}") for i in range(2)]
        turned, by_act, by_dve = sem("turned"), sem("by_act"), sem("by_dve")
        stored = [sem(f"stored{i}") for i in range(2)]
        zeroed = sem("zeroed")
        HALF = ((0, CUT), (CUT, T))

        def size(g):
            return (1, 1) if isinstance(g, int) and g == GROUPS - 1 else (GB, 4)

        def past(value):
            return not isinstance(value, int) or value > 0

        def groups(eng, one):
            pair[0] = 0
            one(0, 0)
            one(1, 1)
            with eng.Fori(1, (GROUPS - 1) // 2) as i:
                pair[0] = i
                one(i * 2, 0)
                one(i * 2 + 1, 1)
            pair[0] = (GROUPS - 1) // 2
            one(GROUPS - 1, 0)

        def evacuate(eng, first_unit, done):
            def one(g, place):
                n, k = size(g)
                rows = P if n == GB else NB
                if past(pair[0]):
                    eng.wait_ge(stored[place], pair[0] * 16)
                if n < GB:
                    eng.wait_ge(zeroed, 1)
                for u in range(first_unit, UNITS, 2):
                    eng.wait_ge(turned, g * UNITS + (u + 1))
                    tiles = min(2, T - 2 * u)
                    of = psum[u % 8][:, :].bitcast(BF)[0:rows, 0:tiles * k * P].rearrange("p (a l e n) -> p a l e n", l=k, e=2, n=NB)
                    for a in range(tiles):
                        to = out[place][0:rows, 4 * u + 2 * a:4 * u + 2 * a + 2, 0:k, :].rearrange("p e l n -> p l e n")
                        if eng.engine == mybir.EngineType.DVE:
                            last = eng.tensor_copy(to, of[:, a])
                        else:
                            last = eng.activation(to, of[:, a], ACT.Copy)
                        last.then_inc(done, 1)
            return one

        pair = [0]
        ACT_PER, DVE_PER = 13, 12

        with nc.Block() as block:
            @block.sync
            def _(sync):
                def one(g, place):
                    n, _ = size(g)
                    for h, (a0, a1) in enumerate(HALF):
                        if past(g):
                            wait_apart(sync, turned, g * UNITS - (UNITS - CUT // 2 if h == 0 else 0))
                        sync.dma_start(part[h][:, 0:n, 0:(a1 - a0) * NB],
                                       m["sum_adj"].rearrange("(b p) c -> p b c", p=P)
                                       [:, bass.ds(g * GB, n), a0 * NB:a1 * NB]).then_inc(loaded[h], 16)
                groups(sync, one)

            @block.tensor
            def _(pe):
                def one(g, place):
                    n, k = size(g)
                    for u in range(UNITS):
                        h = int(2 * u >= CUT)
                        if u in (0, CUT // 2):
                            wait_apart(pe, loaded[h], g * 16 + 16)
                        back, group = (u - 8, g) if u >= 8 else ((u + 8, g - 1) if u + 8 < UNITS else (u, g - 1))
                        if past(group + 1):
                            s, per = (by_dve, DVE_PER) if u % 2 else (by_act, ACT_PER)
                            n_done = min(back // 2 * 2 + 2, per)
                            wait_apart(pe, s, group * per + n_done)
                        bank = psum[u % 8][:, :].bitcast(BF)
                        for a in range(2 * u, min(2 * u + 2, T)):
                            for c in range(k):
                                at = ((a - 2 * u) * k + c) * P
                                for e in range(min(2, n)):
                                    last = pe.transpose(bank[e * NB:e * NB + NB, at:at + P],
                                                        part[h][:, 2 * c + e, (a - HALF[h][0]) * NB:(a - HALF[h][0] + 1) * NB],
                                                        ident_bf[:, :])
                        last.then_inc(turned, 1)
                groups(pe, one)

            @block.scalar
            def _(act):
                groups(act, evacuate(act, 0, by_act))

            @block.vector
            def _(dve):
                groups(dve, evacuate(dve, 1, by_dve))

            @block.gpsimd
            def _(pool):
                def one(g, place):
                    _, k = size(g)
                    if k == 1:
                        pool.wait_ge(stored[0], pair[0] * 16)
                        pool.memset(out[0][NB:P, :, 0, :], 0.0).then_inc(zeroed, 1)
                        pool.wait_ge(zeroed, 1)
                    pool.wait_ge(by_act, g * ACT_PER + ACT_PER)
                    pool.wait_ge(by_dve, g * DVE_PER + DVE_PER)
                    pool.dma_start(m["sum_adj_t"].rearrange("(b p) c -> p b c", p=P)
                                   [:, :, bass.ds(g * (4 * NB), k * NB)].rearrange("p b (l n) -> p b l n", n=NB),
                                   out[place][:, 0:BATCHES, 0:k, :]).then_inc(stored[place], 16)
                groups(pool, one)
                pool.wait_ge(stored[0], 16 * 4)
                pool.wait_ge(stored[1], 16 * 3)



def gyro_sum(nc, A, m):
    table_sb, table, deg, rdeg, first_f, edge_code, x_sb = (
        m[k] for k in ("table_sb", "table", "deg", "rdeg", "first_f", "edge_code", "x_sb"))
    W = max(b - a for a, b in TILE_GROUPS)
    NG = len(TILE_GROUPS)
    BLOCK = KB // STEPS
    PAIR = 2
    with stage(nc, "g_") as (sb, sem):
        most, most_all = sb("most", [P, NG], FP), sb("most_all", [P, NG], FP)
        trips_f = sb("trips_f", [P, 2 * NG], FP)
        trips = sb("trips", [P, 2 * NG], I32)
        lists = sb("lists", [P, W, KB], I32)
        at_edge_f, at_edge = sb("at_edge_f", [P, W], FP), sb("at_edge", [P, W], I32)
        source = sb("source", [P, STEPS, W], I32)
        ring = sb("ring", [P, STEPS, W, TW], FP)
        junk = sb("junk", [P, PAIR, W, D], BF)
        u, add = sb("u", [P, W, D], FP), sb("add", [P, W, D], FP)
        nth = sb("nth", [P, PAIR, W], FP)
        dot_h = sb("dot_h", [P, PAIR, W], FP)
        s0, s1, s2, s3, s4, p = (sb(f"s{i}", [P, PAIR, W], FP) for i in range(6))
        y = sb("y", [P, PAIR, 4, W], FP)
        z = sb("z", [P, 4, W], FP)
        za, zb = sb("za", [P, 4, W], FP), sb("zb", [P, 4, W], FP)
        ab = sb("ab", [P, 2, W], FP)
        dot_u, c0, c1, c2, c3, gamma = (sb(f"c{i}", [P, W], FP) for i in range(6))
        fin = sb("fin", [P, 13, T], FP)
        total = sb("total", [P, T, D], FP)

        vec, maxed, counted, sized = sem("vec"), sem("maxed"), sem("counted"), sem("sized")
        squared, stored, out_done, finished = sem("squared"), sem("stored"), sem("out_done"), sem("finished")
        edges_at, edge_next, src_ready, indexed = sem("edges_at"), sem("edge_next"), sem("src_ready"), sem("indexed")
        listed = [sem(f"listed{g}") for g in range(NG)]
        gathered = [[sem(f"gathered{g}_{j}") for j in range(STEPS)] for g in range(NG)]
        freed, gammas, scaled, stepped, to_act, from_act = (
            sem(n) for n in ("freed", "gammas", "scaled", "stepped", "to_act", "from_act"))

        def walk(eng, begin, refill, body, end):
            eng.wait_ge(sized, 1)
            bodies_of = [eng.value_load(trips[0:1, g:g + 1], min_val=1, max_val=E // STEPS) for g in range(NG)]
            blocks_of = [eng.value_load(trips[0:1, NG + g:NG + g + 1], min_val=1, max_val=-(-E // KB)) for g in range(NG)]
            bodies, blocks = 0, 0
            for g in range(NG):
                begin(g)
                with eng.Fori(0, blocks_of[g]) as b:
                    refill(g, blocks + b, b)
                    with eng.register(f"bodies_{g}") as reg:
                        eng.reg_mov(reg, bodies_of[g] - b * BLOCK)
                        eng.reg_alu(reg, reg, BLOCK, ALU.min)
                        here = eng.snap(reg, min_val=1, max_val=BLOCK)
                        with eng.Fori(0, here) as it:
                            body(g, bodies + (b * BLOCK + it), b * BLOCK + it, it)
                end(g)
                bodies, blocks = bodies + bodies_of[g], blocks + blocks_of[g]

        def nothing(*_):
            pass

        with nc.Block() as block:
            @block.sync
            def _(sync):
                sync.wait_ge(squared, 1)
                full = (T - 1) * P
                sync.dma_start(table[0:full, :].rearrange("(t p) d -> p t d", p=P), table_sb[:, 0:T - 1, :]).then_inc(stored, 16)
                sync.dma_start(table[full:N, :], table_sb[0:LAST, T - 1, :]).then_inc(stored, 16)
                sync.wait_ge(finished, 1)
                sync.dma_start(A["out"][0:full, :].rearrange("(t p) d -> p t d", p=P), total[:, 0:T - 1, :]).then_inc(out_done, 16)
                sync.dma_start(A["out"][full:N, :], total[0:LAST, T - 1, :]).then_inc(out_done, 16)
                sync.wait_ge(out_done, 32)
                sync.wait_ge(stored, 32)

            @block.gpsimd
            def _(pool):
                pool.wait_ge(maxed, 1)
                pool.partition_all_reduce(most_all[:, :], most[:, :], P, bass.bass_isa.ReduceOp.max).then_inc(counted, 1)
                pool.wait_ge(stored, 32)

                def refill(g, blocks, b):
                    n = TILE_GROUPS[g][1] - TILE_GROUPS[g][0]
                    wait_apart(pool, edges_at, blocks + 1)
                    for t in range(n):
                        pool.indirect_dma_start(lists[:, t, :], None, edge_code,
                                                bass.IndirectOffsetOnAxis(at_edge[:, t:t + 1], 0)).then_inc(listed[g], 16)
                    pool.wait_ge(src_ready, blocks + 1)

                def body(g, count, local, it):
                    n = TILE_GROUPS[g][1] - TILE_GROUPS[g][0]
                    for j in range(STEPS):
                        pool.wait_ge(freed, count * STEPS + (j + 1))
                        pool.tensor_copy(source[:, j, 0:n], lists[:, 0:n, bass.ds(it * STEPS + j, 1)]
                                         .rearrange("p t o -> p (t o)")).then_inc(indexed, 1)
                        wait_apart(pool, indexed, count * STEPS + (j + 1))
                        for t in range(n):
                            pool.indirect_dma_start(ring[:, j, t, :], None, table,
                                                    bass.IndirectOffsetOnAxis(source[:, j, t:t + 1], 0)) \
                                .then_inc(gathered[g][j], 16)

                walk(pool, nothing, refill, body, nothing)

            @block.scalar
            def _(act):
                def body(g, count, local, it):
                    n = TILE_GROUPS[g][1] - TILE_GROUPS[g][0]
                    for j in range(STEPS):
                        act.wait_ge(gammas, count * STEPS + (j + 1))
                        for t in range(n):
                            one = act.activation(add[:, t, :], ring[:, j, t, 0:D], ACT.Copy, scale=gamma[:, t:t + 1])
                        one.then_inc(scaled, 1)

                walk(act, nothing, nothing, body, nothing)
                act.wait_ge(to_act, 1)
                act.activation(fin[:, 1, :], fin[:, 0, :], ACT.Sqrt).then_inc(from_act, 1)
                act.wait_ge(to_act, 2)
                act.activation(fin[:, 4, :], fin[:, 3, :], ACT.Ln).then_inc(from_act, 1)
                act.wait_ge(to_act, 3)
                act.activation(fin[:, 5, :], fin[:, 4, :], ACT.Tanh, scale=0.5).then_inc(from_act, 1)

            @block.vector
            def _(dve):
                v = Tally(dve, vec)
                for g, (a, b) in enumerate(TILE_GROUPS):
                    v(dve.tensor_reduce(most[:, g:g + 1], deg[:, a:b], AX.X, ALU.max))
                v.settle()
                dve.memset(junk[:, 0, 0, 0:1], 0.0).then_inc(maxed, 1)
                dve.wait_ge(counted, 1)
                for g0, per in ((0, STEPS), (NG, KB)):
                    v(dve.tensor_scalar(trips_f[:, g0:g0 + NG], most_all[:, :], float(per - 1), float(per), ALU.add, ALU.max))
                v.settle()
                v.chain(dve.tensor_copy(trips[:, :], trips_f[:, :]))
                for g0, per in ((0, STEPS), (NG, KB)):
                    v(dve.tensor_scalar(trips[:, g0:g0 + NG], trips[:, g0:g0 + NG], per.bit_length() - 1, None,
                                        ALU.logical_shift_right))
                v.settle()
                dve.memset(junk[:, 0, 0, 1:2], 0.0).then_inc(sized, 1)
                v.chain(dve.memset(table_sb[:, :, D:TW], 0.0))
                for t in range(T):
                    last = dve.tensor_tensor_reduce(out=total[:, t, :], in0=table_sb[:, t, 0:D], in1=table_sb[:, t, 0:D],
                                                    scale=1.0, scalar=0.0, op0=ALU.mult, op1=ALU.add,
                                                    accum_out=table_sb[:, t, D:D + 1])
                last.then_inc(squared, 1)
                dve.wait_ge(squared, 1)
                for j in range(STEPS):
                    dve.memset(junk[:, 0, 0, 2 + j:3 + j], 0.0).then_inc(freed, 1)

                def begin(g):
                    a, b = TILE_GROUPS[g]
                    v(dve.memset(u[:, :, :], 0.0))
                    v(dve.memset(z[:, :, :], 0.0))
                    for j in range(PAIR):
                        v(dve.memset(nth[:, j, :], float(j)))
                    v(dve.tensor_copy(at_edge_f[:, 0:b - a], first_f[:, a:b]))
                    v.settle()

                def refill(g, blocks, b):
                    n = TILE_GROUPS[g][1] - TILE_GROUPS[g][0]
                    dve.tensor_copy(at_edge[:, 0:n], at_edge_f[:, 0:n]).then_inc(edges_at, 1)
                    dve.wait_ge(edges_at, blocks + 1)
                    dve.tensor_scalar(at_edge_f[:, 0:n], at_edge_f[:, 0:n], float(KB), float(E), ALU.add, ALU.min).then_inc(edge_next, 1)
                    dve.wait_ge(listed[g], b * (16 * n) + 16 * n)
                    dve.tensor_scalar(lists[:, 0:n, :], lists[:, 0:n, :], TYPE_BITS, None, ALU.logical_shift_right).then_inc(src_ready, 1)
                    dve.wait_ge(edge_next, blocks + 1)

                def body(g, count, local, it):
                    a, b = TILE_GROUPS[g]
                    n = b - a
                    w = Tally(dve, stepped, count * BODY_COUNT)
                    h_n = table_sb[:, a:b, :]
                    S = h_n[:, :, D].unsqueeze(1).broadcast_to([P, PAIR, n])
                    for q in range(STEPS // PAIR):
                        for j in range(PAIR):
                            dve.wait_ge(gathered[g][q * PAIR + j], local * (16 * n) + 16 * n)
                            for t in range(n):
                                one = dve.tensor_tensor_reduce(
                                    out=junk[:, j, t, :], in0=ring[:, q * PAIR + j, t, 0:D], in1=h_n[:, t, 0:D], scale=1.0,
                                    scalar=0.0, op0=ALU.mult, op1=ALU.add, accum_out=dot_h[:, j, t:t + 1])
                        w.chain(one)
                        s = ring[:, q * PAIR:(q + 1) * PAIR, 0:n, D]
                        g_ = dot_h[:, :, 0:n]
                        A1, sS, mask, negB, D1 = (x[:, :, 0:n] for x in (s0, s1, s2, s3, s4))
                        pp, qq = p[:, :, 0:n], y[:, :, 1, 0:n]
                        m_h, m_m = y[:, :, 0, 0:n], y[:, :, 3, 0:n]
                        w(dve.tensor_scalar(A1, g_, -2.0, 1.0, ALU.mult, ALU.add))
                        w(dve.tensor_tensor(sS, s, S, ALU.mult))
                        w(dve.tensor_tensor(mask, nth[:, :, 0:n], deg[:, a:b].unsqueeze(1).broadcast_to([P, PAIR, n]), ALU.is_lt))
                        w(dve.tensor_scalar(negB, s, -1.0, None, ALU.add))
                        w.settle()
                        w(dve.tensor_tensor(D1, A1, sS, ALU.add))
                        w(dve.tensor_scalar(nth[:, :, :], nth[:, :, :], float(PAIR), None, ALU.add))
                        w.settle()
                        w(dve.tensor_tensor(A1, A1, S, ALU.add))
                        w(dve.tensor_scalar(D1, D1, BALL_EPS, None, ALU.max))
                        w.settle()
                        w.chain(dve.reciprocal(D1, D1))
                        w.chain(dve.tensor_tensor(D1, D1, mask, ALU.mult))
                        w(dve.tensor_tensor(pp, A1, D1, ALU.mult))
                        w(dve.tensor_tensor(qq, negB, D1, ALU.mult))
                        w.settle()
                        w(dve.tensor_tensor(s0[:, :, 0:n], pp, g_, ALU.mult))
                        w(dve.tensor_tensor(s1[:, :, 0:n], qq, S, ALU.mult))
                        w(dve.tensor_tensor(s2[:, :, 0:n], pp, s, ALU.mult))
                        w(dve.tensor_tensor(s3[:, :, 0:n], qq, g_, ALU.mult))
                        w.settle()
                        w(dve.tensor_tensor(m_h, s0[:, :, 0:n], s1[:, :, 0:n], ALU.add))
                        w(dve.tensor_tensor(s2[:, :, 0:n], s2[:, :, 0:n], s3[:, :, 0:n], ALU.add))
                        w.settle()
                        w(dve.tensor_tensor(s0[:, :, 0:n], m_h, qq, ALU.mult))
                        w(dve.tensor_tensor(s1[:, :, 0:n], s2[:, :, 0:n], pp, ALU.mult))
                        w.settle()
                        w.chain(dve.tensor_tensor(m_m, s0[:, :, 0:n], s1[:, :, 0:n], ALU.add))

                        for j in range(PAIR):
                            k = q * PAIR + j
                            t_, w_, X, xy = (z[:, i, 0:n] for i in range(4))
                            alpha, beta = ab[:, 0, 0:n], ab[:, 1, 0:n]
                            for t in range(n):
                                one = dve.tensor_tensor_reduce(
                                    out=junk[:, j, t, :], in0=ring[:, k, t, 0:D], in1=u[:, t, :], scale=1.0,
                                    scalar=0.0, op0=ALU.mult, op1=ALU.add, accum_out=dot_u[:, t:t + 1])
                            w(one)
                            w(dve.tensor_tensor(c0[:, 0:n], w_, dot_h[:, j, 0:n], ALU.mult))
                            w(dve.tensor_tensor(c1[:, 0:n], y[:, j, 1, 0:n], t_, ALU.mult))
                            w(dve.tensor_tensor(c2[:, 0:n], X, y[:, j, 3, 0:n], ALU.mult))
                            w(dve.tensor_scalar(beta, X, -1.0, 1.0, ALU.mult, ALU.add))
                            w.settle()
                            w.chain(dve.tensor_tensor(c0[:, 0:n], c0[:, 0:n], dot_u[:, 0:n], ALU.add))
                            w.chain(dve.tensor_tensor(c0[:, 0:n], c0[:, 0:n], p[:, j, 0:n], ALU.mult))
                            w(dve.tensor_tensor(xy, c0[:, 0:n], c1[:, 0:n], ALU.add))
                            w(dve.tensor_tensor(y[:, j, 2, 0:n], c0[:, 0:n], c1[:, 0:n], ALU.add))
                            w.settle()
                            w(dve.scalar_tensor_tensor(alpha, xy, 2.0, y[:, j, 3, 0:n], ALU.mult, ALU.add))
                            w(dve.scalar_tensor_tensor(c3[:, 0:n], xy, 2.0, c2[:, 0:n], ALU.mult, ALU.add))
                            w.settle()
                            w(dve.tensor_scalar(alpha, alpha, 1.0, None, ALU.add))
                            w(dve.tensor_scalar(c3[:, 0:n], c3[:, 0:n], 1.0, BALL_EPS, ALU.add, ALU.max))
                            w.settle()
                            w.chain(dve.reciprocal(c3[:, 0:n], c3[:, 0:n]))
                            w.chain(dve.tensor_tensor(ab[:, :, 0:n], ab[:, :, 0:n],
                                                      c3[:, 0:n].unsqueeze(1).broadcast_to([P, 2, n]), ALU.mult))
                            dve.tensor_tensor(gamma[:, 0:n], beta, p[:, j, 0:n], ALU.mult).then_inc(gammas, 1)
                            w(dve.tensor_tensor(za[:, :, 0:n], z[:, :, 0:n], alpha.unsqueeze(1).broadcast_to([P, 4, n]), ALU.mult))
                            w(dve.tensor_tensor(zb[:, :, 0:n], y[:, j, :, 0:n], beta.unsqueeze(1).broadcast_to([P, 4, n]), ALU.mult))
                            w.settle()
                            w.chain(dve.tensor_tensor(z[:, :, 0:n], za[:, :, 0:n], zb[:, :, 0:n], ALU.add))
                            w.chain(dve.tensor_tensor(za[:, 0:2, 0:n], z[:, 2:4, 0:n], ab[:, :, 0:n], ALU.mult))
                            w.chain(dve.tensor_tensor(X, za[:, 0, 0:n], za[:, 1, 0:n], ALU.add))
                            dve.wait_ge(scaled, count * STEPS + (k + 1))
                            for t in range(n):
                                one = dve.scalar_tensor_tensor(u[:, t, :], u[:, t, :], ab[:, 0, t:t + 1], add[:, t, :],
                                                               ALU.mult, ALU.add)
                            one.then_inc(freed, 1)
                            dve.wait_ge(freed, count * STEPS + (STEPS + k + 1))
                    assert w.n == BODY_COUNT, w.n

                BODY_COUNT = (STEPS // PAIR) * 22 + STEPS * 20

                def end(g):
                    a, b = TILE_GROUPS[g]
                    for t in range(b - a):
                        v(dve.scalar_tensor_tensor(total[:, a + t, :], table_sb[:, a + t, 0:D], z[:, 1, t:t + 1], u[:, t, :],
                                                   ALU.mult, ALU.add))
                    v.settle()
                    for t in range(b - a):
                        for j, (x, to) in enumerate(((total, 0), (table_sb, 2))):
                            v(dve.tensor_tensor_reduce(out=junk[:, j, t, :], in0=total[:, a + t, :], in1=x[:, a + t, 0:D],
                                                       scale=1.0, scalar=0.0, op0=ALU.mult, op1=ALU.add,
                                                       accum_out=fin[:, to, a + t:a + t + 1]))
                    v.settle()

                walk(dve, begin, refill, body, end)
                square, norm, dot, ratio, log, tanh, zc, up, down, f, A_, B_, inside = (fin[:, i, :] for i in range(13))
                S = table_sb[:, :, D]
                dve.tensor_scalar(square, square, 1e-30, None, ALU.max).then_inc(to_act, 1)
                dve.wait_ge(from_act, 1)
                v.chain(dve.tensor_scalar(zc, norm, BALL_EPS, float(np.float32(1.0 - BALL_EPS)), ALU.max, ALU.min))
                v(dve.tensor_scalar(up, zc, 1.0, None, ALU.add))
                v(dve.tensor_scalar(down, zc, -1.0, 1.0, ALU.mult, ALU.add))
                v.settle()
                v.chain(dve.reciprocal(down, down))
                dve.tensor_tensor(ratio, up, down, ALU.mult).then_inc(to_act, 1)
                v(dve.reciprocal(f, zc))
                v(dve.tensor_scalar(inside, norm, BALL_EPS, None, ALU.is_gt))
                v.settle()
                v.chain(dve.tensor_tensor(f, f, inside, ALU.mult))
                dve.wait_ge(from_act, 2)
                dve.tensor_tensor(log, log, rdeg[:, :], ALU.mult).then_inc(to_act, 1)
                dve.wait_ge(from_act, 3)
                v.chain(dve.tensor_tensor(f, f, tanh, ALU.mult))
                v(dve.tensor_tensor(dot, dot, f, ALU.mult))
                v(dve.tensor_tensor(square, square, f, ALU.mult))
                v.settle()
                v.chain(dve.tensor_tensor(square, square, f, ALU.mult))
                v(dve.tensor_scalar(dot, dot, 2.0, 1.0, ALU.mult, ALU.add))
                v(dve.tensor_tensor(down, S, square, ALU.mult))
                v.settle()
                v(dve.tensor_tensor(A_, dot, square, ALU.add))
                v(dve.tensor_tensor(down, down, dot, ALU.add))
                v(dve.tensor_scalar(B_, S, -1.0, 1.0, ALU.mult, ALU.add))
                v.settle()
                v.chain(dve.tensor_scalar(down, down, BALL_EPS, None, ALU.max))
                v.chain(dve.reciprocal(down, down))
                v(dve.tensor_tensor(A_, A_, down, ALU.mult))
                v(dve.tensor_tensor(B_, B_, down, ALU.mult))
                v.settle()
                v.chain(dve.tensor_tensor(B_, B_, f, ALU.mult))
                for t in range(T):
                    v(dve.scalar_tensor_tensor(total[:, t, :], total[:, t, :], B_[:, t:t + 1], x_sb[:, t, :], ALU.mult, ALU.add))
                v.settle()
                for t in range(T):
                    one = dve.scalar_tensor_tensor(total[:, t, :], table_sb[:, t, 0:D], A_[:, t:t + 1], total[:, t, :],
                                                   ALU.mult, ALU.add)
                one.then_inc(finished, 1)


_INS = ["x", "src", "dst", "edge_type_5", "L0_gnn_weights", "L0_gnn_roots", "L0_gnn_biases", "L1_gnn_W_self",
        "L1_gnn_b_self", "L1_gnn_W_neig", "L1_gnn_b_neig", "L2_gnn_W1_l", "L2_gnn_b1_l", "L2_gnn_W1_r",
        "L2_gnn_W2_l", "L2_gnn_b2_l", "L2_gnn_W2_r"]


def kernel(**inputs):
    import concourse.bacc as bacc
    from concourse.bass_utils import run_bass_kernel_spmd

    nc = bacc.Bacc("TRN2", target_bir_lowering=False, num_devices=1)
    arrays, handles = {}, {}
    for name in _INS:
        a = np.ascontiguousarray(inputs[name])
        arrays[f"in_{name}"] = a
        handles[name] = nc.dram_tensor(f"in_{name}", a.shape, mybir.dt.from_np(a.dtype), kind="ExternalInput").ap()
    handles["out"] = nc.dram_tensor("out_0", (N, D), FP, kind="ExternalOutput").ap()
    build(nc, handles)
    return run_bass_kernel_spmd(nc, [arrays], core_ids=[0]).results[0]["out_0"]
```

```python
from contextlib import ExitStack, contextmanager

import concourse.bass as bass
import numpy as np
from concourse import mybir

N = 3125
E = 100000
D = 128
R = 5
P = 128
T = -(-N // P)
LAST = N - (T - 1) * P
EP = 125
EC = E // EP
KB = 64
HC = 20
NB = 64
SB = (T + 1) // 2
C = R * T
BATCHES = 2 * T - 1
GN = 512
GB = GN // NB
GROUPS = -(-N // GN)
OH = 32
TYPE_BITS = 3
RW = D + 4
TW = RW + D
STEPS = 4
TILE_GROUPS = ((0, 7), (7, 16), (16, T))
EPS = 1e-5
NORM_BOUND = 11.3
NORM_SCALE = 1024.0
BALL_EPS = 1e-7

DT = mybir.dt
FP, HF, I32 = DT.float32, DT.float16, DT.int32
ALU = mybir.AluOpType
ACT = mybir.ActivationFunctionType
AX = mybir.AxisListType


@contextmanager
def stage(nc, prefix):
    sems = []
    with ExitStack() as ctx:
        def sb(name, shape, dtype):
            return ctx.enter_context(nc.sbuf_tensor(prefix + name, shape, dtype))

        def sem(name):
            sems.append(nc.alloc_semaphore(prefix + name))
            return sems[-1]

        yield sb, sem
    nc.clear_and_free_semaphores(sems)
    nc.all_engine_barrier()


def wait_apart(eng, sem, value):
    eng.wait_ge(sem, value)
    if not isinstance(value, int):
        eng.sem_inc(APART[0], 1)


APART = [None]


class Tally:

    def __init__(self, engine, sem, at=0):
        self.engine, self.sem, self.at, self.n = engine, sem, at, 0

    def __call__(self, instruction):
        self.at, self.n = self.at + 1, self.n + 1
        instruction.then_inc(self.sem, 1)
        return self.at

    def settle(self, at=None):
        self.engine.wait_ge(self.sem, self.at if at is None else at)

    def chain(self, instruction):
        self(instruction)
        self.settle()


def build(nc, A, upto=99):
    ctx = ExitStack()
    with ctx:
        def sb(name, shape, dtype):
            return ctx.enter_context(nc.sbuf_tensor(name, shape, dtype))

        def sem(name):
            return ctx.enter_context(nc.semaphore(name))

        def dram(name, shape, dtype):
            return nc.dram_tensor(name, shape, dtype, kind="Internal").ap()

        psum = [ctx.enter_context(nc.psum_tensor(f"bank{i}", [P, 512], FP)) for i in range(8)]

        edge_code = dram("edge_code", (E + KB, 1), I32)
        adj = dram("adj", (BATCHES * P, C * NB), HF)
        sum_adj = dram("sum_adj", (BATCHES * P, T * NB), HF)
        sum_adj_t = dram("sum_adj_t", (BATCHES * P, T * NB), HF)

        table = dram("table", (T * P, TW), FP)
        key_row = dram("key_row", (T, P), FP)
        order = dram("order", (T * P, 4), FP)

        ident = sb("ident", [P, P], FP)
        ident_h = sb("ident_h", [P, P], HF)
        below = sb("below", [P, P], FP)
        ones = sb("ones", [P, P], FP)
        cnt = sb("cnt", [P, T, R], FP)
        deg = sb("deg", [P, T + 1], FP)
        rcnt = sb("rcnt", [P, T, R], FP)
        rdeg = sb("rdeg", [P, T], FP)
        first_edge = sb("first_edge", [P, T], I32)
        first_f = sb("first_f", [P, T], FP)

        APART[0] = nc.alloc_semaphore("waits_apart")
        preprocess(nc, A, locals())
        if upto >= 1:
            build_adjacency(nc, A, locals())

        x_sb = sb("x_sb", [P, T, D], FP)
        base = sb("base", [P, T, D], FP)
        parts = [sb(f"parts{i}", [P, T, 2, D], HF) for i in range(2)]
        scales = sb("scales", [P, 6], FP)
        unscales = sb("unscales", [P, 6], FP)
        key = sb("key", [P, T + R], FP)
        place = sb("place", [P, T + R], FP)
        record = sb("record", [P, T, 4], FP)
        record_o = sb("record_o", [P, T, 4], FP)
        node_o = sb("node_o", [P, T], I32)
        place_i = sb("place_i", [P, T], I32)
        at_edge = sb("at_edge", [P, T], I32)
        lists_o = sb("lists_o", [P, T, KB], I32)
        one_col = sb("one_col", [P, T, 1], FP)
        w_rel = sb("w_rel", [P, 3 * R, D], FP)
        w_root = sb("w_root", [P, 3, D], FP)
        w_two = sb("w_two", [P, 4, D], FP)
        w_turned = sb("w_turned", [P, 2, D], FP)
        bias_0 = sb("bias_0", [P, 3, D], FP)
        bias_1 = sb("bias_1", [P, 2, D], FP)
        bias_2 = sb("bias_2", [P, 2, D], FP)

        m = locals()
        if upto >= 2:
            start_features(nc, A, m)
        layers = [
            dict(rels=R, streams=[adj], scale=rcnt, w=w_rel[:, 0:R], root=w_root[:, 1], bias=bias_0[:, 1], make_sum=True),
            dict(rels=R, streams=[adj], scale=rcnt, w=w_rel[:, R:2 * R], root=w_root[:, 2], bias=bias_0[:, 2], rank=True),
            dict(rels=R, streams=[adj], scale=rcnt, w=w_rel[:, 2 * R:3 * R], root=w_turned[:, 0], bias=bias_1[:, 0], norm=True, put_in_order=True),
            dict(rels=1, streams=[sum_adj, sum_adj_t], scale=one_col, w=w_turned[:, 1:2], root=w_two[:, 1], bias=bias_2[:, 0], norm=True),
            dict(rels=1, streams=[sum_adj], scale=rdeg, w=w_two[:, 0:1], root=w_two[:, 3], bias=bias_2[:, 1]),
            dict(rels=1, streams=[sum_adj], scale=rdeg, w=w_two[:, 2:3], root=None, bias=None, norm=True),
        ]
        for n, layer in enumerate(layers):
            if n == 5:
                table_sb = sb("table_sb", [P, T, RW], FP)
                m["table_sb"] = table_sb
            if upto >= 3 + n:
                conv_layer(nc, m, n, **layer)
            if n == 2 and upto >= 3 + n:
                transpose_sum(nc, m)
        if upto >= 9:
            gyro_sum(nc, A, m)


def preprocess(nc, A, m):
    psum, cnt, deg, rcnt, rdeg = m["psum"], m["cnt"], m["deg"], m["rcnt"], m["rdeg"]
    first_edge, first_f = m["first_edge"], m["first_f"]
    ident, ident_h, below, ones = m["ident"], m["ident_h"], m["below"], m["ones"]
    edge_code = m["edge_code"]
    with stage(nc, "p_") as (sb, sem):

        dst_e = sb("dst_e", [EP, EC], I32)
        src_e = sb("src_e", [EP, EC], I32)
        typ_e = sb("typ_e", [EP, EC], I32)
        low_i = sb("low_i", [EP, EC], I32)
        tile_i = sb("tile_i", [EP, EC], I32)
        code_i = sb("code_i", [EP, EC], I32)
        low_b = sb("low_bf", [EP, EC], HF)
        code_b = sb("code_b", [EP, EC], HF)
        zero_i = sb("zero_i", [1, KB], I32)
        count_to = sb("count_to", [EP, P, HC], HF)
        hot_low = sb("hot_low", [EP, 2, P, HC], HF)
        hot_code = sb("hot_code", [EP, 2, C, HC], HF)
        tot = sb("tot", [P, T], FP)
        upto_tile = sb("upto_tile", [P, T], FP)

        made, loaded, coded, stored = sem("made"), sem("loaded"), sem("coded"), sem("stored")
        hot, used = sem("hot"), sem("used")
        vec, deg_ready, prefix = sem("vec"), sem("deg"), sem("prefix")
        hist = psum[0][:, 0:C]
        total, lower = psum[1][:, 0:T], psum[2][:, 0:T]

        with nc.Block() as block:
            @block.sync
            def _(sync):
                sync.dma_start(dst_e[:, :], A["dst"].rearrange("(p c) -> p c", c=EC)).then_inc(loaded, 16)
                sync.dma_start(typ_e[:, :], A["edge_type_5"].rearrange("(p c) -> p c", c=EC)).then_inc(loaded, 16)
                sync.dma_start(src_e[:, :], A["src"].rearrange("(p c) -> p c", c=EC)).then_inc(loaded, 16)
                sync.wait_ge(coded, 1)
                sync.dma_start(edge_code[0:E, :].rearrange("(p c) o -> p (c o)", c=EC), src_e[:, :]).then_inc(stored, 16)
                sync.dma_start(edge_code[E:E + KB, :].rearrange("(a c) o -> a (c o)", a=1), zero_i[:, :]).then_inc(stored, 16)
                sync.wait_ge(stored, 32)

            @block.gpsimd
            def _(pool):
                pool.iota(count_to[:, :, :], [[1, P], [0, HC]], base=0, channel_multiplier=0,
                          allow_small_or_imprecise_dtypes=True).then_inc(made, 1)
                pool.memset(zero_i[:, :], 0).then_inc(made, 1)
                pool.memset(ident[:, :], 0.0).then_inc(made, 1)
                pool.memset(ident_h[:, :], 0.0).then_inc(made, 1)
                pool.memset(below[:, :], 0.0).then_inc(made, 1)
                pool.memset(ones[:, :], 1.0).then_inc(made, 1)
                pool.memset(deg[:, T:T + 1], 0.0).then_inc(made, 1)
                pool.wait_ge(made, 7)
                for x in (ident, ident_h):
                    pool.affine_select(out=x[:, :], in_=x[:, :], compare_op=ALU.not_equal, fill=1.0,
                                       base=0, pattern=[[-1, P]], channel_multiplier=1).then_inc(made, 1)
                pool.affine_select(out=below[:, :], in_=below[:, :], compare_op=ALU.is_ge, fill=1.0,
                                   base=0, pattern=[[-1, P]], channel_multiplier=1).then_inc(made, 1)

            @block.vector
            def _(dve):
                v = Tally(dve, vec)
                dve.wait_ge(loaded, 48)
                v(dve.tensor_scalar(low_i[:, :], dst_e[:, :], P - 1, None, ALU.bitwise_and))
                v(dve.tensor_scalar(tile_i[:, :], dst_e[:, :], 7, None, ALU.logical_shift_right))
                v.settle()
                v(dve.tensor_copy(low_b[:, :], low_i[:, :]))
                v(dve.scalar_tensor_tensor(code_b[:, :], tile_i[:, :], float(R), typ_e[:, :], ALU.mult, ALU.add))
                v.chain(dve.scalar_tensor_tensor(code_i[:, :], src_e[:, :], float(1 << TYPE_BITS), typ_e[:, :],
                                                 ALU.mult, ALU.add))
                dve.wait_ge(made, 2)
                dve.tensor_copy(src_e[:, :], code_i[:, :]).then_inc(coded, 1)

                def make_hot(col, step, slot, wait):
                    if wait:
                        dve.wait_ge(used, step - 1)
                    dve.tensor_tensor(hot_low[:, slot], count_to[:, :, :],
                                      low_b[:, bass.ds(col, HC)].unsqueeze(1).broadcast_to([EP, P, HC]),
                                      ALU.is_equal).then_inc(hot, 1)
                    dve.tensor_tensor(hot_code[:, slot], count_to[:, 0:C, :],
                                      code_b[:, bass.ds(col, HC)].unsqueeze(1).broadcast_to([EP, C, HC]),
                                      ALU.is_equal).then_inc(hot, 1)

                make_hot(0, 0, 0, False)
                make_hot(HC, 1, 1, False)
                with dve.Fori(1, EC // HC // 2) as i:
                    make_hot(i * (2 * HC), i * 2, 0, True)
                    make_hot(i * (2 * HC) + HC, i * 2 + 1, 1, True)
                dve.wait_ge(used, EC // HC)
                v(dve.tensor_copy(cnt[:, :, :], hist.rearrange("p (t r) -> p t r", r=R)))
                v.chain(dve.tensor_reduce(deg[:, 0:T], hist.rearrange("p (t r) -> p t r", r=R), AX.X, ALU.add))
                dve.wait_ge(vec, v.at)
                v(dve.tensor_scalar(rcnt[:, :, :], cnt[:, :, :], 1.0, None, ALU.max))
                v(dve.tensor_scalar(rdeg[:, :], deg[:, 0:T], 1.0, None, ALU.max))
                dve.tensor_copy(upto_tile[:, :], deg[:, 0:T]).then_inc(deg_ready, 1)
                v.settle()
                v(dve.reciprocal(rcnt[:, :, :], rcnt[:, :, :]))
                v(dve.reciprocal(rdeg[:, :], rdeg[:, :]))
                dve.wait_ge(prefix, 2)
                v.chain(dve.tensor_copy(tot[:, :], total))
                v.chain(dve.tensor_tensor_scan(upto_tile[:, :], ones[:, 0:T], tot[:, :], 0.0, ALU.mult, ALU.add))
                v.chain(dve.tensor_tensor(upto_tile[:, :], upto_tile[:, :], tot[:, :], ALU.subtract))
                v.chain(dve.tensor_tensor(first_f[:, :], upto_tile[:, :], lower, ALU.add))
                v.chain(dve.tensor_copy(first_edge[:, :], first_f[:, :]))

            @block.tensor
            def _(pe):
                def count(step, slot, begin=False, end=False):
                    pe.wait_ge(hot, step * 2 + 2)
                    for c in range(HC):
                        last = pe.matmul(hist, hot_low[:, slot, :, c], hot_code[:, slot, :, c],
                                         start=begin and c == 0, stop=end and c == HC - 1)
                    last.then_inc(used, 1)

                count(0, 0, begin=True)
                count(1, 1)
                with pe.Fori(1, EC // HC // 2 - 1) as i:
                    count(i * 2, 0)
                    count(i * 2 + 1, 1)
                count(EC // HC - 2, 0)
                count(EC // HC - 1, 1, end=True)
                pe.wait_ge(made, 10)
                pe.wait_ge(deg_ready, 1)
                pe.matmul(total, ones[:, :], upto_tile[:, :], start=True, stop=True).then_inc(prefix, 1)
                pe.matmul(lower, below[:, :], upto_tile[:, :], start=True, stop=True).then_inc(prefix, 1)


def build_adjacency(nc, A, m):
    psum, deg, first_edge, edge_code, adj = m["psum"], m["deg"], m["first_edge"], m["edge_code"], m["adj"]
    ident_h = m["ident_h"]
    with stage(nc, "b_") as (sb, sem):

        lists = sb("lists", [P, 2 * SB, KB], I32)
        low_l = sb("low_l", [P, 2 * SB, KB], I32)
        tile_l = sb("tile_l", [P, 2 * SB, KB], I32)
        rel_l = sb("rel_l", [P, 2 * SB, KB], I32)
        valid = sb("valid", [P, 2 * SB, KB], FP)
        slot_no = sb("slot_no", [P, KB], FP)
        low_n = sb("low_n", [P, 2 * SB, KB], HF)
        code_f = sb("code_f", [P, 2 * SB, KB], FP)
        code_n = sb("code_n", [P, 2 * SB, KB], HF)
        low_t = sb("low_t", [P, SB, P], HF)
        code_t = sb("code_t", [P, SB, P], HF)
        count_to = sb("count_to_b", [P, P, OH], HF)
        hot_low = sb("hot_low_b", [P, 2, P, OH], HF)
        hot_code = sb("hot_code_b", [P, 2, C, OH], HF)
        batch = sb("batch", [P, 2, 2, C, NB], HF)

        made, fetched, turned = sem("made"), sem("fetched"), sem("turned")
        turned_sb, hot, used = sem("turned_sb"), sem("hot"), sem("used")
        vec, by_act, by_dve = sem("vec"), sem("by_act"), sem("by_dve")
        store = [sem(f"store{h}") for h in range(2)]
        UNITS = 2 * OH // 4
        DVE_UNITS = (3, 8, 13)
        ACT_UNITS = tuple(u for u in range(UNITS) if u not in DVE_UNITS)
        LAST_DVE_UNITS = tuple(u for u in DVE_UNITS if u < 8)
        LAST_ACT_UNITS = tuple(u for u in ACT_UNITS if u < 8)
        turn_go, copied = sem("turn_go"), sem("copied")

        def evacuate(eng, s, k, units, first=False):
            q, h = k // 2, k % 2
            if h == 0 and not first:
                eng.wait_ge(store[q], s * 32)
            for u in units:
                before = s * 4 * UNITS + (k * UNITS if not (isinstance(s, int) and s == SB - 1) else k * (UNITS // 2))
                eng.wait_ge(used, before + (u + 1))
                at = h * OH + u % 8 * 4
                to = batch[:, q, u // 8, :, at:at + 4].rearrange("p c n -> p n c")
                of = psum[u % 8][:, 0:4 * C].rearrange("p (n c) -> p n c", c=C)
                if eng.engine == mybir.EngineType.DVE:
                    eng.tensor_copy(to, of).then_inc(by_dve, 1)
                else:
                    eng.activation(to, of, ACT.Copy).then_inc(by_act, 1)

        with nc.Block() as block:
            @block.gpsimd
            def _(pool):
                pool.iota(slot_no[:, :], [[1, KB]], base=0, channel_multiplier=0,
                          allow_small_or_imprecise_dtypes=True).then_inc(made, 1)
                pool.iota(count_to[:, :, :], [[1, P], [0, OH]], base=0, channel_multiplier=0,
                          allow_small_or_imprecise_dtypes=True).then_inc(made, 1)
                pool.memset(lists[:, T, :], 0).then_inc(made, 1)
                for t in range(T):
                    pool.indirect_dma_start(lists[:, t, :], None, edge_code,
                                            bass.IndirectOffsetOnAxis(first_edge[:, t:t + 1], 0)).then_inc(fetched, 16)

            @block.vector
            def _(dve):
                v = Tally(dve, vec)
                dve.wait_ge(made, 3)
                dve.wait_ge(fetched, 16 * T)
                v(dve.tensor_scalar(tile_l[:, :, :], lists[:, :, :], TYPE_BITS + 7, None, ALU.logical_shift_right))
                v(dve.tensor_scalar(rel_l[:, :, :], lists[:, :, :], (1 << TYPE_BITS) - 1, None, ALU.bitwise_and))
                v(dve.tensor_scalar(low_l[:, :, :], lists[:, :, :], TYPE_BITS, P - 1, ALU.logical_shift_right, ALU.bitwise_and))
                v(dve.tensor_tensor(valid[:, :, :], slot_no[:, :].unsqueeze(1).broadcast_to([P, 2 * SB, KB]),
                                    deg[:, :].unsqueeze(2).broadcast_to([P, 2 * SB, KB]), ALU.is_lt))
                v.settle()
                v(dve.scalar_tensor_tensor(code_f[:, :, :], rel_l[:, :, :], float(T), tile_l[:, :, :], ALU.mult, ALU.add))
                v(dve.tensor_copy(low_n[:, :, :], low_l[:, :, :]))
                v.settle()
                v.chain(dve.scalar_tensor_tensor(code_f[:, :, :], code_f[:, :, :], 1.0, valid[:, :, :], ALU.add, ALU.mult))
                v.chain(dve.tensor_scalar(code_n[:, :, :], code_f[:, :, :], -1.0, None, ALU.add))
                coded = v.at
                dve.nop().then_inc(turn_go, 1)
                for s in range(SB):
                    dve.wait_ge(turned, 2 * s + 2)
                    v(dve.tensor_copy(low_t[:, s, :], psum[2 * s % 8][:, 0:P // 2].bitcast(HF)))
                    dve.tensor_copy(code_t[:, s, :], psum[(2 * s + 1) % 8][:, 0:P // 2].bitcast(HF)).then_inc(copied, 1)
                v.settle()
                dve.wait_ge(copied, SB)

                def make_hot(step, s, k):
                    if not (isinstance(step, int) and step < 2):
                        dve.wait_ge(used, step * UNITS - UNITS)
                    at = k // 2 * NB + k % 2 * OH
                    for to, codes, n in ((hot_low, low_t, P), (hot_code, code_t, C)):
                        dve.tensor_tensor(to[:, k % 2], count_to[:, 0:n, :],
                                          codes[:, bass.ds(s, 1), at:at + OH].broadcast_to([P, n, OH]),
                                          ALU.is_equal).then_inc(hot, 1)

                def four_steps(s, first=False):
                    for k in range(4):
                        make_hot(s * 4 + (k + 1), s + (k + 1) // 4, (k + 1) % 4)
                        evacuate(dve, s, k, DVE_UNITS, first)

                make_hot(0, 0, 0)
                four_steps(0, True)
                with dve.Fori(1, SB - 1) as s:
                    four_steps(s)
                make_hot((SB - 1) * 4 + 1, SB - 1, 1)
                for k in range(2):
                    evacuate(dve, SB - 1, k, LAST_DVE_UNITS)

            @block.scalar
            def _(act):
                for k in range(4):
                    evacuate(act, 0, k, ACT_UNITS, True)
                with act.Fori(1, SB - 1) as s:
                    for k in range(4):
                        evacuate(act, s, k, ACT_UNITS)
                for k in range(2):
                    evacuate(act, SB - 1, k, LAST_ACT_UNITS)

            @block.tensor
            def _(pe):
                pe.wait_ge(turn_go, 1)
                for s in range(SB):
                    if s >= 4:
                        pe.wait_ge(copied, s - 3)
                    for n, x in enumerate((low_n, code_n)):
                        pe.transpose(psum[(2 * s + n) % 8][:, 0:P // 2].bitcast(HF),
                                     x[:, 2 * s:2 * s + 2, :].rearrange("p t k -> p (t k)"),
                                     ident_h[:, :]).then_inc(turned, 1)
                pe.wait_ge(copied, SB)

                def count(s, k, units, first=False):
                    step = s * 4 + k
                    pe.wait_ge(hot, step * 2 + 2)
                    for u in range(units):
                        if not (first and k == 0 and u < 8):
                            if u < 8:
                                last_u = u + 8 if not (isinstance(s, int) and s == SB - 1 and k == 1) else u
                                short = isinstance(s, int) and s == SB - 1 and k == 1
                                done = ((LAST_DVE_UNITS, LAST_ACT_UNITS) if short else (DVE_UNITS, ACT_UNITS))
                                dve_one = last_u in done[0]
                                sem_, mine, per = (by_dve, done[0], len(DVE_UNITS)) if dve_one else (by_act, done[1], len(ACT_UNITS))
                                pe.wait_ge(sem_, (step - 1) * per + (mine.index(last_u) + 1))
                            else:
                                last_u = u - 8
                                sem_, mine = (by_dve, DVE_UNITS) if last_u in DVE_UNITS else (by_act, ACT_UNITS)
                                pe.wait_ge(sem_, step * len(mine) + (mine.index(last_u) + 1))
                        j = u // 8
                        rows = slice(j * KB, j * KB + KB)
                        for n in range(4):
                            i = u % 8 * 4 + n
                            last = pe.matmul(psum[u % 8][:, n * C:n * C + C], hot_low[rows, k % 2, :, i],
                                             hot_code[rows, k % 2, :, i], start=True, stop=True)
                        last.then_inc(used, 1)

                for k in range(4):
                    count(0, k, UNITS, True)
                with pe.Fori(1, SB - 1) as s:
                    for k in range(4):
                        count(s, k, UNITS)
                for k in range(2):
                    count(SB - 1, k, UNITS // 2)

            @block.sync
            def _(sync):
                def put(s, q, tiles=2):
                    step = s * 4 + (q * 2 + 2)
                    if tiles == 2:
                        wait_apart(sync, by_dve, step * len(DVE_UNITS))
                        wait_apart(sync, by_act, step * len(ACT_UNITS))
                    else:
                        sync.wait_ge(by_dve, (SB - 1) * 4 * len(DVE_UNITS) + 2 * len(LAST_DVE_UNITS))
                        sync.wait_ge(by_act, (SB - 1) * 4 * len(ACT_UNITS) + 2 * len(LAST_ACT_UNITS))
                    for j in range(tiles):
                        sync.dma_start(adj[bass.ds(s * (4 * P) + (2 * j + q) * P, P), :],
                                       batch[:, q, j].rearrange("p c n -> p (c n)")).then_inc(store[q], 16)

                with sync.Fori(0, SB - 1) as s:
                    for q in range(2):
                        put(s, q)
                put(SB - 1, 0, 1)
                sync.wait_ge(store[0], 32 * (SB - 1) + 16)
                sync.wait_ge(store[1], 32 * (SB - 1))


def layer_norm(dve, v, x, stats, mean_var, tiles):
    for t in range(tiles):
        v(dve.bn_stats(stats[:, t, :], x[:, t, :]))
    wait_apart(dve, v.sem, v.at)
    for t in range(tiles):
        v(dve.bn_aggr(mean_var[:, t, :], stats[:, t, :]))
    v.settle()


def split(dve, v, parts, h, scale):
    v.chain(dve.tensor_scalar(parts[:, :, 0, :], h, scale, None, ALU.mult))
    v(dve.scalar_tensor_tensor(parts[:, :, 1, :], h, scale, parts[:, :, 0, :], ALU.mult, ALU.subtract))


def start_features(nc, A, m):
    x_sb, base, parts, psum, ident = m["x_sb"], m["base"], m["parts"], m["psum"], m["ident"]
    with stage(nc, "f_") as (sb, sem):

        stats = sb("stats", [P, T, 6], FP)
        mean_var = sb("mean_var", [P, T, 2], FP)
        deviation = sb("deviation", [P, T], FP)
        rstd = sb("rstd", [P, T], FP)
        shift = sb("shift", [P, T], FP)
        h = sb("h", [P, T, D], FP)
        h_t = sb("h_t", [P, T, P], FP)
        w_pair = sb("w_pair", [P, 2, D], FP)
        xs, ws, vec, dev, scaled, normed = (sem(f"{n}") for n in ("xs", "ws", "vec", "dev", "scaled", "normed"))
        turned, copied, rooted, added = (sem(f"{n}") for n in ("turned", "copied", "rooted", "added"))
        sizes = sb("sizes", [P, 3 * R + 3 + 2, D], FP)
        column = sb("column", [P, 3, D], FP)
        bound = sb("bound", [P, 3], FP)
        power_i = sb("power_i", [P, 3], I32)
        inverse_i = sb("inverse_i", [P, 3], I32)
        beyond = sb("beyond", [P, T], FP)
        key_t = sb("key_t", [T, P], FP)
        numbered, keyed, key_out = sem("numbered"), sem("keyed"), sem("key_out")
        sized, summed_w = sem("sized"), sem("summed_w")
        cleared, w_turns, w_copied = sem("cleared"), sem("w_turns"), sem("w_copied")
        QUADS = -(-T // 4)

        with nc.Block() as block:
            @block.sync
            def _(sync):
                x = A["x"]
                full = (T - 1) * P
                for q in range(2):
                    sync.dma_start(x_sb[:, 12 * q:12 * q + 12, :],
                                   x[12 * P * q:12 * P * (q + 1), :].rearrange("(t p) d -> p t d", p=P)).then_inc(xs, 16)
                sync.wait_ge(cleared, 1)
                sync.dma_start(x_sb[0:LAST, T - 1, :], x[full:N, :]).then_inc(xs, 16)
                sync.dma_start(m["w_root"][:, :, :], A["L0_gnn_roots"].rearrange("l d e -> d l e")).then_inc(ws, 16)
                sync.dma_start(m["w_rel"][:, :, :], A["L0_gnn_weights"].rearrange("l r d e -> d (l r) e")).then_inc(ws, 16)
                sync.wait_ge(keyed, 3)
                sync.dma_start(m["key_row"][:, :], key_t[:, :]).then_inc(key_out, 16)
                sync.wait_ge(key_out, 16)
                sync.wait_ge(ws, 16 * 13)

            @block.gpsimd
            def _(pool):
                pool.iota(m["record"][:, :, 0], [[P, T]], base=0, channel_multiplier=1,
                          allow_small_or_imprecise_dtypes=True).then_inc(numbered, 1)

            @block.scalar
            def _(act):
                act.dma_start(m["bias_0"][:, :, :], A["L0_gnn_biases"].unsqueeze(0).broadcast_to([P, 3, D])).then_inc(ws, 16)
                for n, name in enumerate(("L1_gnn_W_self", "L1_gnn_W_neig")):
                    act.dma_start(w_pair[:, n, :], A[name]).then_inc(ws, 16)
                for n, name in enumerate(("L2_gnn_W1_l", "L2_gnn_W1_r", "L2_gnn_W2_l", "L2_gnn_W2_r")):
                    act.dma_start(m["w_two"][:, n, :], A[name]).then_inc(ws, 16)
                for to, name in ((m["bias_1"][:, 0], "L1_gnn_b_self"), (m["bias_1"][:, 1], "L1_gnn_b_neig"),
                                 (m["bias_2"][:, 0], "L2_gnn_b1_l"), (m["bias_2"][:, 1], "L2_gnn_b2_l")):
                    act.dma_start(to, A[name].unsqueeze(0).broadcast_to([P, D])).then_inc(ws, 16)
                act.wait_ge(dev, 1)
                act.activation(deviation[:, :], deviation[:, :], ACT.Sqrt).then_inc(dev, 1)
                act.wait_ge(scaled, 1)
                for t in range(T):
                    act.activation(h[:, t, :], x_sb[:, t, :], ACT.Relu, scale=rstd[:, t:t + 1],
                                   bias=shift[:, t:t + 1]).then_inc(normed, 1)
                for q in range(QUADS):
                    n = min(4, T - 4 * q)
                    act.wait_ge(turned, q + 1)
                    act.activation(h_t[:, 4 * q:4 * q + n, :], psum[q % 4][:, 0:n * P].rearrange("p (t n) -> p t n", n=P),
                                   ACT.Copy).then_inc(copied, 1)
                act.wait_ge(w_turns, 2)
                act.activation(m["w_turned"][:, :, :], psum[7][:, 0:2 * P].rearrange("p (t n) -> p t n", n=P),
                               ACT.Copy).then_inc(w_copied, 1)

            @block.vector
            def _(dve):
                v = Tally(dve, vec)
                dve.memset(x_sb[:, T - 1, :], 0.0).then_inc(cleared, 1)
                for x, value in ((m["scales"], NORM_SCALE), (m["unscales"], 1.0 / NORM_SCALE)):
                    v(dve.memset(x[:, :], value))
                v(dve.memset(m["one_col"][:, :, :], 1.0))
                record, key = m["record"], m["key"]
                v(dve.memset(key[:, :], 0.0))
                v(dve.tensor_copy(record[:, :, 1], m["deg"][:, 0:T]))
                v(dve.tensor_copy(record[:, :, 2], m["first_f"][:, :]))
                v(dve.tensor_copy(record[:, :, 3], m["rdeg"][:, :]))
                dve.wait_ge(numbered, 1)
                v(dve.tensor_scalar(beyond[:, :], record[:, :, 0], float(N), -4096.0, ALU.is_ge, ALU.mult))
                v.settle()
                v.chain(dve.tensor_scalar(key[:, 0:T], record[:, :, 1], 2000.0, 4096.0, ALU.min, ALU.mult))
                v.chain(dve.tensor_tensor(key[:, 0:T], key[:, 0:T], record[:, :, 0], ALU.add))
                dve.tensor_tensor(key[:, 0:T], key[:, 0:T], beyond[:, :], ALU.add).then_inc(keyed, 1)
                dve.wait_ge(keyed, 2)
                dve.tensor_copy(key_t[:, :], psum[5][0:T, 0:P]).then_inc(keyed, 1)
                dve.wait_ge(xs, 48)
                layer_norm(dve, v, x_sb, stats, mean_var, T)
                dve.tensor_scalar(deviation[:, :], mean_var[:, :, 1], EPS, None, ALU.add).then_inc(dev, 1)
                dve.wait_ge(dev, 2)
                v.chain(dve.reciprocal(rstd[:, :], deviation[:, :]))
                dve.scalar_tensor_tensor(shift[:, :], mean_var[:, :, 0], -1.0, rstd[:, :], ALU.mult, ALU.mult).then_inc(scaled, 1)
                dve.wait_ge(normed, T)
                split(dve, v, parts[0][:, :, :, :], h[:, :, :], m["scales"][:, 0:1])
                dve.wait_ge(ws, 16 * 13)
                for to, of, n in ((0, m["w_rel"], 3 * R), (3 * R, m["w_root"], 3), (3 * R + 3, m["w_two"], 2)):
                    v(dve.scalar_tensor_tensor(sizes[:, to:to + n, :], of[:, 0:n, :], -1.0, of[:, 0:n, :], ALU.mult, ALU.max))
                v.settle()
                for l in range(2):
                    v(dve.tensor_reduce(column[:, l, :], sizes[:, l * R:(l + 1) * R, :].rearrange("p r e -> p e r"), AX.X, ALU.add))
                v.settle()
                for l in range(2):
                    v(dve.tensor_tensor(column[:, l, :], column[:, l, :], sizes[:, 3 * R + l, :], ALU.add))
                dve.tensor_tensor(column[:, 2, :], sizes[:, 3 * R + 3, :], sizes[:, 3 * R + 4, :], ALU.add).then_inc(sized, 1)
                v.settle()
                dve.wait_ge(summed_w, 1)
                v.chain(dve.tensor_copy(column[:, :, :], psum[6][:, 0:3 * D].rearrange("p (l e) -> p l e", e=D)))
                for l, bias in enumerate((m["bias_0"][:, 0], m["bias_0"][:, 1], m["bias_2"][:, 0])):
                    size = sizes[:, l, :]
                    v(dve.scalar_tensor_tensor(size, bias, -1.0, bias, ALU.mult, ALU.max))
                v.settle()
                for l, of in ((0, NORM_BOUND), (2, NORM_BOUND), (1, bound[:, 0:1])):
                    v.chain(dve.scalar_tensor_tensor(sizes[:, l, :], column[:, l, :], of, sizes[:, l, :], ALU.mult, ALU.add))
                    v.chain(dve.tensor_reduce(bound[:, l:l + 1], sizes[:, l, :], AX.X, ALU.max))
                v.chain(dve.tensor_scalar(bound[:, :], bound[:, :], 2.0 ** -40, 2.0 ** 40, ALU.max, ALU.min))
                v.chain(dve.tensor_scalar(power_i[:, :], bound[:, :].bitcast(I32), 0x7F800000, None, ALU.bitwise_and))
                v.chain(dve.tensor_scalar(inverse_i[:, :], power_i[:, :], -1.0, float(254 << 23), ALU.mult, ALU.add))
                for at, l in ((1, 0), (2, 1), (5, 2)):
                    v(dve.tensor_scalar(m["scales"][:, at:at + 1], inverse_i[:, l:l + 1].bitcast(FP), 2.0 ** 14, None, ALU.mult))
                    v(dve.tensor_scalar(m["unscales"][:, at:at + 1], power_i[:, l:l + 1].bitcast(FP), 2.0 ** -14, None, ALU.mult))
                for q in range(QUADS):
                    n = min(4, T - 4 * q)
                    dve.wait_ge(rooted, q + 1)
                    dve.tensor_tensor(base[:, 4 * q:4 * q + n, :],
                                      psum[4 + q % 2][:, 0:n * D].rearrange("p (t n) -> p t n", n=D),
                                      m["bias_0"][:, 0:1, :].broadcast_to([P, n, D]), ALU.add).then_inc(added, 1)
                v(dve.tensor_tensor(m["bias_1"][:, 0], m["bias_1"][:, 0], m["bias_1"][:, 1], ALU.add))

            @block.tensor
            def _(pe):
                pe.wait_ge(keyed, 1)
                pe.transpose(psum[5][0:T, 0:P], m["key"][:, 0:T], ident[:, :]).then_inc(keyed, 1)
                pe.wait_ge(normed, T)
                for q in range(QUADS):
                    n = min(4, T - 4 * q)
                    if q >= 4:
                        pe.wait_ge(copied, q - 3)
                    for t in range(n):
                        last = pe.transpose(psum[q % 4][:, t * P:t * P + P], h[:, 4 * q + t, :], ident[:, :])
                    last.then_inc(turned, 1)
                pe.wait_ge(ws, 16 * 13)
                pe.wait_ge(sized, 1)
                pe.matmul(psum[6][:, 0:3 * D], m["ones"][:, :], column[:, :, :].rearrange("p l e -> p (l e)"),
                          start=True, stop=True).then_inc(summed_w, 1)
                for n in range(2):
                    pe.transpose(psum[7][:, n * P:n * P + P], w_pair[:, n, :], ident[:, :]).then_inc(w_turns, 1)
                for q in range(QUADS):
                    n = min(4, T - 4 * q)
                    pe.wait_ge(copied, q + 1)
                    if q >= 2:
                        pe.wait_ge(added, q - 1)
                    for t in range(n):
                        last = pe.matmul(psum[4 + q % 2][:, t * D:t * D + D], h_t[:, 4 * q + t, :],
                                         m["w_root"][:, 0, :], start=True, stop=True)
                    last.then_inc(rooted, 1)


HALVES = ((0, 13), (13, T))
HW = 13


def conv_layer(nc, m, number, rels, streams, scale, w, root, bias, norm=False, make_sum=False, rank=False,
               put_in_order=False):
    psum, ident, base, x_sb = m["psum"], m["ident"], m["base"], m["x_sb"]
    now, then = m["parts"][number % 2], m["parts"][1 - number % 2]
    per_body = 1 if rels > 1 else 2
    spb = per_body * rels
    BANK, BACK = ((0, 1, 0, 1, 2), (3, 3, 2, 2, 5)) if rels == 5 else ((0, 1), (2, 2))
    S = len(streams)
    halves = 2 * S
    slots = 5 if rels == 5 else 4
    with stage(nc, f"l{number}_") as (sb, sem):

        slot = [sb(f"slot{i}", [P, GB, HW * NB], HF) for i in range(slots)]
        sums = [sb(f"sums{i}", [P, GN], FP) for i in range(3)]
        acc = sb("acc", [P, 4, D], FP)
        hbuf = [sb(f"h{i}", [P, 4, D], FP) for i in range(2)]
        h_t = sb("h_t", [P, GN], FP)
        stats = sb("stats", [P, 4, 6], FP)
        mean_var = sb("mean_var", [P, 4, 2], FP)
        deviation = sb("deviation", [P, 4], FP)
        rstd = sb("rstd", [P, 4], FP)
        shift = sb("shift", [P, 4], FP)
        total = [sb(f"total{i}", [P, GB, HW * NB], HF) for i in range(2)] if make_sum else None

        if rank:
            key_all = sb("key_all", [P, T * P], FP)
            above = sb("above", [P, T * P], HF)
            keys_in, ranked = sem("keys_in"), sem("ranked")
        if put_in_order:
            lists_in, ordered, read_back, placed = sem("lists_in"), sem("ordered"), sem("read_back"), sem("placed")
        arrived = [sem(f"arrived{i}") for i in range(slots)]
        half_done, sums_copied, w_done, acc_done = sem("half_done"), sem("sums_copied"), sem("w_done"), sem("acc_done")
        h_done, turned, h_copied, based, base_added = (sem(n) for n in ("h_done", "turned", "h_copied", "based", "base_added"))
        vec, var_done, dev_done, scaled, summed, total_out = (
            sem(n) for n in ("vec", "var_done", "dev_done", "scaled", "summed", "total_out"))

        act_norm, acc_read = sem("act_norm"), sem("acc_read")
        if norm:
            h_done_of = lambda g: (act_norm, g * 4 + size(g)[1])
        else:
            h_done_of = lambda g: (acc_read, g + 1)

        def added(seq):
            full = (GROUPS - 1) * rels
            return full * 4 + seq - full if isinstance(seq, int) and seq > full else seq * 4

        def is_past(value):
            return not isinstance(value, int) or value > 0

        def wait(eng, s, value):
            if is_past(value):
                eng.wait_ge(s, value)

        def size(g):
            return (1, 1) if isinstance(g, int) and g == GROUPS - 1 else (GB, 4)

        def bodies(eng, body):
            body(0, False)
            if rels > 1:
                with eng.Fori(1, GROUPS - 1) as i:
                    body(i, False)
            else:
                body(1, False)
                body(2, False)
            body((GROUPS - 1) // per_body, True)

        def products(i, last):
            for b in range(rels if last else spb):
                yield i * spb + b, b, i * per_body + b // rels, b % rels

        def tiles_of(g, k):
            return bass.ds(g * 4, k)

        def slot_of(g):
            return slot_by_group[0]

        slot_by_group = [0]

        def schedule(eng, at_seq, after_seq, turn, root_product):
            def behind(i, b, back):
                q = b - back
                body_i = i
                while q < 0:
                    q, body_i = q + spb, body_i - 1
                if isinstance(i, int) and body_i < 0:
                    return None
                return body_i * spb + q, q, body_i * per_body + q // rels, q % rels

            def ended(i, b, back):
                p = behind(i, b, back)
                if p is None or p[3] != rels - 1:
                    return None
                slot_by_group[0] = p[1] // rels
                return p[2]

            def body(i, last):
                for seq, b, g, r in products(i, last):
                    at_seq(i, seq, b, g)
                    p = behind(i, b, 1)
                    if p is not None:
                        after_seq(*p)
                    if root is not None:
                        g2 = ended(i, b, 2)
                        if g2 is not None:
                            turn(g2)
                        g3 = ended(i, b, 3)
                        if g3 is not None:
                            root_product(g3)
                if last:
                    end = rels
                    for b in range(end, end + 3):
                        if b == end:
                            after_seq(*behind(i, b, 1))
                        if root is not None:
                            for back, what in ((2, turn), (3, root_product)):
                                if b - back < end:
                                    gx = ended(i, b, back)
                                    if gx is not None:
                                        what(gx)
            bodies(eng, body)

        with nc.Block() as block:
            @block.sync
            def _(sync):
                if rank:
                    sync.dma_start(key_all[:, :], m["key_row"].rearrange("t p -> (t p)").unsqueeze(0).broadcast_to([P, T * P])) \
                        .then_inc(keys_in, 16)

                def body(i, last):
                    for seq, b, g, r in products(i, last):
                        n, _ = size(g)
                        for k in range(halves):
                            hb = b * halves + k
                            here = i * (spb * halves) + hb
                            if is_past(here - slots + 1):
                                wait_apart(sync, half_done, here - slots + 1)
                                if make_sum:
                                    wait_apart(sync, summed, here - slots + 1)
                            a0, a1 = HALVES[k % 2]
                            of = streams[k // 2].rearrange("(b p) c -> p b c", p=P)
                            sync.dma_start(slot[hb % slots][:, 0:n, 0:(a1 - a0) * NB],
                                           of[:, bass.ds(g * GB, n), (r * T + a0) * NB:(r * T + a1) * NB]) \
                                .then_inc(arrived[hb % slots], 16)
                bodies(sync, body)

            @block.tensor
            def _(pe):
                def aggregate(i, seq, b, g):
                    n, _ = size(g)
                    bank = psum[BANK[b]][:, 0:n * NB].rearrange("p (b n) -> p b n", n=NB)
                    wait(pe, sums_copied, seq - BACK[b] + 1)
                    for k in range(halves):
                        hb = b * halves + k
                        pe.wait_ge(arrived[hb % slots],
                                   i * (spb * halves // slots * 16) + (hb // slots + 1) * 16)
                        a0, a1 = HALVES[k % 2]
                        for a in range(a0, a1):
                            for part in range(2):
                                one = pe.matmul(bank, now[:, a, part, :],
                                                slot[hb % slots][:, 0:n, (a - a0) * NB:(a - a0 + 1) * NB],
                                                start=(k == 0 and a == 0 and part == 0),
                                                stop=(k == halves - 1 and a == T - 1 and part == 1))
                        one.then_inc(half_done, 1)

                def weigh(seq, b, g, r):
                    _, k = size(g)
                    pe.wait_ge(sums_copied, seq + 1)
                    wait(pe, acc_done, added(seq - BACK[b] + 1))
                    for t in range(k):
                        one = pe.matmul(psum[3 + BANK[b]][:, t * D:t * D + D], sums[BANK[b]][:, t * P:t * P + P],
                                        w[:, r, :], start=True, stop=True)
                    one.then_inc(w_done, 1)

                def turn(g):
                    _, k = size(g)
                    pe.wait_ge(*h_done_of(g))
                    wait(pe, h_copied, g)
                    for t in range(k):
                        one = pe.transpose(psum[6][:, t * P:t * P + P], hbuf[slot_of(g)][:, t, :], ident[:, :])
                    one.then_inc(turned, 1)

                def root_product(g):
                    _, k = size(g)
                    pe.wait_ge(h_copied, g + 1)
                    wait(pe, base_added, g)
                    for t in range(k):
                        one = pe.matmul(psum[7][:, t * D:t * D + D], h_t[:, t * P:t * P + P], root,
                                        start=True, stop=True)
                    one.then_inc(based, 1)

                schedule(pe, aggregate, weigh, turn, root_product)

            @block.scalar
            def _(act):
                def copy_sums(i, seq, b, g):
                    n, k = size(g)
                    act.wait_ge(half_done, (seq + 1) * halves)
                    wait(act, w_done, seq - BACK[b] + 1)
                    act.activation(sums[BANK[b]][:, 0:n * NB], psum[BANK[b]][:, 0:n * NB], ACT.Copy,
                                   scale=m["unscales"][:, number:number + 1]) \
                        .then_inc(sums_copied, 1)

                def normalise(seq, b, g, r):
                    if not norm or r != rels - 1:
                        return
                    _, k = size(g)
                    act.wait_ge(var_done, g + 1)
                    act.activation(deviation[:, 0:k], deviation[:, 0:k], ACT.Sqrt).then_inc(dev_done, 1)
                    act.wait_ge(scaled, g + 1)
                    for t in range(k):
                        act.activation(m["table_sb"][:, tiles_of(g, k), 0:D][:, t, :] if root is None else hbuf[b // rels][:, t, :],
                                       x_sb[:, tiles_of(g, k), :][:, t, :], ACT.Relu, scale=rstd[:, t:t + 1],
                                       bias=shift[:, t:t + 1]).then_inc(act_norm, 1)

                def copy_turned(g):
                    _, k = size(g)
                    act.wait_ge(turned, g + 1)
                    wait(act, based, g)
                    act.activation(h_t[:, 0:k * P], psum[6][:, 0:k * P], ACT.Copy).then_inc(h_copied, 1)

                schedule(act, copy_sums, normalise, copy_turned, lambda g: None)

            @block.vector
            def _(dve):
                per_step = (9 if norm else 0) + (2 if root is not None else 0)

                def begin(i, seq, b, g):
                    if rank and i is not GROUPS - 1:
                        if isinstance(seq, int) and seq == 0:
                            dve.wait_ge(keys_in, 16)
                        else:
                            dve.wait_ge(ranked, seq)
                        dve.tensor_scalar(above[:, :], key_all[:, :], m["key"][:, bass.ds(seq, 1)], None, ALU.is_gt, ALU.add,
                                          accum_out=m["place"][:, bass.ds(seq, 1)]).then_inc(ranked, 1)
                    if not make_sum:
                        return
                    r = b
                    n, _ = size(g)
                    for k in range(halves):
                        hb = b * halves + k
                        dve.wait_ge(arrived[hb % slots],
                                    i * (spb * halves // slots * 16) + (hb // slots + 1) * 16)
                        a0, a1 = HALVES[k]
                        to, of = total[k][:, 0:n, 0:(a1 - a0) * NB], slot[hb % slots][:, 0:n, 0:(a1 - a0) * NB]
                        if r == 0:
                            wait(dve, total_out, g * 32)
                            dve.tensor_copy(to, of).then_inc(summed, 1)
                        else:
                            dve.wait_ge(summed, i * (spb * halves) + hb - 1)
                            dve.tensor_tensor(to, to, of, ALU.add).then_inc(summed, 1)

                def add(seq, b, g, r):
                    _, k = size(g)
                    dve.wait_ge(w_done, seq + 1)
                    if r:
                        dve.wait_ge(acc_done, added(seq))
                    else:
                        wait(dve, acc_read, g)
                    for t in range(k):
                        dve.scalar_tensor_tensor(
                            acc[:, t, :], psum[3 + BANK[b]][:, t * D:t * D + D],
                            scale[:, tiles_of(g, k), r][:, t:t + 1] if len(scale.shape) == 3 else scale[:, tiles_of(g, k)][:, t:t + 1],
                            acc[:, t, :] if r else base[:, tiles_of(g, k), :][:, t, :],
                            ALU.mult, ALU.add).then_inc(acc_done, 1)
                    if r != rels - 1:
                        return
                    dve.wait_ge(acc_done, added(seq + 1))
                    mine = hbuf[b // rels]
                    if root is not None:
                        wait(dve, turned, g - per_body + 1)
                    v = Tally(dve, vec, g * per_step)
                    start = v.at
                    if norm:
                        xs = x_sb[:, tiles_of(g, k), :]
                        dve.tensor_tensor(xs, xs, acc[:, 0:k, :], ALU.add).then_inc(acc_read, 1)
                        wait_apart(dve, acc_read, g + 1)
                        layer_norm(dve, v, xs, stats, mean_var, k)
                        dve.tensor_scalar(deviation[:, 0:k], mean_var[:, 0:k, 1], EPS, None, ALU.add).then_inc(var_done, 1)
                        dve.wait_ge(dev_done, g + 1)
                        v.chain(dve.reciprocal(rstd[:, 0:k], deviation[:, 0:k]))
                        dve.scalar_tensor_tensor(shift[:, 0:k], mean_var[:, 0:k, 0], -1.0, rstd[:, 0:k],
                                                 ALU.mult, ALU.mult).then_inc(scaled, 1)
                        dve.wait_ge(act_norm, g * 4 + k)
                    else:
                        dve.tensor_scalar(mine[:, 0:k, :], acc[:, 0:k, :], 0.0, None, ALU.max).then_inc(acc_read, 1)
                        dve.wait_ge(acc_read, g + 1)
                    if root is not None:
                        split(dve, v, then[:, tiles_of(g, k), :, :], mine[:, 0:k, :], m["scales"][:, number + 1:number + 2])
                    if k == 4 and isinstance(start, int):
                        assert v.at - start == per_step

                def add_base(g):
                    _, k = size(g)
                    dve.wait_ge(based, g + 1)
                    dve.tensor_tensor(base[:, tiles_of(g, k), :],
                                      psum[7][:, 0:k * D].rearrange("p (t d) -> p t d", d=D),
                                      bias.unsqueeze(1).broadcast_to([P, k, D]), ALU.add).then_inc(base_added, 1)

                schedule(dve, begin, add, lambda g: None, add_base)

            if put_in_order:
                @block.gpsimd
                def _(pool):
                    pool.tensor_copy(m["place_i"][:, :], m["place"][:, 0:T]).then_inc(placed, 1)
                    pool.wait_ge(placed, 1)
                    for t in range(T):
                        pool.indirect_dma_start(m["order"], bass.IndirectOffsetOnAxis(m["place_i"][:, t:t + 1], 0),
                                                m["record"][:, t, :], None).then_inc(ordered, 16)
                    pool.wait_ge(ordered, 16 * T)
                    pool.dma_start(m["record_o"][:, :, :], m["order"].rearrange("(t p) c -> p t c", p=P)).then_inc(read_back, 16)
                    pool.wait_ge(read_back, 16)
                    pool.tensor_copy(m["node_o"][:, :], m["record_o"][:, :, 0]).then_inc(placed, 1)
                    pool.tensor_copy(m["at_edge"][:, :], m["record_o"][:, :, 2]).then_inc(placed, 1)
                    pool.wait_ge(placed, 3)
                    for t in range(T):
                        pool.indirect_dma_start(m["lists_o"][:, t, :], None, m["edge_code"],
                                                bass.IndirectOffsetOnAxis(m["at_edge"][:, t:t + 1], 0)).then_inc(lists_in, 16)
                    pool.wait_ge(lists_in, 16 * T)

            if make_sum:
                @block.gpsimd
                def _(pool):
                    def body(i, last):
                        n, _ = size(i)
                        pool.wait_ge(summed, i * 10 + 10)
                        for k, (a0, a1) in enumerate(HALVES):
                            pool.dma_start(m["sum_adj"].rearrange("(b p) c -> p b c", p=P)
                                           [:, bass.ds(i * GB, n), a0 * NB:a1 * NB],
                                           total[k][:, 0:n, 0:(a1 - a0) * NB]).then_inc(total_out, 16)
                    bodies(pool, body)
                    pool.wait_ge(total_out, 32 * GROUPS)


def transpose_sum(nc, m):
    psum, ident_h = m["psum"], m["ident_h"]
    CUT = 12
    UNITS = -(-T // 2)
    with stage(nc, "t_") as (sb, sem):

        part = [sb(f"in{i}", [P, GB, (T - CUT) * NB], HF) for i in range(2)]
        out = [sb(f"out{i}", [P, 2 * T, 4, NB], HF) for i in range(2)]
        loaded = [sem(f"loaded{i}") for i in range(2)]
        turned, by_act, by_dve = sem("turned"), sem("by_act"), sem("by_dve")
        stored = [sem(f"stored{i}") for i in range(2)]
        zeroed = sem("zeroed")
        HALF = ((0, CUT), (CUT, T))

        def size(g):
            return (1, 1) if isinstance(g, int) and g == GROUPS - 1 else (GB, 4)

        def past(value):
            return not isinstance(value, int) or value > 0

        def groups(eng, one):
            pair[0] = 0
            one(0, 0)
            one(1, 1)
            with eng.Fori(1, (GROUPS - 1) // 2) as i:
                pair[0] = i
                one(i * 2, 0)
                one(i * 2 + 1, 1)
            pair[0] = (GROUPS - 1) // 2
            one(GROUPS - 1, 0)

        def evacuate(eng, first_unit, done):
            def one(g, place):
                n, k = size(g)
                rows = P if n == GB else NB
                if past(pair[0]):
                    eng.wait_ge(stored[place], pair[0] * 16)
                if n < GB:
                    eng.wait_ge(zeroed, 1)
                for u in range(first_unit, UNITS, 2):
                    eng.wait_ge(turned, g * UNITS + (u + 1))
                    tiles = min(2, T - 2 * u)
                    of = psum[u % 8][:, :].bitcast(HF)[0:rows, 0:tiles * k * P].rearrange("p (a l e n) -> p a l e n", l=k, e=2, n=NB)
                    for a in range(tiles):
                        to = out[place][0:rows, 4 * u + 2 * a:4 * u + 2 * a + 2, 0:k, :].rearrange("p e l n -> p l e n")
                        if eng.engine == mybir.EngineType.DVE:
                            last = eng.tensor_copy(to, of[:, a])
                        else:
                            last = eng.activation(to, of[:, a], ACT.Copy)
                        last.then_inc(done, 1)
            return one

        pair = [0]
        ACT_PER, DVE_PER = 13, 12

        with nc.Block() as block:
            @block.sync
            def _(sync):
                def one(g, place):
                    n, _ = size(g)
                    for h, (a0, a1) in enumerate(HALF):
                        if past(g):
                            wait_apart(sync, turned, g * UNITS - (UNITS - CUT // 2 if h == 0 else 0))
                        sync.dma_start(part[h][:, 0:n, 0:(a1 - a0) * NB],
                                       m["sum_adj"].rearrange("(b p) c -> p b c", p=P)
                                       [:, bass.ds(g * GB, n), a0 * NB:a1 * NB]).then_inc(loaded[h], 16)
                groups(sync, one)

            @block.tensor
            def _(pe):
                def one(g, place):
                    n, k = size(g)
                    for u in range(UNITS):
                        h = int(2 * u >= CUT)
                        if u in (0, CUT // 2):
                            wait_apart(pe, loaded[h], g * 16 + 16)
                        back, group = (u - 8, g) if u >= 8 else ((u + 8, g - 1) if u + 8 < UNITS else (u, g - 1))
                        if past(group + 1):
                            s, per = (by_dve, DVE_PER) if u % 2 else (by_act, ACT_PER)
                            n_done = min(back // 2 * 2 + 2, per)
                            wait_apart(pe, s, group * per + n_done)
                        bank = psum[u % 8][:, :].bitcast(HF)
                        for a in range(2 * u, min(2 * u + 2, T)):
                            for c in range(k):
                                at = ((a - 2 * u) * k + c) * P
                                for e in range(min(2, n)):
                                    last = pe.transpose(bank[e * NB:e * NB + NB, at:at + P],
                                                        part[h][:, 2 * c + e, (a - HALF[h][0]) * NB:(a - HALF[h][0] + 1) * NB],
                                                        ident_h[:, :])
                        last.then_inc(turned, 1)
                groups(pe, one)

            @block.scalar
            def _(act):
                groups(act, evacuate(act, 0, by_act))

            @block.vector
            def _(dve):
                groups(dve, evacuate(dve, 1, by_dve))

            @block.gpsimd
            def _(pool):
                def one(g, place):
                    _, k = size(g)
                    if k == 1:
                        pool.wait_ge(stored[0], pair[0] * 16)
                        pool.memset(out[0][NB:P, :, 0, :], 0.0).then_inc(zeroed, 1)
                        pool.wait_ge(zeroed, 1)
                    pool.wait_ge(by_act, g * ACT_PER + ACT_PER)
                    pool.wait_ge(by_dve, g * DVE_PER + DVE_PER)
                    pool.dma_start(m["sum_adj_t"].rearrange("(b p) c -> p b c", p=P)
                                   [:, :, bass.ds(g * (4 * NB), k * NB)].rearrange("p b (l n) -> p b l n", n=NB),
                                   out[place][:, 0:BATCHES, 0:k, :]).then_inc(stored[place], 16)
                groups(pool, one)
                pool.wait_ge(stored[0], 16 * 4)
                pool.wait_ge(stored[1], 16 * 3)



def gyro_sum(nc, A, m):
    table_sb, table, edge_code, x_sb = (m[k] for k in ("table_sb", "table", "edge_code", "x_sb"))
    record_o, node_o, at_edge, lists = (m[k] for k in ("record_o", "node_o", "at_edge", "lists_o"))
    deg, rdeg = record_o[:, :, 1], record_o[:, :, 3]
    W = max(b - a for a, b in TILE_GROUPS)
    NG = len(TILE_GROUPS)
    BLOCK = KB // STEPS
    PAIR = 2
    with stage(nc, "g_") as (sb, sem):
        most, most_all = sb("most", [P, NG], FP), sb("most_all", [P, NG], FP)
        trips_f = sb("trips_f", [P, 2 * NG], FP)
        trips = sb("trips", [P, 2 * NG], I32)
        own = sb("own", [P, T, TW], FP)
        source = sb("source", [P, STEPS, W], I32)
        ring = sb("ring", [P, STEPS, W, RW], FP)
        junk = sb("junk", [P, PAIR, W, D], HF)
        squares = sb("squares", [P, T, D], HF)
        u, add = sb("u", [P, W, D], FP), sb("add", [P, W, D], FP)
        nth = sb("nth", [P, PAIR, W], FP)
        dot_h = sb("dot_h", [P, PAIR, W], FP)
        s0, s1, s2, s3, s4, p = (sb(f"s{i}", [P, PAIR, W], FP) for i in range(6))
        y = sb("y", [P, PAIR, 4, W], FP)
        z = sb("z", [P, 4, W], FP)
        za, zb = sb("za", [P, 4, W], FP), sb("zb", [P, 4, W], FP)
        ab = sb("ab", [P, 2, W], FP)
        dot_u, c0, c1, c2, c3, gamma = (sb(f"c{i}", [P, W], FP) for i in range(6))
        fin = sb("fin", [P, 13, T], FP)
        total = sb("total", [P, T, D], FP)

        vec, maxed, counted, sized = sem("vec"), sem("maxed"), sem("counted"), sem("sized")
        squared, stored, out_done, finished = sem("squared"), sem("stored"), sem("out_done"), sem("finished")
        edges_at, edge_next, src_ready, indexed = sem("edges_at"), sem("edge_next"), sem("src_ready"), sem("indexed")
        listed = [sem(f"listed{g}") for g in range(NG)]
        owned = [sem(f"owned{g}") for g in range(NG)]
        CHUNKS = 3
        gathered = [[sem(f"gathered{g}_{j}") for j in range(STEPS)] for g in range(NG)]
        freed, gammas, scaled, stepped, to_act, from_act = (
            sem(n) for n in ("freed", "gammas", "scaled", "stepped", "to_act", "from_act"))

        def walk(eng, begin, refill, body, end):
            eng.wait_ge(sized, 1)
            bodies_of = [eng.value_load(trips[0:1, g:g + 1], min_val=1, max_val=E // STEPS) for g in range(NG)]
            more_of = [eng.value_load(trips[0:1, NG + g:NG + g + 1], min_val=0, max_val=E // KB) for g in range(NG)]
            bodies, blocks = 0, 0
            for g in range(NG):
                begin(g)
                with eng.register(f"bodies_{g}") as reg:
                    eng.reg_mov(reg, bodies_of[g])
                    eng.reg_alu(reg, reg, BLOCK, ALU.min)
                    here = eng.snap(reg, min_val=1, max_val=BLOCK)
                    with eng.Fori(0, here) as it:
                        body(g, bodies + it, it, it)
                with eng.If(more_of[g] > 0):
                    with eng.Fori(0, more_of[g]) as again:
                        b = again + 1
                        refill(g, blocks + b, b)
                        with eng.register(f"more_{g}") as reg:
                            eng.reg_mov(reg, bodies_of[g] - b * BLOCK)
                            eng.reg_alu(reg, reg, BLOCK, ALU.min)
                            here = eng.snap(reg, min_val=1, max_val=BLOCK)
                            with eng.Fori(0, here) as it:
                                body(g, bodies + (b * BLOCK + it), b * BLOCK + it, it)
                end(g)
                bodies, blocks = bodies + bodies_of[g], blocks + more_of[g]

        def nothing(*_):
            pass

        with nc.Block() as block:
            @block.sync
            def _(sync):
                sync.wait_ge(squared, 1)
                sync.dma_start(table[:, 0:RW].rearrange("(t p) d -> p t d", p=P), table_sb[:, :, :]).then_inc(stored, 16)
                sync.dma_start(table[:, RW:TW].rearrange("(t p) d -> p t d", p=P), x_sb[:, :, :]).then_inc(stored, 16)
                sync.wait_ge(stored, 32)

            @block.gpsimd
            def _(pool):
                pool.wait_ge(maxed, 1)
                pool.partition_all_reduce(most_all[:, :], most[:, :], P, bass.bass_isa.ReduceOp.max).then_inc(counted, 1)
                pool.wait_ge(stored, 32)

                def begin(g):
                    a, b = TILE_GROUPS[g]
                    for t in range(a, b):
                        pool.indirect_dma_start(own[:, t, :], None, table, bass.IndirectOffsetOnAxis(node_o[:, t:t + 1], 0)) \
                            .then_inc(owned[g], 16)
                    if g == 0:
                        pool.wait_ge(src_ready, 1)

                def refill(g, blocks, b):
                    a, e = TILE_GROUPS[g]
                    wait_apart(pool, edges_at, blocks)
                    for t in range(a, e):
                        pool.indirect_dma_start(lists[:, t, :], None, edge_code,
                                                bass.IndirectOffsetOnAxis(at_edge[:, t:t + 1], 0)).then_inc(listed[g], 16)
                    pool.wait_ge(src_ready, blocks + 1)

                def body(g, count, local, it):
                    n = TILE_GROUPS[g][1] - TILE_GROUPS[g][0]
                    for j in range(STEPS):
                        pool.wait_ge(freed, count * STEPS + (j + 1))
                        pool.tensor_copy(source[:, j, 0:n], lists[:, TILE_GROUPS[g][0]:TILE_GROUPS[g][1], bass.ds(it * STEPS + j, 1)]
                                         .rearrange("p t o -> p (t o)")).then_inc(indexed, 1)
                        wait_apart(pool, indexed, count * STEPS + (j + 1))
                        for t in range(n):
                            pool.indirect_dma_start(ring[:, j, t, :], None, table,
                                                    bass.IndirectOffsetOnAxis(source[:, j, t:t + 1], 0)) \
                                .then_inc(gathered[g][j], 16)

                walk(pool, begin, refill, body, nothing)
                pool.wait_ge(finished, 1)
                for t in range(T):
                    pool.indirect_dma_start(A["out"], bass.IndirectOffsetOnAxis(node_o[:, t:t + 1], 0), total[:, t, :], None,
                                            bounds_check=N - 1, oob_is_err=False).then_inc(out_done, 16)
                pool.wait_ge(out_done, 16 * T)

            @block.scalar
            def _(act):
                def body(g, count, local, it):
                    n = TILE_GROUPS[g][1] - TILE_GROUPS[g][0]
                    for j in range(STEPS):
                        act.wait_ge(gammas, count * STEPS + (j + 1))
                        for c in range(CHUNKS):
                            for t in range(n * c // CHUNKS, n * (c + 1) // CHUNKS):
                                one = act.activation(add[:, t, :], ring[:, j, t, 0:D], ACT.Copy, scale=gamma[:, t:t + 1])
                            one.then_inc(scaled, 1)

                walk(act, nothing, nothing, body, nothing)
                act.wait_ge(to_act, 1)
                act.activation(fin[:, 1, :], fin[:, 0, :], ACT.Sqrt).then_inc(from_act, 1)
                act.wait_ge(to_act, 2)
                act.activation(fin[:, 4, :], fin[:, 3, :], ACT.Ln).then_inc(from_act, 1)
                act.wait_ge(to_act, 3)
                act.activation(fin[:, 5, :], fin[:, 4, :], ACT.Tanh, scale=0.5).then_inc(from_act, 1)

            @block.vector
            def _(dve):
                v = Tally(dve, vec)
                for g, (a, b) in enumerate(TILE_GROUPS):
                    v(dve.tensor_reduce(most[:, g:g + 1], deg[:, a:b], AX.X, ALU.max))
                v.settle()
                dve.memset(junk[:, 0, 0, 0:1], 0.0).then_inc(maxed, 1)
                dve.wait_ge(counted, 1)
                for g0, plus, least in ((0, STEPS - 1, STEPS), (NG, -1, 0)):
                    v(dve.tensor_scalar(trips_f[:, g0:g0 + NG], most_all[:, :], float(plus), float(least), ALU.add, ALU.max))
                v.settle()
                v.chain(dve.tensor_copy(trips[:, :], trips_f[:, :]))
                for g0, per in ((0, STEPS), (NG, KB)):
                    v(dve.tensor_scalar(trips[:, g0:g0 + NG], trips[:, g0:g0 + NG], per.bit_length() - 1, None,
                                        ALU.logical_shift_right))
                v.settle()
                dve.memset(junk[:, 0, 0, 1:2], 0.0).then_inc(sized, 1)
                v.chain(dve.memset(table_sb[:, :, D:RW], 0.0))
                v(dve.tensor_scalar(lists[:, :, :], lists[:, :, :], TYPE_BITS, None, ALU.logical_shift_right))
                v.settle()
                dve.memset(junk[:, 0, 0, 6:7], 0.0).then_inc(src_ready, 1)
                for t in range(T):
                    last = dve.tensor_tensor_reduce(out=squares[:, t, :], in0=table_sb[:, t, 0:D], in1=table_sb[:, t, 0:D],
                                                    scale=1.0, scalar=0.0, op0=ALU.mult, op1=ALU.add,
                                                    accum_out=table_sb[:, t, D:D + 1])
                last.then_inc(squared, 1)
                dve.wait_ge(squared, 1)
                for j in range(STEPS):
                    dve.memset(junk[:, 0, 0, 2 + j:3 + j], 0.0).then_inc(freed, 1)

                def begin(g):
                    a, b = TILE_GROUPS[g]
                    v(dve.memset(u[:, :, :], 0.0))
                    v(dve.memset(z[:, :, :], 0.0))
                    for j in range(PAIR):
                        v(dve.memset(nth[:, j, :], float(j)))
                    v.settle()
                    dve.wait_ge(owned[g], 16 * (b - a))

                def refill(g, blocks, b):
                    a, e = TILE_GROUPS[g]
                    n = e - a
                    edge = record_o[:, a:e, 2]
                    dve.tensor_scalar(edge, edge, float(KB), float(E), ALU.add, ALU.min).then_inc(edge_next, 1)
                    dve.wait_ge(edge_next, blocks)
                    dve.tensor_copy(at_edge[:, a:e], edge).then_inc(edges_at, 1)
                    dve.wait_ge(listed[g], b * (16 * n))
                    dve.tensor_scalar(lists[:, a:e, :], lists[:, a:e, :], TYPE_BITS, None, ALU.logical_shift_right).then_inc(src_ready, 1)

                def body(g, count, local, it):
                    a, b = TILE_GROUPS[g]
                    n = b - a
                    w = Tally(dve, stepped, count * BODY_COUNT)
                    h_n = own[:, a:b, :]
                    S = h_n[:, :, D].unsqueeze(1).broadcast_to([P, PAIR, n])
                    for q in range(STEPS // PAIR):
                        for j in range(PAIR):
                            dve.wait_ge(gathered[g][q * PAIR + j], local * (16 * n) + 16 * n)
                            for t in range(n):
                                one = dve.tensor_tensor_reduce(
                                    out=junk[:, j, t, :], in0=ring[:, q * PAIR + j, t, 0:D], in1=h_n[:, t, 0:D], scale=1.0,
                                    scalar=0.0, op0=ALU.mult, op1=ALU.add, accum_out=dot_h[:, j, t:t + 1])
                        w.chain(one)
                        s = ring[:, q * PAIR:(q + 1) * PAIR, 0:n, D]
                        g_ = dot_h[:, :, 0:n]
                        A1, sS, mask, negB, D1 = (x[:, :, 0:n] for x in (s0, s1, s2, s3, s4))
                        pp, qq = p[:, :, 0:n], y[:, :, 1, 0:n]
                        m_h, m_m = y[:, :, 0, 0:n], y[:, :, 3, 0:n]
                        w(dve.tensor_scalar(A1, g_, -2.0, 1.0, ALU.mult, ALU.add))
                        w(dve.tensor_tensor(sS, s, S, ALU.mult))
                        w(dve.tensor_tensor(mask, nth[:, :, 0:n], deg[:, a:b].unsqueeze(1).broadcast_to([P, PAIR, n]), ALU.is_lt))
                        w(dve.tensor_scalar(negB, s, -1.0, None, ALU.add))
                        w.settle()
                        w(dve.tensor_tensor(D1, A1, sS, ALU.add))
                        w(dve.tensor_scalar(nth[:, :, :], nth[:, :, :], float(PAIR), None, ALU.add))
                        w.settle()
                        w(dve.tensor_tensor(A1, A1, S, ALU.add))
                        w(dve.tensor_scalar(D1, D1, BALL_EPS, None, ALU.max))
                        w.settle()
                        w.chain(dve.reciprocal(D1, D1))
                        w.chain(dve.tensor_tensor(D1, D1, mask, ALU.mult))
                        w(dve.tensor_tensor(pp, A1, D1, ALU.mult))
                        w(dve.tensor_tensor(qq, negB, D1, ALU.mult))
                        w.settle()
                        w(dve.tensor_tensor(s0[:, :, 0:n], pp, g_, ALU.mult))
                        w(dve.tensor_tensor(s1[:, :, 0:n], qq, S, ALU.mult))
                        w(dve.tensor_tensor(s2[:, :, 0:n], pp, s, ALU.mult))
                        w(dve.tensor_tensor(s3[:, :, 0:n], qq, g_, ALU.mult))
                        w.settle()
                        w(dve.tensor_tensor(m_h, s0[:, :, 0:n], s1[:, :, 0:n], ALU.add))
                        w(dve.tensor_tensor(s2[:, :, 0:n], s2[:, :, 0:n], s3[:, :, 0:n], ALU.add))
                        w.settle()
                        w(dve.tensor_tensor(s0[:, :, 0:n], m_h, qq, ALU.mult))
                        w(dve.tensor_tensor(s1[:, :, 0:n], s2[:, :, 0:n], pp, ALU.mult))
                        w.settle()
                        w.chain(dve.tensor_tensor(m_m, s0[:, :, 0:n], s1[:, :, 0:n], ALU.add))

                        for j in range(PAIR):
                            k = q * PAIR + j
                            t_, w_, X, xy = (z[:, i, 0:n] for i in range(4))
                            alpha, beta = ab[:, 0, 0:n], ab[:, 1, 0:n]
                            for t in range(n):
                                one = dve.tensor_tensor_reduce(
                                    out=junk[:, j, t, :], in0=ring[:, k, t, 0:D], in1=u[:, t, :], scale=1.0,
                                    scalar=0.0, op0=ALU.mult, op1=ALU.add, accum_out=dot_u[:, t:t + 1])
                            w(one)
                            w(dve.tensor_tensor(c0[:, 0:n], w_, dot_h[:, j, 0:n], ALU.mult))
                            w(dve.tensor_tensor(c1[:, 0:n], y[:, j, 1, 0:n], t_, ALU.mult))
                            w(dve.tensor_tensor(c2[:, 0:n], X, y[:, j, 3, 0:n], ALU.mult))
                            w(dve.tensor_scalar(beta, X, -1.0, 1.0, ALU.mult, ALU.add))
                            w.settle()
                            w.chain(dve.tensor_tensor(c0[:, 0:n], c0[:, 0:n], dot_u[:, 0:n], ALU.add))
                            w.chain(dve.tensor_tensor(c0[:, 0:n], c0[:, 0:n], p[:, j, 0:n], ALU.mult))
                            w(dve.tensor_tensor(xy, c0[:, 0:n], c1[:, 0:n], ALU.add))
                            w(dve.tensor_tensor(y[:, j, 2, 0:n], c0[:, 0:n], c1[:, 0:n], ALU.add))
                            w.settle()
                            w(dve.scalar_tensor_tensor(alpha, xy, 2.0, y[:, j, 3, 0:n], ALU.mult, ALU.add))
                            w(dve.scalar_tensor_tensor(c3[:, 0:n], xy, 2.0, c2[:, 0:n], ALU.mult, ALU.add))
                            w.settle()
                            w(dve.tensor_scalar(alpha, alpha, 1.0, None, ALU.add))
                            w(dve.tensor_scalar(c3[:, 0:n], c3[:, 0:n], 1.0, BALL_EPS, ALU.add, ALU.max))
                            w.settle()
                            w.chain(dve.reciprocal(c3[:, 0:n], c3[:, 0:n]))
                            w.chain(dve.tensor_tensor(ab[:, :, 0:n], ab[:, :, 0:n],
                                                      c3[:, 0:n].unsqueeze(1).broadcast_to([P, 2, n]), ALU.mult))
                            dve.tensor_tensor(gamma[:, 0:n], beta, p[:, j, 0:n], ALU.mult).then_inc(gammas, 1)
                            w(dve.tensor_tensor(za[:, :, 0:n], z[:, :, 0:n], alpha.unsqueeze(1).broadcast_to([P, 4, n]), ALU.mult))
                            w(dve.tensor_tensor(zb[:, :, 0:n], y[:, j, :, 0:n], beta.unsqueeze(1).broadcast_to([P, 4, n]), ALU.mult))
                            w.settle()
                            w.chain(dve.tensor_tensor(z[:, :, 0:n], za[:, :, 0:n], zb[:, :, 0:n], ALU.add))
                            w.chain(dve.tensor_tensor(za[:, 0:2, 0:n], z[:, 2:4, 0:n], ab[:, :, 0:n], ALU.mult))
                            w.chain(dve.tensor_tensor(X, za[:, 0, 0:n], za[:, 1, 0:n], ALU.add))
                            for c in range(CHUNKS):
                                dve.wait_ge(scaled, count * (STEPS * CHUNKS) + (k * CHUNKS + c + 1))
                                for t in range(n * c // CHUNKS, n * (c + 1) // CHUNKS):
                                    one = dve.scalar_tensor_tensor(u[:, t, :], u[:, t, :], ab[:, 0, t:t + 1], add[:, t, :],
                                                                   ALU.mult, ALU.add)
                            one.then_inc(freed, 1)
                            dve.wait_ge(freed, count * STEPS + (STEPS + k + 1))
                    assert w.n == BODY_COUNT, w.n

                BODY_COUNT = (STEPS // PAIR) * 22 + STEPS * 20

                def end(g):
                    a, b = TILE_GROUPS[g]
                    for t in range(b - a):
                        v(dve.scalar_tensor_tensor(total[:, a + t, :], own[:, a + t, 0:D], z[:, 1, t:t + 1], u[:, t, :],
                                                   ALU.mult, ALU.add))
                    v.settle()
                    for t in range(b - a):
                        for j, (x, to) in enumerate(((total, 0), (own, 2))):
                            v(dve.tensor_tensor_reduce(out=junk[:, j, t, :], in0=total[:, a + t, :], in1=x[:, a + t, 0:D],
                                                       scale=1.0, scalar=0.0, op0=ALU.mult, op1=ALU.add,
                                                       accum_out=fin[:, to, a + t:a + t + 1]))
                    v.settle()

                walk(dve, begin, refill, body, end)
                square, norm, dot, ratio, log, tanh, zc, up, down, f, A_, B_, inside = (fin[:, i, :] for i in range(13))
                S = own[:, :, D]
                dve.tensor_scalar(square, square, 1e-30, None, ALU.max).then_inc(to_act, 1)
                dve.wait_ge(from_act, 1)
                v.chain(dve.tensor_scalar(zc, norm, BALL_EPS, float(np.float32(1.0 - BALL_EPS)), ALU.max, ALU.min))
                v(dve.tensor_scalar(up, zc, 1.0, None, ALU.add))
                v(dve.tensor_scalar(down, zc, -1.0, 1.0, ALU.mult, ALU.add))
                v.settle()
                v.chain(dve.reciprocal(down, down))
                dve.tensor_tensor(ratio, up, down, ALU.mult).then_inc(to_act, 1)
                v(dve.reciprocal(f, zc))
                v(dve.tensor_scalar(inside, norm, BALL_EPS, None, ALU.is_gt))
                v.settle()
                v.chain(dve.tensor_tensor(f, f, inside, ALU.mult))
                dve.wait_ge(from_act, 2)
                dve.tensor_tensor(log, log, rdeg, ALU.mult).then_inc(to_act, 1)
                dve.wait_ge(from_act, 3)
                v.chain(dve.tensor_tensor(f, f, tanh, ALU.mult))
                v(dve.tensor_tensor(dot, dot, f, ALU.mult))
                v(dve.tensor_tensor(square, square, f, ALU.mult))
                v.settle()
                v.chain(dve.tensor_tensor(square, square, f, ALU.mult))
                v(dve.tensor_scalar(dot, dot, 2.0, 1.0, ALU.mult, ALU.add))
                v(dve.tensor_tensor(down, S, square, ALU.mult))
                v.settle()
                v(dve.tensor_tensor(A_, dot, square, ALU.add))
                v(dve.tensor_tensor(down, down, dot, ALU.add))
                v(dve.tensor_scalar(B_, S, -1.0, 1.0, ALU.mult, ALU.add))
                v.settle()
                v.chain(dve.tensor_scalar(down, down, BALL_EPS, None, ALU.max))
                v.chain(dve.reciprocal(down, down))
                v(dve.tensor_tensor(A_, A_, down, ALU.mult))
                v(dve.tensor_tensor(B_, B_, down, ALU.mult))
                v.settle()
                v.chain(dve.tensor_tensor(B_, B_, f, ALU.mult))
                for t in range(T):
                    v(dve.scalar_tensor_tensor(total[:, t, :], total[:, t, :], B_[:, t:t + 1], own[:, t, RW:TW], ALU.mult, ALU.add))
                v.settle()
                for t in range(T):
                    one = dve.scalar_tensor_tensor(total[:, t, :], own[:, t, 0:D], A_[:, t:t + 1], total[:, t, :],
                                                   ALU.mult, ALU.add)
                one.then_inc(finished, 1)


_INS = ["x", "src", "dst", "edge_type_5", "L0_gnn_weights", "L0_gnn_roots", "L0_gnn_biases", "L1_gnn_W_self",
        "L1_gnn_b_self", "L1_gnn_W_neig", "L1_gnn_b_neig", "L2_gnn_W1_l", "L2_gnn_b1_l", "L2_gnn_W1_r",
        "L2_gnn_W2_l", "L2_gnn_b2_l", "L2_gnn_W2_r"]


def kernel(**inputs):
    import concourse.bacc as bacc
    from concourse.bass_utils import run_bass_kernel_spmd

    nc = bacc.Bacc("TRN2", target_bir_lowering=False, num_devices=1)
    arrays, handles = {}, {}
    for name in _INS:
        a = np.ascontiguousarray(inputs[name])
        arrays[f"in_{name}"] = a
        handles[name] = nc.dram_tensor(f"in_{name}", a.shape, mybir.dt.from_np(a.dtype), kind="ExternalInput").ap()
    handles["out"] = nc.dram_tensor("out_0", (N, D), FP, kind="ExternalOutput").ap()
    build(nc, handles)
    return run_bass_kernel_spmd(nc, [arrays], core_ids=[0]).results[0]["out_0"]
```

```python
import itertools
from contextlib import ExitStack, contextmanager

import concourse.bass as bass
import numpy as np
from concourse import mybir

N = 3125
E = 100000
D = 128
R = 5
P = 128
T = -(-N // P)
LAST = N - (T - 1) * P
EP = 125
EC = E // EP
KB = 64
HC = 20
NB = 64
SB = (T + 1) // 2
C = R * T
BATCHES = 2 * T - 1
GN = 512
GB = GN // NB
GROUPS = -(-N // GN)
OH = 32
TYPE_BITS = 3
RW = D + 4
TW = RW + D
STEPS = 4
TILE_GROUPS = ((0, 11, 3), (11, T, 7))
EPS = 1e-5
NORM_BOUND = 11.3
NORM_SCALE = 1024.0
BALL_EPS = 1e-7

DT = mybir.dt
FP, HF, I32 = DT.float32, DT.float16, DT.int32
ALU = mybir.AluOpType
ACT = mybir.ActivationFunctionType
AX = mybir.AxisListType


@contextmanager
def stage(nc, prefix):
    sems = []
    with ExitStack() as ctx:
        def sb(name, shape, dtype):
            return ctx.enter_context(nc.sbuf_tensor(prefix + name, shape, dtype))

        def sem(name):
            sems.append(nc.alloc_semaphore(prefix + name))
            return sems[-1]

        yield sb, sem
    nc.clear_and_free_semaphores(sems)
    nc.all_engine_barrier()


def wait_apart(eng, sem, value):
    eng.wait_ge(sem, value)
    if not isinstance(value, int):
        eng.sem_inc(APART[0], 1)


APART = [None]


class Gap:

    def __init__(self, tally, n, piece, k):
        self.tally, self.n, self.piece, self.k, self.t = tally, n, piece, k, 0

    def step(self):
        if self.t < self.n:
            self.piece(self.k, self.t)
            self.t += 1

    def settle(self):
        at = self.tally.at
        self.step()
        self.tally.settle(at)

    def chain(self, instruction):
        self.tally(instruction)
        self.settle()

    def finish(self):
        while self.t < self.n:
            self.step()
        self.tally.settle()


class Tally:

    def __init__(self, engine, sem, at=0):
        self.engine, self.sem, self.at, self.n = engine, sem, at, 0

    def __call__(self, instruction):
        self.at, self.n = self.at + 1, self.n + 1
        instruction.then_inc(self.sem, 1)
        return self.at

    def settle(self, at=None):
        self.engine.wait_ge(self.sem, self.at if at is None else at)

    def chain(self, instruction):
        self(instruction)
        self.settle()


def build(nc, A, upto=99):
    ctx = ExitStack()
    with ctx:
        def sb(name, shape, dtype):
            return ctx.enter_context(nc.sbuf_tensor(name, shape, dtype))

        def sem(name):
            return ctx.enter_context(nc.semaphore(name))

        def dram(name, shape, dtype):
            return nc.dram_tensor(name, shape, dtype, kind="Internal").ap()

        psum = [ctx.enter_context(nc.psum_tensor(f"bank{i}", [P, 512], FP)) for i in range(8)]

        edge_code = dram("edge_code", (E + KB, 1), I32)
        adj = dram("adj", (BATCHES * P, C * NB), HF)
        sum_adj = dram("sum_adj", (BATCHES * P, T * NB), HF)

        table = dram("table", (T * P, TW), FP)
        key_row = dram("key_row", (T, P), FP)
        overflow_rows = dram("overflow_rows", (T * P, 2 * D), HF)
        order = dram("order", (T * P, 4), FP)

        ident = sb("ident", [P, P], FP)
        ident_h = sb("ident_h", [P, P], HF)
        below = sb("below", [P, P], FP)
        ones = sb("ones", [P, P], FP)
        cnt = sb("cnt", [P, T, R], FP)
        deg = sb("deg", [P, T + 1], FP)
        rcnt = sb("rcnt", [P, T, R], FP)
        rdeg = sb("rdeg", [P, T], FP)
        first_edge = sb("first_edge", [P, T], I32)
        first_f = sb("first_f", [P, T], FP)
        x_sb = sb("x_sb", [P, T, D], FP)

        APART[0] = nc.alloc_semaphore("waits_apart")
        preprocess(nc, A, locals())
        if upto >= 1:
            build_adjacency(nc, A, locals())

        base = sb("base", [P, T, D], FP)
        parts = [sb(f"parts{i}", [P, T, 2, D], HF) for i in range(2)]
        scales = sb("scales", [P, 6], FP)
        unscales = sb("unscales", [P, 6], FP)
        key = sb("key", [P, T + R], FP)
        place = sb("place", [P, T + R], FP)
        record = sb("record", [P, T, 4], FP)
        record_o = sb("record_o", [P, T, 4], FP)
        node_o = sb("node_o", [P, T], I32)
        place_i = sb("place_i", [P, T], I32)
        at_edge = sb("at_edge", [P, T], I32)
        lists_o = sb("lists_o", [P, T, KB], I32)
        one_col = sb("one_col", [P, T, 1], FP)
        past_kb = sb("past_kb", [P, 1], I32)
        w_rel = sb("w_rel", [P, 3 * R, D], FP)
        w_root = sb("w_root", [P, 3, D], FP)
        w_two = sb("w_two", [P, 4, D], FP)
        w_turned = sb("w_turned", [P, 2, D], FP)
        bias_0 = sb("bias_0", [P, 3, D], FP)
        bias_1 = sb("bias_1", [P, 2, D], FP)
        bias_2 = sb("bias_2", [P, 2, D], FP)

        m = locals()
        if upto >= 2:
            start_features(nc, A, m)
        layers = [
            dict(rels=R, stream=adj, scale=rcnt, w=w_rel[:, 0:R], root=w_root[:, 1], bias=bias_0[:, 1], make_sum=True),
            dict(rels=R, stream=adj, scale=rcnt, w=w_rel[:, R:2 * R], root=w_root[:, 2], bias=bias_0[:, 2], rank=True),
            dict(rels=R, stream=adj, scale=rcnt, w=w_rel[:, 2 * R:3 * R], root=w_turned[:, 0], bias=bias_1[:, 0], norm=True, put_in_order=True),
            dict(rels=1, stream=sum_adj, both_ways=True, scale=one_col, w=w_turned[:, 1:2], root=w_two[:, 1], bias=bias_2[:, 0], norm=True),
            dict(rels=1, stream=sum_adj, scale=rdeg, w=w_two[:, 0:1], root=w_two[:, 3], bias=bias_2[:, 1]),
            dict(rels=1, stream=sum_adj, scale=rdeg, w=w_two[:, 2:3], root=None, bias=None, norm=True),
        ]
        for n, layer in enumerate(layers):
            if n == 5:
                table_sb = sb("table_sb", [P, T, RW], FP)
                m["table_sb"] = table_sb
            if upto >= 3 + n:
                overflow_edges(nc, m, n, layer["rels"], layer.get("both_ways", False), layer["scale"], layer["w"])
                conv_layer(nc, m, n, **layer)
        if upto >= 9:
            gyro_sum(nc, A, m)


def preprocess(nc, A, m):
    psum, cnt, deg, rcnt, rdeg = m["psum"], m["cnt"], m["deg"], m["rcnt"], m["rdeg"]
    first_edge, first_f = m["first_edge"], m["first_f"]
    ident, ident_h, below, ones = m["ident"], m["ident_h"], m["below"], m["ones"]
    edge_code, x_sb = m["edge_code"], m["x_sb"]
    with stage(nc, "p_") as (sb, sem):

        dst_e = sb("dst_e", [EP, EC], I32)
        src_e = sb("src_e", [EP, EC], I32)
        typ_e = sb("typ_e", [EP, EC], I32)
        low_i = sb("low_i", [EP, EC], I32)
        tile_i = sb("tile_i", [EP, EC], I32)
        code_i = sb("code_i", [EP, EC], I32)
        low_b = sb("low_bf", [EP, EC], HF)
        code_b = sb("code_b", [EP, EC], HF)
        zero_i = sb("zero_i", [1, KB], I32)
        count_to = sb("count_to", [EP, P, HC], HF)
        hot_low = sb("hot_low", [EP, 2, P, HC], HF)
        hot_code = sb("hot_code", [EP, 2, C, HC], HF)
        tot = sb("tot", [P, T], FP)
        upto_tile = sb("upto_tile", [P, T], FP)

        made, loaded, coded, stored = sem("made"), sem("loaded"), sem("coded"), sem("stored")
        hot, used = sem("hot"), sem("used")
        cleared, x_in = sem("cleared"), sem("x_in")
        vec, deg_ready, prefix = sem("vec"), sem("deg"), sem("prefix")
        hist = psum[0][:, 0:C]
        total, lower = psum[1][:, 0:T], psum[2][:, 0:T]

        with nc.Block() as block:
            @block.sync
            def _(sync):
                sync.dma_start(dst_e[:, :], A["dst"].rearrange("(p c) -> p c", c=EC)).then_inc(loaded, 16)
                sync.dma_start(typ_e[:, :], A["edge_type_5"].rearrange("(p c) -> p c", c=EC)).then_inc(loaded, 16)
                sync.dma_start(src_e[:, :], A["src"].rearrange("(p c) -> p c", c=EC)).then_inc(loaded, 16)
                x, full = A["x"], (T - 1) * P
                for q in range(2):
                    sync.dma_start(x_sb[:, 12 * q:12 * q + 12, :],
                                   x[12 * P * q:12 * P * (q + 1), :].rearrange("(t p) d -> p t d", p=P)).then_inc(x_in, 16)
                sync.wait_ge(cleared, 1)
                sync.dma_start(x_sb[0:LAST, T - 1, :], x[full:N, :]).then_inc(x_in, 16)
                sync.wait_ge(coded, 1)
                sync.dma_start(edge_code[0:E, :].rearrange("(p c) o -> p (c o)", c=EC), src_e[:, :]).then_inc(stored, 16)
                sync.dma_start(edge_code[E:E + KB, :].rearrange("(a c) o -> a (c o)", a=1), zero_i[:, :]).then_inc(stored, 16)
                sync.wait_ge(stored, 32)
                sync.wait_ge(x_in, 48)

            @block.gpsimd
            def _(pool):
                pool.iota(count_to[:, :, :], [[1, P], [0, HC]], base=0, channel_multiplier=0,
                          allow_small_or_imprecise_dtypes=True).then_inc(made, 1)
                pool.memset(x_sb[:, T - 1, :], 0.0).then_inc(cleared, 1)
                pool.memset(zero_i[:, :], 0).then_inc(made, 1)
                pool.memset(ident[:, :], 0.0).then_inc(made, 1)
                pool.memset(ident_h[:, :], 0.0).then_inc(made, 1)
                pool.memset(below[:, :], 0.0).then_inc(made, 1)
                pool.memset(ones[:, :], 1.0).then_inc(made, 1)
                pool.memset(deg[:, T:T + 1], 0.0).then_inc(made, 1)
                pool.wait_ge(made, 7)
                for x in (ident, ident_h):
                    pool.affine_select(out=x[:, :], in_=x[:, :], compare_op=ALU.not_equal, fill=1.0,
                                       base=0, pattern=[[-1, P]], channel_multiplier=1).then_inc(made, 1)
                pool.affine_select(out=below[:, :], in_=below[:, :], compare_op=ALU.is_ge, fill=1.0,
                                   base=0, pattern=[[-1, P]], channel_multiplier=1).then_inc(made, 1)

            @block.vector
            def _(dve):
                v = Tally(dve, vec)
                dve.wait_ge(loaded, 48)
                v(dve.tensor_scalar(low_i[:, :], dst_e[:, :], P - 1, None, ALU.bitwise_and))
                v(dve.tensor_scalar(tile_i[:, :], dst_e[:, :], 7, None, ALU.logical_shift_right))
                v.settle()
                v(dve.tensor_copy(low_b[:, :], low_i[:, :]))
                v(dve.scalar_tensor_tensor(code_b[:, :], tile_i[:, :], float(R), typ_e[:, :], ALU.mult, ALU.add))
                v.chain(dve.scalar_tensor_tensor(code_i[:, :], src_e[:, :], float(1 << TYPE_BITS), typ_e[:, :],
                                                 ALU.mult, ALU.add))
                dve.wait_ge(made, 2)
                dve.tensor_copy(src_e[:, :], code_i[:, :]).then_inc(coded, 1)

                def make_hot(col, step, slot, wait):
                    if wait:
                        dve.wait_ge(used, step - 1)
                    dve.tensor_tensor(hot_low[:, slot], count_to[:, :, :],
                                      low_b[:, bass.ds(col, HC)].unsqueeze(1).broadcast_to([EP, P, HC]),
                                      ALU.is_equal).then_inc(hot, 1)
                    dve.tensor_tensor(hot_code[:, slot], count_to[:, 0:C, :],
                                      code_b[:, bass.ds(col, HC)].unsqueeze(1).broadcast_to([EP, C, HC]),
                                      ALU.is_equal).then_inc(hot, 1)

                make_hot(0, 0, 0, False)
                make_hot(HC, 1, 1, False)
                with dve.Fori(1, EC // HC // 2) as i:
                    make_hot(i * (2 * HC), i * 2, 0, True)
                    make_hot(i * (2 * HC) + HC, i * 2 + 1, 1, True)
                dve.wait_ge(used, EC // HC)
                v(dve.tensor_copy(cnt[:, :, :], hist.rearrange("p (t r) -> p t r", r=R)))
                v.chain(dve.tensor_reduce(deg[:, 0:T], hist.rearrange("p (t r) -> p t r", r=R), AX.X, ALU.add))
                dve.wait_ge(vec, v.at)
                v(dve.tensor_scalar(rcnt[:, :, :], cnt[:, :, :], 1.0, None, ALU.max))
                v(dve.tensor_scalar(rdeg[:, :], deg[:, 0:T], 1.0, None, ALU.max))
                dve.tensor_copy(upto_tile[:, :], deg[:, 0:T]).then_inc(deg_ready, 1)
                v.settle()
                v(dve.reciprocal(rcnt[:, :, :], rcnt[:, :, :]))
                v(dve.reciprocal(rdeg[:, :], rdeg[:, :]))
                dve.wait_ge(prefix, 2)
                v.chain(dve.tensor_copy(tot[:, :], total))
                v.chain(dve.tensor_tensor_scan(upto_tile[:, :], ones[:, 0:T], tot[:, :], 0.0, ALU.mult, ALU.add))
                v.chain(dve.tensor_tensor(upto_tile[:, :], upto_tile[:, :], tot[:, :], ALU.subtract))
                v.chain(dve.tensor_tensor(first_f[:, :], upto_tile[:, :], lower, ALU.add))
                v.chain(dve.tensor_copy(first_edge[:, :], first_f[:, :]))

            @block.tensor
            def _(pe):
                def count(step, slot, begin=False, end=False):
                    pe.wait_ge(hot, step * 2 + 2)
                    for c in range(HC):
                        last = pe.matmul(hist, hot_low[:, slot, :, c], hot_code[:, slot, :, c],
                                         start=begin and c == 0, stop=end and c == HC - 1)
                    last.then_inc(used, 1)

                count(0, 0, begin=True)
                count(1, 1)
                with pe.Fori(1, EC // HC // 2 - 1) as i:
                    count(i * 2, 0)
                    count(i * 2 + 1, 1)
                count(EC // HC - 2, 0)
                count(EC // HC - 1, 1, end=True)
                pe.wait_ge(made, 10)
                pe.wait_ge(deg_ready, 1)
                pe.matmul(total, ones[:, :], upto_tile[:, :], start=True, stop=True).then_inc(prefix, 1)
                pe.matmul(lower, below[:, :], upto_tile[:, :], start=True, stop=True).then_inc(prefix, 1)


def build_adjacency(nc, A, m):
    psum, deg, first_edge, edge_code, adj = m["psum"], m["deg"], m["first_edge"], m["edge_code"], m["adj"]
    ident_h = m["ident_h"]
    with stage(nc, "b_") as (sb, sem):

        lists = sb("lists", [P, 2 * SB, KB], I32)
        low_l = sb("low_l", [P, 2 * SB, KB], I32)
        tile_l = sb("tile_l", [P, 2 * SB, KB], I32)
        rel_l = sb("rel_l", [P, 2 * SB, KB], I32)
        valid = sb("valid", [P, 2 * SB, KB], FP)
        slot_no = sb("slot_no", [P, KB], FP)
        low_n = sb("low_n", [P, 2 * SB, KB], HF)
        code_f = sb("code_f", [P, 2 * SB, KB], FP)
        code_n = sb("code_n", [P, 2 * SB, KB], HF)
        low_t = sb("low_t", [P, SB, P], HF)
        code_t = sb("code_t", [P, SB, P], HF)
        count_to = sb("count_to_b", [P, P, OH], HF)
        hot_low = sb("hot_low_b", [P, 2, P, OH], HF)
        hot_code = sb("hot_code_b", [P, 2, C, OH], HF)
        batch = sb("batch", [P, 2, 2, C, NB], HF)

        made, fetched, turned = sem("made"), [sem(f"fetched{h}") for h in range(2)], sem("turned")
        turned_sb, hot, used = sem("turned_sb"), sem("hot"), sem("used")
        vec, by_act, by_dve = sem("vec"), sem("by_act"), sem("by_dve")
        store = [sem(f"store{h}") for h in range(2)]
        UNITS = 2 * OH // 4
        DVE_UNITS = (3, 8, 13)
        ACT_UNITS = tuple(u for u in range(UNITS) if u not in DVE_UNITS)
        LAST_DVE_UNITS = tuple(u for u in DVE_UNITS if u < 8)
        LAST_ACT_UNITS = tuple(u for u in ACT_UNITS if u < 8)
        turn_go, copied = sem("turn_go"), sem("copied")

        def evacuate(eng, s, k, units, first=False):
            q, h = k // 2, k % 2
            if h == 0 and not first:
                eng.wait_ge(store[q], s * 32)
            for u in units:
                before = s * 4 * UNITS + (k * UNITS if not (isinstance(s, int) and s == SB - 1) else k * (UNITS // 2))
                eng.wait_ge(used, before + (u + 1))
                at = h * OH + u % 8 * 4
                to = batch[:, q, u // 8, :, at:at + 4].rearrange("p c n -> p n c")
                of = psum[u % 8][:, 0:4 * C].rearrange("p (n c) -> p n c", c=C)
                if eng.engine == mybir.EngineType.DVE:
                    eng.tensor_copy(to, of).then_inc(by_dve, 1)
                else:
                    eng.activation(to, of, ACT.Copy).then_inc(by_act, 1)

        with nc.Block() as block:
            @block.gpsimd
            def _(pool):
                pool.iota(slot_no[:, :], [[1, KB]], base=0, channel_multiplier=0,
                          allow_small_or_imprecise_dtypes=True).then_inc(made, 1)
                pool.iota(count_to[:, :, :], [[1, P], [0, OH]], base=0, channel_multiplier=0,
                          allow_small_or_imprecise_dtypes=True).then_inc(made, 1)
                pool.memset(lists[:, T, :], 0).then_inc(made, 1)
                for t in range(T):
                    pool.indirect_dma_start(lists[:, t, :], None, edge_code,
                                            bass.IndirectOffsetOnAxis(first_edge[:, t:t + 1], 0)).then_inc(fetched[t // SB], 16)

            @block.vector
            def _(dve):
                v = Tally(dve, vec)
                dve.wait_ge(made, 3)
                for half, (t0, t1) in enumerate(((0, SB), (SB, 2 * SB))):
                    dve.wait_ge(fetched[half], 16 * (min(t1, T) - t0))
                    shape = [P, t1 - t0, KB]
                    v(dve.tensor_scalar(tile_l[:, t0:t1, :], lists[:, t0:t1, :], TYPE_BITS + 7, None, ALU.logical_shift_right))
                    v(dve.tensor_scalar(rel_l[:, t0:t1, :], lists[:, t0:t1, :], (1 << TYPE_BITS) - 1, None, ALU.bitwise_and))
                    v(dve.tensor_scalar(low_l[:, t0:t1, :], lists[:, t0:t1, :], TYPE_BITS, P - 1,
                                        ALU.logical_shift_right, ALU.bitwise_and))
                    v(dve.tensor_tensor(valid[:, t0:t1, :], slot_no[:, :].unsqueeze(1).broadcast_to(shape),
                                        deg[:, t0:t1].unsqueeze(2).broadcast_to(shape), ALU.is_lt))
                    v.settle()
                    v(dve.scalar_tensor_tensor(code_f[:, t0:t1, :], rel_l[:, t0:t1, :], float(T), tile_l[:, t0:t1, :],
                                               ALU.mult, ALU.add))
                    v(dve.tensor_copy(low_n[:, t0:t1, :], low_l[:, t0:t1, :]))
                    v.settle()
                    v.chain(dve.scalar_tensor_tensor(code_f[:, t0:t1, :], code_f[:, t0:t1, :], 1.0, valid[:, t0:t1, :],
                                                     ALU.add, ALU.mult))
                    v.chain(dve.tensor_scalar(code_n[:, t0:t1, :], code_f[:, t0:t1, :], -1.0, None, ALU.add))
                dve.nop().then_inc(turn_go, 1)
                for s in range(SB):
                    dve.wait_ge(turned, 2 * s + 2)
                    v(dve.tensor_copy(low_t[:, s, :], psum[2 * s % 8][:, 0:P // 2].bitcast(HF)))
                    dve.tensor_copy(code_t[:, s, :], psum[(2 * s + 1) % 8][:, 0:P // 2].bitcast(HF)).then_inc(copied, 1)
                v.settle()
                dve.wait_ge(copied, SB)

                def make_hot(step, s, k):
                    if not (isinstance(step, int) and step < 2):
                        dve.wait_ge(used, step * UNITS - UNITS)
                    at = k // 2 * NB + k % 2 * OH
                    for to, codes, n in ((hot_low, low_t, P), (hot_code, code_t, C)):
                        dve.tensor_tensor(to[:, k % 2], count_to[:, 0:n, :],
                                          codes[:, bass.ds(s, 1), at:at + OH].broadcast_to([P, n, OH]),
                                          ALU.is_equal).then_inc(hot, 1)

                def four_steps(s, first=False):
                    for k in range(4):
                        make_hot(s * 4 + (k + 1), s + (k + 1) // 4, (k + 1) % 4)
                        evacuate(dve, s, k, DVE_UNITS, first)

                make_hot(0, 0, 0)
                four_steps(0, True)
                with dve.Fori(1, SB - 1) as s:
                    four_steps(s)
                make_hot((SB - 1) * 4 + 1, SB - 1, 1)
                for k in range(2):
                    evacuate(dve, SB - 1, k, LAST_DVE_UNITS)

            @block.scalar
            def _(act):
                for k in range(4):
                    evacuate(act, 0, k, ACT_UNITS, True)
                with act.Fori(1, SB - 1) as s:
                    for k in range(4):
                        evacuate(act, s, k, ACT_UNITS)
                for k in range(2):
                    evacuate(act, SB - 1, k, LAST_ACT_UNITS)

            @block.tensor
            def _(pe):
                pe.wait_ge(turn_go, 1)
                for s in range(SB):
                    if s >= 4:
                        pe.wait_ge(copied, s - 3)
                    for n, x in enumerate((low_n, code_n)):
                        pe.transpose(psum[(2 * s + n) % 8][:, 0:P // 2].bitcast(HF),
                                     x[:, 2 * s:2 * s + 2, :].rearrange("p t k -> p (t k)"),
                                     ident_h[:, :]).then_inc(turned, 1)
                pe.wait_ge(copied, SB)

                def count(s, k, units, first=False):
                    step = s * 4 + k
                    pe.wait_ge(hot, step * 2 + 2)
                    for u in range(units):
                        if not (first and k == 0 and u < 8):
                            if u < 8:
                                last_u = u + 8 if not (isinstance(s, int) and s == SB - 1 and k == 1) else u
                                short = isinstance(s, int) and s == SB - 1 and k == 1
                                done = ((LAST_DVE_UNITS, LAST_ACT_UNITS) if short else (DVE_UNITS, ACT_UNITS))
                                dve_one = last_u in done[0]
                                sem_, mine, per = (by_dve, done[0], len(DVE_UNITS)) if dve_one else (by_act, done[1], len(ACT_UNITS))
                                pe.wait_ge(sem_, (step - 1) * per + (mine.index(last_u) + 1))
                            else:
                                last_u = u - 8
                                sem_, mine = (by_dve, DVE_UNITS) if last_u in DVE_UNITS else (by_act, ACT_UNITS)
                                pe.wait_ge(sem_, step * len(mine) + (mine.index(last_u) + 1))
                        j = u // 8
                        rows = slice(j * KB, j * KB + KB)
                        for n in range(4):
                            i = u % 8 * 4 + n
                            last = pe.matmul(psum[u % 8][:, n * C:n * C + C], hot_low[rows, k % 2, :, i],
                                             hot_code[rows, k % 2, :, i], start=True, stop=True)
                        last.then_inc(used, 1)

                for k in range(4):
                    count(0, k, UNITS, True)
                with pe.Fori(1, SB - 1) as s:
                    for k in range(4):
                        count(s, k, UNITS)
                for k in range(2):
                    count(SB - 1, k, UNITS // 2)

            @block.sync
            def _(sync):
                def put(s, q, tiles=2):
                    step = s * 4 + (q * 2 + 2)
                    if tiles == 2:
                        wait_apart(sync, by_dve, step * len(DVE_UNITS))
                        wait_apart(sync, by_act, step * len(ACT_UNITS))
                    else:
                        sync.wait_ge(by_dve, (SB - 1) * 4 * len(DVE_UNITS) + 2 * len(LAST_DVE_UNITS))
                        sync.wait_ge(by_act, (SB - 1) * 4 * len(ACT_UNITS) + 2 * len(LAST_ACT_UNITS))
                    for j in range(tiles):
                        sync.dma_start(adj[bass.ds(s * (4 * P) + (2 * j + q) * P, P), :],
                                       batch[:, q, j].rearrange("p c n -> p (c n)")).then_inc(store[q], 16)

                with sync.Fori(0, SB - 1) as s:
                    for q in range(2):
                        put(s, q)
                put(SB - 1, 0, 1)
                sync.wait_ge(store[0], 32 * (SB - 1) + 16)
                sync.wait_ge(store[1], 32 * (SB - 1))


def layer_norm(dve, v, x, stats, mean_var, tiles):
    for t in range(tiles):
        v(dve.bn_stats(stats[:, t, :], x[:, t, :]))
    wait_apart(dve, v.sem, v.at)
    for t in range(tiles):
        v(dve.bn_aggr(mean_var[:, t, :], stats[:, t, :]))
    v.settle()


def split(dve, v, parts, h, scale):
    v.chain(dve.tensor_scalar(parts[:, :, 0, :], h, scale, None, ALU.mult))
    v(dve.scalar_tensor_tensor(parts[:, :, 1, :], h, scale, parts[:, :, 0, :], ALU.mult, ALU.subtract))


def start_features(nc, A, m):
    x_sb, base, parts, psum, ident = m["x_sb"], m["base"], m["parts"], m["psum"], m["ident"]
    with stage(nc, "f_") as (sb, sem):

        stats = sb("stats", [P, T, 6], FP)
        mean_var = sb("mean_var", [P, T, 2], FP)
        deviation = sb("deviation", [P, T], FP)
        rstd = sb("rstd", [P, T], FP)
        shift = sb("shift", [P, T], FP)
        h = sb("h", [P, T, D], FP)
        h_t = sb("h_t", [P, T, P], FP)
        w_pair = sb("w_pair", [P, 2, D], FP)
        ws, vec, dev, scaled, normed = (sem(f"{n}") for n in ("ws", "vec", "dev", "scaled", "normed"))
        turned, copied, rooted, added = (sem(f"{n}") for n in ("turned", "copied", "rooted", "added"))
        most, most_all = sb("most", [P, 1], FP), sb("most_all", [P, 1], FP)
        filled = sem("filled")
        sizes = sb("sizes", [P, 3 * R + 3 + 2, D], FP)
        column = sb("column", [P, 3, D], FP)
        bound = sb("bound", [P, 3], FP)
        power_i = sb("power_i", [P, 3], I32)
        inverse_i = sb("inverse_i", [P, 3], I32)
        beyond = sb("beyond", [P, T], FP)
        key_t = sb("key_t", [T, P], FP)
        numbered, keyed, key_out = sem("numbered"), sem("keyed"), sem("key_out")
        sized, summed_w = sem("sized"), sem("summed_w")
        w_turns, w_copied = sem("w_turns"), sem("w_copied")
        QUADS = -(-T // 4)

        with nc.Block() as block:
            @block.sync
            def _(sync):
                sync.dma_start(m["w_root"][:, :, :], A["L0_gnn_roots"].rearrange("l d e -> d l e")).then_inc(ws, 16)
                sync.dma_start(m["w_rel"][:, :, :], A["L0_gnn_weights"].rearrange("l r d e -> d (l r) e")).then_inc(ws, 16)
                sync.wait_ge(keyed, 3)
                sync.dma_start(m["key_row"][:, :], key_t[:, :]).then_inc(key_out, 16)
                sync.wait_ge(key_out, 16)
                sync.wait_ge(ws, 16 * 13)

            @block.gpsimd
            def _(pool):
                pool.wait_ge(filled, 1)
                pool.partition_all_reduce(most_all[:, :], most[:, :], P, bass.bass_isa.ReduceOp.max).then_inc(filled, 1)
                pool.iota(m["record"][:, :, 0], [[P, T]], base=0, channel_multiplier=1,
                          allow_small_or_imprecise_dtypes=True).then_inc(numbered, 1)

            @block.scalar
            def _(act):
                act.dma_start(m["bias_0"][:, :, :], A["L0_gnn_biases"].unsqueeze(0).broadcast_to([P, 3, D])).then_inc(ws, 16)
                for n, name in enumerate(("L1_gnn_W_self", "L1_gnn_W_neig")):
                    act.dma_start(w_pair[:, n, :], A[name]).then_inc(ws, 16)
                for n, name in enumerate(("L2_gnn_W1_l", "L2_gnn_W1_r", "L2_gnn_W2_l", "L2_gnn_W2_r")):
                    act.dma_start(m["w_two"][:, n, :], A[name]).then_inc(ws, 16)
                for to, name in ((m["bias_1"][:, 0], "L1_gnn_b_self"), (m["bias_1"][:, 1], "L1_gnn_b_neig"),
                                 (m["bias_2"][:, 0], "L2_gnn_b1_l"), (m["bias_2"][:, 1], "L2_gnn_b2_l")):
                    act.dma_start(to, A[name].unsqueeze(0).broadcast_to([P, D])).then_inc(ws, 16)
                act.wait_ge(dev, 1)
                act.activation(deviation[:, :], deviation[:, :], ACT.Sqrt).then_inc(dev, 1)
                act.wait_ge(scaled, 1)
                for t in range(T):
                    act.activation(h[:, t, :], x_sb[:, t, :], ACT.Relu, scale=rstd[:, t:t + 1],
                                   bias=shift[:, t:t + 1]).then_inc(normed, 1)
                for q in range(QUADS):
                    n = min(4, T - 4 * q)
                    act.wait_ge(turned, q + 1)
                    act.activation(h_t[:, 4 * q:4 * q + n, :], psum[q % 4][:, 0:n * P].rearrange("p (t n) -> p t n", n=P),
                                   ACT.Copy).then_inc(copied, 1)
                act.wait_ge(w_turns, 2)
                act.activation(m["w_turned"][:, :, :], psum[7][:, 0:2 * P].rearrange("p (t n) -> p t n", n=P),
                               ACT.Copy).then_inc(w_copied, 1)

            @block.vector
            def _(dve):
                v = Tally(dve, vec)
                dve.tensor_reduce(most[:, :], m["deg"][:, 0:T], AX.X, ALU.max).then_inc(filled, 1)
                for x, value in ((m["scales"], NORM_SCALE), (m["unscales"], 1.0 / NORM_SCALE)):
                    v(dve.memset(x[:, :], value))
                v(dve.memset(m["one_col"][:, :, :], 1.0))
                record, key = m["record"], m["key"]
                v(dve.memset(key[:, :], 0.0))
                v(dve.tensor_copy(record[:, :, 1], m["deg"][:, 0:T]))
                v(dve.tensor_copy(record[:, :, 2], m["first_f"][:, :]))
                v(dve.tensor_copy(record[:, :, 3], m["rdeg"][:, :]))
                dve.wait_ge(numbered, 1)
                v(dve.tensor_scalar(beyond[:, :], record[:, :, 0], float(N), -4096.0, ALU.is_ge, ALU.mult))
                v.settle()
                v.chain(dve.tensor_scalar(key[:, 0:T], record[:, :, 1], 2000.0, 4096.0, ALU.min, ALU.mult))
                v.chain(dve.tensor_tensor(key[:, 0:T], key[:, 0:T], record[:, :, 0], ALU.add))
                dve.tensor_tensor(key[:, 0:T], key[:, 0:T], beyond[:, :], ALU.add).then_inc(keyed, 1)
                dve.wait_ge(keyed, 2)
                dve.tensor_copy(key_t[:, :], psum[5][0:T, 0:P]).then_inc(keyed, 1)
                layer_norm(dve, v, x_sb, stats, mean_var, T)
                dve.tensor_scalar(deviation[:, :], mean_var[:, :, 1], EPS, None, ALU.add).then_inc(dev, 1)
                dve.wait_ge(dev, 2)
                v.chain(dve.reciprocal(rstd[:, :], deviation[:, :]))
                dve.scalar_tensor_tensor(shift[:, :], mean_var[:, :, 0], -1.0, rstd[:, :], ALU.mult, ALU.mult).then_inc(scaled, 1)
                dve.wait_ge(ws, 16 * 13)
                for to, of, n in ((0, m["w_rel"], 3 * R), (3 * R, m["w_root"], 3), (3 * R + 3, m["w_two"], 2)):
                    v(dve.scalar_tensor_tensor(sizes[:, to:to + n, :], of[:, 0:n, :], -1.0, of[:, 0:n, :], ALU.mult, ALU.max))
                v.settle()
                for l in range(2):
                    v(dve.tensor_reduce(column[:, l, :], sizes[:, l * R:(l + 1) * R, :].rearrange("p r e -> p e r"), AX.X, ALU.add))
                v.settle()
                for l in range(2):
                    v(dve.tensor_tensor(column[:, l, :], column[:, l, :], sizes[:, 3 * R + l, :], ALU.add))
                dve.tensor_tensor(column[:, 2, :], sizes[:, 3 * R + 3, :], sizes[:, 3 * R + 4, :], ALU.add).then_inc(sized, 1)
                v.settle()
                dve.wait_ge(summed_w, 1)
                v.chain(dve.tensor_copy(column[:, :, :], psum[6][:, 0:3 * D].rearrange("p (l e) -> p l e", e=D)))
                for l, bias in enumerate((m["bias_0"][:, 0], m["bias_0"][:, 1], m["bias_2"][:, 0])):
                    size = sizes[:, l, :]
                    v(dve.scalar_tensor_tensor(size, bias, -1.0, bias, ALU.mult, ALU.max))
                v.settle()
                for l, of in ((0, NORM_BOUND), (2, NORM_BOUND), (1, bound[:, 0:1])):
                    v.chain(dve.scalar_tensor_tensor(sizes[:, l, :], column[:, l, :], of, sizes[:, l, :], ALU.mult, ALU.add))
                    v.chain(dve.tensor_reduce(bound[:, l:l + 1], sizes[:, l, :], AX.X, ALU.max))
                v.chain(dve.tensor_scalar(bound[:, :], bound[:, :], 2.0 ** -40, 2.0 ** 40, ALU.max, ALU.min))
                v.chain(dve.tensor_scalar(power_i[:, :], bound[:, :].bitcast(I32), 0x7F800000, None, ALU.bitwise_and))
                v.chain(dve.tensor_scalar(inverse_i[:, :], power_i[:, :], -1.0, float(254 << 23), ALU.mult, ALU.add))
                for at, l in ((1, 0), (2, 1), (5, 2)):
                    v(dve.tensor_scalar(m["scales"][:, at:at + 1], inverse_i[:, l:l + 1].bitcast(FP), 2.0 ** 14, None, ALU.mult))
                    v(dve.tensor_scalar(m["unscales"][:, at:at + 1], power_i[:, l:l + 1].bitcast(FP), 2.0 ** -14, None, ALU.mult))
                dve.wait_ge(normed, T)
                split(dve, v, parts[0][:, :, :, :], h[:, :, :], m["scales"][:, 0:1])
                for q in range(QUADS):
                    n = min(4, T - 4 * q)
                    dve.wait_ge(rooted, q + 1)
                    dve.tensor_tensor(base[:, 4 * q:4 * q + n, :],
                                      psum[4 + q % 2][:, 0:n * D].rearrange("p (t n) -> p t n", n=D),
                                      m["bias_0"][:, 0:1, :].broadcast_to([P, n, D]), ALU.add).then_inc(added, 1)
                v(dve.tensor_tensor(m["bias_1"][:, 0], m["bias_1"][:, 0], m["bias_1"][:, 1], ALU.add))
                dve.wait_ge(filled, 2)
                v(dve.tensor_scalar(m["past_kb"][:, :], most_all[:, :], -float(KB), 0.0, ALU.add, ALU.max))

            @block.tensor
            def _(pe):
                pe.wait_ge(keyed, 1)
                pe.transpose(psum[5][0:T, 0:P], m["key"][:, 0:T], ident[:, :]).then_inc(keyed, 1)
                pe.wait_ge(ws, 16 * 13)
                pe.wait_ge(sized, 1)
                pe.matmul(psum[6][:, 0:3 * D], m["ones"][:, :], column[:, :, :].rearrange("p l e -> p (l e)"),
                          start=True, stop=True).then_inc(summed_w, 1)
                for n in range(2):
                    pe.transpose(psum[7][:, n * P:n * P + P], w_pair[:, n, :], ident[:, :]).then_inc(w_turns, 1)
                for q in range(QUADS):
                    n = min(4, T - 4 * q)
                    pe.wait_ge(normed, 4 * q + n)
                    if q >= 4:
                        pe.wait_ge(copied, q - 3)
                    for t in range(n):
                        last = pe.transpose(psum[q % 4][:, t * P:t * P + P], h[:, 4 * q + t, :], ident[:, :])
                    last.then_inc(turned, 1)
                for q in range(QUADS):
                    n = min(4, T - 4 * q)
                    pe.wait_ge(copied, q + 1)
                    if q >= 2:
                        pe.wait_ge(added, q - 1)
                    for t in range(n):
                        last = pe.matmul(psum[4 + q % 2][:, t * D:t * D + D], h_t[:, 4 * q + t, :],
                                         m["w_root"][:, 0, :], start=True, stop=True)
                    last.then_inc(rooted, 1)


def overflow_edges(nc, m, number, rels, both_ways, scale, w):
    psum, base, ident, past_kb = m["psum"], m["base"], m["ident"], m["past_kb"]
    now, rows_dram, edge_code = m["parts"][number % 2], m["overflow_rows"], m["edge_code"]
    with stage(nc, f"o{number}_") as (sb, sem):
        edge_f, at = sb("edge_f", [P, T], FP), sb("at", [P, T], I32)
        codes, source = sb("codes", [P, T], I32), sb("source", [P, T], I32)
        type_i, type_f = sb("type_i", [P, T], I32), sb("type_f", [P, T], FP)
        kth, is_edge, coef = sb("kth", [P, T], FP), sb("is_edge", [P, T], FP), sb("coef", [P, T, rels], FP)
        rows = sb("rows", [P, T, 2, D], HF)
        features, share = sb("features", [P, T, D], FP), sb("share", [P, T, D], FP)
        sums = sb("sums", [P, T, rels, D], FP)
        one, one_t = sb("one", [P, rels, D], FP), sb("one_t", [P, rels, P], FP)
        if both_ways:
            source_f, local = sb("source_f", [P, T], FP), sb("local", [P, T], FP)
            count_to, hot = sb("count_to", [P, P], FP), sb("hot", [P, T, P], HF)
        tabled, vec, at_ready, coded, sources, fetched, rounds = (
            sem(n) for n in ("tabled", "vec", "at_ready", "coded", "sources", "fetched", "rounds"))
        at_scaled = sem("at_scaled")
        numbered, hots, back, picked, turned, copied, multiplied, added = (
            sem(n) for n in ("numbered", "hots", "back", "picked", "turned", "copied", "multiplied", "added"))

        with nc.Block() as block:
            @block.sync
            def _(sync):
                past = sync.value_load(past_kb[0:1, 0:1], min_val=0, max_val=E)
                with sync.If(past > 0):
                    sync.dma_start(rows_dram.rearrange("(t p) c -> p t c", p=P), now[:, :, :, :].rearrange("p t h d -> p t (h d)")) \
                        .then_inc(tabled, 16)
                    sync.wait_ge(tabled, 16)

            @block.gpsimd
            def _(pool):
                past = pool.value_load(past_kb[0:1, 0:1], min_val=0, max_val=E)
                with pool.If(past > 0):
                    if both_ways:
                        pool.iota(count_to[:, :], [[1, P]], base=0, channel_multiplier=0,
                                  allow_small_or_imprecise_dtypes=True).then_inc(numbered, 1)
                    pool.wait_ge(tabled, 16)
                    with pool.Fori(0, past) as k:
                        wait_apart(pool, at_ready, k + 1)
                        for t in range(T):
                            pool.indirect_dma_start(codes[:, t:t + 1], None, edge_code,
                                                    bass.IndirectOffsetOnAxis(at[:, t:t + 1], 0)).then_inc(coded, 16)
                        wait_apart(pool, sources, k + 1)
                        for t in range(T):
                            pool.indirect_dma_start(rows[:, t, :, :].rearrange("p h d -> p (h d)"), None, rows_dram,
                                                    bass.IndirectOffsetOnAxis(source[:, t:t + 1], 0)).then_inc(fetched, 16)

            @block.vector
            def _(dve):
                past = dve.value_load(past_kb[0:1, 0:1], min_val=0, max_val=E)
                with dve.If(past > 0):
                    v = Tally(dve, vec)
                    v(dve.memset(sums[:, :, :, :], 0.0))
                    v(dve.memset(kth[:, :], float(KB - 1)))
                    v(dve.tensor_scalar(edge_f[:, :], m["first_f"][:, :], float(KB - 1), float(E), ALU.add, ALU.min))
                    v.settle()
                    if both_ways:
                        dve.wait_ge(numbered, 1)
                    PER_ROUND = 7 + 3 * rels + (1 if both_ways else 0)
                    with dve.Fori(0, past) as k:
                        u = Tally(dve, rounds, k * PER_ROUND)
                        u.chain(dve.tensor_scalar(edge_f[:, :], edge_f[:, :], 1.0, float(E), ALU.add, ALU.min))
                        dve.tensor_copy(at[:, :], edge_f[:, :]).then_inc(at_ready, 1)
                        u(dve.tensor_scalar(kth[:, :], kth[:, :], 1.0, None, ALU.add))
                        dve.wait_ge(coded, k * (16 * T) + 16 * T)
                        dve.tensor_scalar(source[:, :], codes[:, :], TYPE_BITS, None, ALU.logical_shift_right).then_inc(sources, 1)
                        u(dve.tensor_scalar(type_i[:, :], codes[:, :], (1 << TYPE_BITS) - 1, None, ALU.bitwise_and))
                        u.settle()
                        u(dve.tensor_tensor(is_edge[:, :], kth[:, :], m["deg"][:, 0:T], ALU.is_lt))
                        u(dve.tensor_copy(type_f[:, :], type_i[:, :]))
                        u.settle()
                        for r in range(rels):
                            u(dve.tensor_scalar(coef[:, :, r], type_f[:, :], float(r) if rels > 1 else 0.0, None,
                                                ALU.is_equal if rels > 1 else ALU.is_ge))
                        u.settle()
                        u.chain(dve.tensor_tensor(coef[:, :, :], coef[:, :, :],
                                                  is_edge[:, :].unsqueeze(2).broadcast_to([P, T, rels]), ALU.mult))
                        dve.wait_ge(fetched, k * (16 * T) + 16 * T)
                        u.chain(dve.tensor_tensor(features[:, :, :], rows[:, :, 0, :], rows[:, :, 1, :], ALU.add))
                        for r in range(rels):
                            u.chain(dve.tensor_tensor(share[:, :, :], features[:, :, :],
                                                      coef[:, :, r].unsqueeze(2).broadcast_to([P, T, D]), ALU.mult))
                            u.chain(dve.tensor_tensor(sums[:, :, r, :], sums[:, :, r, :], share[:, :, :], ALU.add))
                        if both_ways:
                            dve.wait_ge(sources, k + 1)
                            dve.tensor_scalar(source_f[:, :], source[:, :], 1.0, None, ALU.add).then_inc(vec, 1)
                            dve.wait_ge(vec, 3 + k * (2 + 2 * T) + 1)
                            u.chain(dve.tensor_tensor(source_f[:, :], source_f[:, :], is_edge[:, :], ALU.mult))
                            dve.tensor_scalar(local[:, :], source_f[:, :], float(P) - 1.0, None, ALU.add).then_inc(vec, 1)
                            wait_apart(dve, vec, 3 + k * (2 + 2 * T) + 2)
                            with dve.Fori(0, T) as c:
                                dve.tensor_scalar(local[:, :], local[:, :], -float(P), None, ALU.add).then_inc(vec, 1)
                                dve.wait_ge(vec, k * (2 + 2 * T) + (c * 2 + 6))
                                dve.tensor_tensor(hot[:, :, :], local[:, :].unsqueeze(2).broadcast_to([P, T, P]),
                                                  count_to[:, :].unsqueeze(1).broadcast_to([P, T, P]), ALU.is_equal).then_inc(hots, 1)
                                dve.wait_ge(back, k * T + (c + 1))
                                dve.tensor_tensor(sums[:, bass.ds(c, 1), 0, :].rearrange("p o d -> p (o d)"),
                                                  sums[:, bass.ds(c, 1), 0, :].rearrange("p o d -> p (o d)"),
                                                  psum[0][:, 0:D], ALU.add).then_inc(vec, 1)
                                wait_apart(dve, vec, k * (2 + 2 * T) + (c * 2 + 7))
                        assert u.n == PER_ROUND, u.n
                    for r in range(rels):
                        factor = scale[:, :, r] if len(scale.shape) == 3 else scale[:, :]
                        dve.tensor_tensor(sums[:, :, r, :], sums[:, :, r, :], factor.unsqueeze(2).broadcast_to([P, T, D]),
                                          ALU.mult).then_inc(at_scaled, 1)
                    dve.wait_ge(at_scaled, rels)
                    dve.tensor_scalar(sums[:, :, :, :], sums[:, :, :, :], m["unscales"][:, number:number + 1], None,
                                      ALU.mult).then_inc(at_scaled, 1)
                    dve.wait_ge(at_scaled, rels + 1)
                    with dve.Fori(0, T) as t:
                        dve.tensor_copy(one[:, :, :], sums[:, bass.ds(t, 1), :, :].rearrange("p o r d -> p (o r) d")).then_inc(picked, 1)
                        dve.wait_ge(turned, t + 1)
                        dve.tensor_copy(one_t[:, 0:min(rels, 4), :], psum[0][:, 0:min(rels, 4) * P].rearrange("p (r n) -> p r n", n=P)) \
                            .then_inc(copied, 1)
                        if rels > 4:
                            dve.tensor_copy(one_t[:, 4:rels, :], psum[1][:, 0:(rels - 4) * P].rearrange("p (r n) -> p r n", n=P)) \
                                .then_inc(copied, 1)
                        dve.wait_ge(multiplied, t + 1)
                        dve.tensor_tensor(base[:, bass.ds(t, 1), :].rearrange("p o d -> p (o d)"),
                                          base[:, bass.ds(t, 1), :].rearrange("p o d -> p (o d)"),
                                          psum[2][:, 0:D], ALU.add).then_inc(added, 1)
                        wait_apart(dve, added, t + 1)

            @block.tensor
            def _(pe):
                past = pe.value_load(past_kb[0:1, 0:1], min_val=0, max_val=E)
                with pe.If(past > 0):
                    if both_ways:
                        with pe.Fori(0, past) as k:
                            with pe.Fori(0, T) as c:
                                pe.wait_ge(hots, k * T + (c + 1))
                                for t in range(T):
                                    for h in range(2):
                                        last = pe.matmul(psum[0][:, 0:D], hot[:, t, :], now[:, t, h, :],
                                                         start=t == 0 and h == 0, stop=t == T - 1 and h == 1)
                                last.then_inc(back, 1)
                    with pe.Fori(0, T) as t:
                        pe.wait_ge(picked, t + 1)
                        for r in range(rels):
                            last = pe.transpose(psum[r // 4][:, r % 4 * P:r % 4 * P + P], one[:, r, :], ident[:, :])
                        last.then_inc(turned, 1)
                        copies = 1 if rels <= 4 else 2
                        pe.wait_ge(copied, t * copies + copies)
                        for r in range(rels):
                            last = pe.matmul(psum[2][:, 0:D], one_t[:, r, :], w[:, r, :], start=r == 0, stop=r == rels - 1)
                        last.then_inc(multiplied, 1)


COLUMNS = 4
HALVES = ((0, 13), (13, T))
HW = 13


def conv_layer(nc, m, number, rels, stream, scale, w, root, bias, norm=False, make_sum=False, rank=False,
               put_in_order=False, both_ways=False):
    psum, ident, ident_h, base, x_sb = m["psum"], m["ident"], m["ident_h"], m["base"], m["x_sb"]
    now, then = m["parts"][number % 2], m["parts"][1 - number % 2]
    per_body = 1 if rels > 1 else 2
    spb = per_body * rels
    BANK, BACK = ((0, 1, 0, 1, 2), (3, 3, 2, 2, 5)) if rels == 5 else ((0, 1), (2, 2))
    halves = 2
    slots = 5 if rels == 5 else 4
    with stage(nc, f"l{number}_") as (sb, sem):

        slot = [sb(f"slot{i}", [P, GB, HW * NB], HF) for i in range(slots)]
        sums = [sb(f"sums{i}", [P, GN], FP) for i in range(3)]
        acc = sb("acc", [P, 4, D], FP)
        hbuf = [sb(f"h{i}", [P, 4, D], FP) for i in range(2)]
        h_t = sb("h_t", [P, GN], FP)
        stats = sb("stats", [P, 4, 6], FP)
        mean_var = sb("mean_var", [P, 4, 2], FP)
        deviation = sb("deviation", [P, 4], FP)
        rstd = sb("rstd", [P, 4], FP)
        shift = sb("shift", [P, 4], FP)
        total = [sb(f"total{i}", [P, GB, HW * NB], HF) for i in range(2)] if make_sum else None

        if both_ways:
            column = [sb(f"column{i}", [P, 2 * HW, 4 * NB], HF) for i in range(COLUMNS)]
            column_in = [sem(f"column_in{i}") for i in range(COLUMNS)]
            column_turned, mixed = sem("column_turned"), sem("mixed")
            mix_bank = [psum[2][:, :].bitcast(HF), psum[5][:, :].bitcast(HF)]
            pairs = [(k, a, min(a + 2, a1)) for k, (a0, a1) in enumerate(HALVES) for a in range(a0, a1, 2)]
        if rank:
            key_all = sb("key_all", [P, T * P], FP)
            above = sb("above", [P, T * P], HF)
            keys_in, ranked = sem("keys_in"), sem("ranked")
        if put_in_order:
            lists_in, ordered, read_back, placed = sem("lists_in"), sem("ordered"), sem("read_back"), sem("placed")
        arrived = [sem(f"arrived{i}") for i in range(slots)]
        half_done, sums_copied, w_done, acc_done = sem("half_done"), sem("sums_copied"), sem("w_done"), sem("acc_done")
        h_done, turned, h_copied, based, base_added = (sem(n) for n in ("h_done", "turned", "h_copied", "based", "base_added"))
        vec, var_done, dev_done, scaled, summed, total_out = (
            sem(n) for n in ("vec", "var_done", "dev_done", "scaled", "summed", "total_out"))

        act_norm, acc_read = sem("act_norm"), sem("acc_read")
        if norm:
            h_done_of = lambda g: (act_norm, g * 4 + size(g)[1])
        else:
            h_done_of = lambda g: (acc_read, g + 1)

        def added(seq):
            full = (GROUPS - 1) * rels
            return full * 4 + seq - full if isinstance(seq, int) and seq > full else seq * 4

        def is_past(value):
            return not isinstance(value, int) or value > 0

        def wait(eng, s, value):
            if is_past(value):
                eng.wait_ge(s, value)

        def size(g):
            return (1, 1) if isinstance(g, int) and g == GROUPS - 1 else (GB, 4)

        def bodies(eng, body):
            body(0, False)
            if rels > 1:
                with eng.Fori(1, GROUPS - 1) as i:
                    body(i, False)
            else:
                body(1, False)
                body(2, False)
            body((GROUPS - 1) // per_body, True)

        def products(i, last):
            for b in range(rels if last else spb):
                yield i * spb + b, b, i * per_body + b // rels, b % rels

        def tiles_of(g, k):
            return bass.ds(g * 4, k)

        def slot_of(g):
            return slot_by_group[0]

        def halves_of_pairs(g):
            return [x * 2 + k for x in range(g + 1) for k, _, _ in pairs]

        slot_by_group = [0]

        def schedule(eng, at_seq, after_seq, turn, root_product):
            def behind(i, b, back):
                q = b - back
                body_i = i
                while q < 0:
                    q, body_i = q + spb, body_i - 1
                if isinstance(i, int) and body_i < 0:
                    return None
                return body_i * spb + q, q, body_i * per_body + q // rels, q % rels

            def ended(i, b, back):
                p = behind(i, b, back)
                if p is None or p[3] != rels - 1:
                    return None
                slot_by_group[0] = p[1] // rels
                return p[2]

            def body(i, last):
                for seq, b, g, r in products(i, last):
                    at_seq(i, seq, b, g)
                    p = behind(i, b, 1)
                    if p is not None:
                        after_seq(*p)
                    if root is not None:
                        g2 = ended(i, b, 2)
                        if g2 is not None:
                            turn(g2)
                        g3 = ended(i, b, 3)
                        if g3 is not None:
                            root_product(g3)
                if last:
                    end = rels
                    for b in range(end, end + 3):
                        if b == end:
                            after_seq(*behind(i, b, 1))
                        if root is not None:
                            for back, what in ((2, turn), (3, root_product)):
                                if b - back < end:
                                    gx = ended(i, b, back)
                                    if gx is not None:
                                        what(gx)
            bodies(eng, body)

        with nc.Block() as block:
            @block.sync
            def _(sync):
                if rank:
                    sync.dma_start(key_all[:, :], m["key_row"].rearrange("t p -> (t p)").unsqueeze(0).broadcast_to([P, T * P])) \
                        .then_inc(keys_in, 16)

                def body(i, last):
                    for seq, b, g, r in products(i, last):
                        n, _ = size(g)
                        for k in range(halves):
                            hb = b * halves + k
                            here = i * (spb * halves) + hb
                            if both_ways:
                                q = g * 2 + k
                                if q >= COLUMNS:
                                    sync.wait_ge(column_turned, sum(x <= q - COLUMNS for x in halves_of_pairs(g)))
                                b0, b1 = HALVES[k][0] * 2, min(HALVES[k][1] * 2, BATCHES)
                                n_c = size(g)[1] * NB
                                sync.dma_start(column[q % COLUMNS][:, 0:b1 - b0, 0:n_c],
                                               stream.rearrange("(b p) c -> p b c", p=P)
                                               [:, b0:b1, g * 4 * NB:g * 4 * NB + n_c]).then_inc(column_in[q % COLUMNS], 16)
                            if is_past(here - slots + 1):
                                wait_apart(sync, half_done, here - slots + 1)
                                if make_sum:
                                    wait_apart(sync, summed, here - slots + 1)
                            a0, a1 = HALVES[k % 2]
                            of = stream.rearrange("(b p) c -> p b c", p=P)
                            sync.dma_start(slot[hb % slots][:, 0:n, 0:(a1 - a0) * NB],
                                           of[:, bass.ds(g * GB, n), (r * T + a0) * NB:(r * T + a1) * NB]) \
                                .then_inc(arrived[hb % slots], 16)
                bodies(sync, body)

            @block.tensor
            def _(pe):
                def turn_column(g, at):
                    _, n_c = size(g)
                    k, a, end = pairs[at]
                    q, done = g * 2 + k, g * len(pairs) + at
                    if a == HALVES[k][0]:
                        pe.wait_ge(column_in[q % COLUMNS], q // COLUMNS * 16 + 16)
                    if done >= 2:
                        pe.wait_ge(mixed, done - 1)
                    for t in range(a, end):
                        for c in range(n_c):
                            for e in range(min(2, BATCHES - 2 * t)):
                                out = mix_bank[done % 2][e * NB:e * NB + NB, ((t - a) * 4 + c) * P:((t - a) * 4 + c + 1) * P]
                                one = pe.transpose(out, column[q % COLUMNS][:, 2 * (t - HALVES[k][0]) + e, c * NB:c * NB + NB],
                                                   ident_h[:, :])
                    one.then_inc(column_turned, 1)

                def aggregate(i, seq, b, g):
                    if both_ways and g == 0:
                        for at in range(len(pairs)):
                            turn_column(0, at)
                    n, _ = size(g)
                    bank = psum[BANK[b]][:, 0:n * NB].rearrange("p (b n) -> p b n", n=NB)
                    wait(pe, sums_copied, seq - BACK[b] + 1)
                    for k in range(halves):
                        hb = b * halves + k
                        if not both_ways:
                            pe.wait_ge(arrived[hb % slots],
                                       i * (spb * halves // slots * 16) + (hb // slots + 1) * 16)
                        a0, a1 = HALVES[k % 2]
                        for a in range(a0, a1):
                            if both_ways and (a - a0) % 2 == 0:
                                at = [x[:2] for x in pairs].index((k, a))
                                if g < GROUPS - 1:
                                    turn_column(g + 1, at)
                                pe.wait_ge(mixed, g * len(pairs) + at + 1)
                            for part in range(2):
                                one = pe.matmul(bank, now[:, a, part, :],
                                                slot[hb % slots][:, 0:n, (a - a0) * NB:(a - a0 + 1) * NB],
                                                start=(k == 0 and a == 0 and part == 0),
                                                stop=(k == halves - 1 and a == T - 1 and part == 1))
                        one.then_inc(half_done, 1)

                def weigh(seq, b, g, r):
                    _, k = size(g)
                    pe.wait_ge(sums_copied, seq + 1)
                    wait(pe, acc_done, added(seq - BACK[b] + 1))
                    for t in range(k):
                        one = pe.matmul(psum[3 + BANK[b]][:, t * D:t * D + D], sums[BANK[b]][:, t * P:t * P + P],
                                        w[:, r, :], start=True, stop=True)
                    one.then_inc(w_done, 1)

                def turn(g):
                    _, k = size(g)
                    pe.wait_ge(*h_done_of(g))
                    wait(pe, h_copied, g)
                    for t in range(k):
                        one = pe.transpose(psum[6][:, t * P:t * P + P], hbuf[slot_of(g)][:, t, :], ident[:, :])
                    one.then_inc(turned, 1)

                def root_product(g):
                    _, k = size(g)
                    pe.wait_ge(h_copied, g + 1)
                    wait(pe, base_added, g)
                    for t in range(k):
                        one = pe.matmul(psum[7][:, t * D:t * D + D], h_t[:, t * P:t * P + P], root,
                                        start=True, stop=True)
                    one.then_inc(based, 1)

                schedule(pe, aggregate, weigh, turn, root_product)

            @block.scalar
            def _(act):
                def copy_sums(i, seq, b, g):
                    n, k = size(g)
                    act.wait_ge(half_done, (seq + 1) * halves)
                    wait(act, w_done, seq - BACK[b] + 1)
                    act.activation(sums[BANK[b]][:, 0:n * NB], psum[BANK[b]][:, 0:n * NB], ACT.Copy,
                                   scale=m["unscales"][:, number:number + 1]) \
                        .then_inc(sums_copied, 1)

                def normalise(seq, b, g, r):
                    if not norm or r != rels - 1:
                        return
                    _, k = size(g)
                    act.wait_ge(var_done, g + 1)
                    act.activation(deviation[:, 0:k], deviation[:, 0:k], ACT.Sqrt).then_inc(dev_done, 1)
                    act.wait_ge(scaled, g + 1)
                    for t in range(k):
                        act.activation(m["table_sb"][:, tiles_of(g, k), 0:D][:, t, :] if root is None else hbuf[b // rels][:, t, :],
                                       x_sb[:, tiles_of(g, k), :][:, t, :], ACT.Relu, scale=rstd[:, t:t + 1],
                                       bias=shift[:, t:t + 1]).then_inc(act_norm, 1)

                def copy_turned(g):
                    _, k = size(g)
                    act.wait_ge(turned, g + 1)
                    wait(act, based, g)
                    act.activation(h_t[:, 0:k * P], psum[6][:, 0:k * P], ACT.Copy).then_inc(h_copied, 1)

                schedule(act, copy_sums, normalise, copy_turned, lambda g: None)

            @block.vector
            def _(dve):
                per_step = (9 if norm else 0) + (2 if root is not None else 0)

                def mix(g):
                    n, _ = size(g)
                    for at, (k, a, end) in enumerate(pairs):
                        half, done = g * halves + k, g * len(pairs) + at
                        a0 = HALVES[k][0]
                        if a == a0:
                            dve.wait_ge(arrived[half % slots], half // slots * 16 + 16)
                        dve.wait_ge(column_turned, done + 1)
                        for t in range(a, end):
                            rows = P if t < T - 1 else NB
                            to = slot[half % slots][0:rows, 0:n, (t - a0) * NB:(t - a0 + 1) * NB]
                            turned_counts = mix_bank[done % 2][0:rows, (t - a) * 4 * P:(t - a) * 4 * P + n * NB]
                            one = dve.tensor_tensor(to, to, turned_counts.rearrange("p (b n) -> p b n", n=NB), ALU.add)
                        one.then_inc(mixed, 1)

                def begin(i, seq, b, g):
                    if rank and i is not GROUPS - 1:
                        if isinstance(seq, int) and seq == 0:
                            dve.wait_ge(keys_in, 16)
                        else:
                            dve.wait_ge(ranked, seq)
                        dve.tensor_scalar(above[:, :], key_all[:, :], m["key"][:, bass.ds(seq, 1)], None, ALU.is_gt, ALU.add,
                                          accum_out=m["place"][:, bass.ds(seq, 1)]).then_inc(ranked, 1)
                    if both_ways:
                        for ahead in ((0, 1) if g == 0 else (g + 1,) if g < GROUPS - 1 else ()):
                            mix(ahead)
                    if not make_sum:
                        return
                    r = b
                    n, _ = size(g)
                    for k in range(halves):
                        hb = b * halves + k
                        dve.wait_ge(arrived[hb % slots],
                                    i * (spb * halves // slots * 16) + (hb // slots + 1) * 16)
                        a0, a1 = HALVES[k]
                        to, of = total[k][:, 0:n, 0:(a1 - a0) * NB], slot[hb % slots][:, 0:n, 0:(a1 - a0) * NB]
                        if r == 0:
                            wait(dve, total_out, g * 32)
                            dve.tensor_copy(to, of).then_inc(summed, 1)
                        else:
                            dve.wait_ge(summed, i * (spb * halves) + hb - 1)
                            dve.tensor_tensor(to, to, of, ALU.add).then_inc(summed, 1)

                def add(seq, b, g, r):
                    _, k = size(g)
                    dve.wait_ge(w_done, seq + 1)
                    if r:
                        dve.wait_ge(acc_done, added(seq))
                    else:
                        wait(dve, acc_read, g)
                    for t in range(k):
                        dve.scalar_tensor_tensor(
                            acc[:, t, :], psum[3 + BANK[b]][:, t * D:t * D + D],
                            scale[:, tiles_of(g, k), r][:, t:t + 1] if len(scale.shape) == 3 else scale[:, tiles_of(g, k)][:, t:t + 1],
                            acc[:, t, :] if r else base[:, tiles_of(g, k), :][:, t, :],
                            ALU.mult, ALU.add).then_inc(acc_done, 1)
                    if r != rels - 1:
                        return
                    dve.wait_ge(acc_done, added(seq + 1))
                    mine = hbuf[b // rels]
                    if root is not None:
                        wait(dve, turned, g - per_body + 1)
                    v = Tally(dve, vec, g * per_step)
                    start = v.at
                    if norm:
                        xs = x_sb[:, tiles_of(g, k), :]
                        dve.tensor_tensor(xs, xs, acc[:, 0:k, :], ALU.add).then_inc(acc_read, 1)
                        wait_apart(dve, acc_read, g + 1)
                        layer_norm(dve, v, xs, stats, mean_var, k)
                        dve.tensor_scalar(deviation[:, 0:k], mean_var[:, 0:k, 1], EPS, None, ALU.add).then_inc(var_done, 1)
                        dve.wait_ge(dev_done, g + 1)
                        v.chain(dve.reciprocal(rstd[:, 0:k], deviation[:, 0:k]))
                        dve.scalar_tensor_tensor(shift[:, 0:k], mean_var[:, 0:k, 0], -1.0, rstd[:, 0:k],
                                                 ALU.mult, ALU.mult).then_inc(scaled, 1)
                        dve.wait_ge(act_norm, g * 4 + k)
                    else:
                        dve.tensor_scalar(mine[:, 0:k, :], acc[:, 0:k, :], 0.0, None, ALU.max).then_inc(acc_read, 1)
                        dve.wait_ge(acc_read, g + 1)
                    if root is not None:
                        split(dve, v, then[:, tiles_of(g, k), :, :], mine[:, 0:k, :], m["scales"][:, number + 1:number + 2])
                    if k == 4 and isinstance(start, int):
                        assert v.at - start == per_step

                def add_base(g):
                    _, k = size(g)
                    dve.wait_ge(based, g + 1)
                    dve.tensor_tensor(base[:, tiles_of(g, k), :],
                                      psum[7][:, 0:k * D].rearrange("p (t d) -> p t d", d=D),
                                      bias.unsqueeze(1).broadcast_to([P, k, D]), ALU.add).then_inc(base_added, 1)

                schedule(dve, begin, add, lambda g: None, add_base)

            if put_in_order:
                @block.gpsimd
                def _(pool):
                    pool.tensor_copy(m["place_i"][:, :], m["place"][:, 0:T]).then_inc(placed, 1)
                    pool.wait_ge(placed, 1)
                    for t in range(T):
                        pool.indirect_dma_start(m["order"], bass.IndirectOffsetOnAxis(m["place_i"][:, t:t + 1], 0),
                                                m["record"][:, t, :], None).then_inc(ordered, 16)
                    pool.wait_ge(ordered, 16 * T)
                    pool.dma_start(m["record_o"][:, :, :], m["order"].rearrange("(t p) c -> p t c", p=P)).then_inc(read_back, 16)
                    pool.wait_ge(read_back, 16)
                    pool.tensor_copy(m["node_o"][:, :], m["record_o"][:, :, 0]).then_inc(placed, 1)
                    pool.tensor_copy(m["at_edge"][:, :], m["record_o"][:, :, 2]).then_inc(placed, 1)
                    pool.wait_ge(placed, 3)
                    for t in range(T):
                        pool.indirect_dma_start(m["lists_o"][:, t, :], None, m["edge_code"],
                                                bass.IndirectOffsetOnAxis(m["at_edge"][:, t:t + 1], 0)).then_inc(lists_in, 16)
                    pool.wait_ge(lists_in, 16 * T)

            if make_sum:
                @block.gpsimd
                def _(pool):
                    def body(i, last):
                        n, _ = size(i)
                        pool.wait_ge(summed, i * 10 + 10)
                        for k, (a0, a1) in enumerate(HALVES):
                            pool.dma_start(m["sum_adj"].rearrange("(b p) c -> p b c", p=P)
                                           [:, bass.ds(i * GB, n), a0 * NB:a1 * NB],
                                           total[k][:, 0:n, 0:(a1 - a0) * NB]).then_inc(total_out, 16)
                    bodies(pool, body)
                    pool.wait_ge(total_out, 32 * GROUPS)


def gyro_sum(nc, A, m):
    table_sb, table, edge_code, x_sb = (m[k] for k in ("table_sb", "table", "edge_code", "x_sb"))
    record_o, node_o, at_edge, lists = (m[k] for k in ("record_o", "node_o", "at_edge", "lists_o"))
    deg, rdeg = record_o[:, :, 1], record_o[:, :, 3]
    W = max(b - a for a, b, _ in TILE_GROUPS)
    NG = len(TILE_GROUPS)
    BLOCK = KB // STEPS
    PAIR = 2
    with stage(nc, "g_") as (sb, sem):
        most, most_all = sb("most", [P, 2 * NG], FP), sb("most_all", [P, 2 * NG], FP)
        trips_f = sb("trips_f", [P, 3 * NG], FP)
        trips = sb("trips", [P, 3 * NG], I32)
        own = sb("own", [P, T, TW], FP)
        source = sb("source", [P, STEPS, W], I32)
        ring = sb("ring", [P, STEPS, W, RW], FP)
        junk = sb("junk", [P, PAIR, W, D], HF)
        junk_h = sb("junk_h", [P, STEPS, W, D], HF)
        squares = sb("squares", [P, T, D], HF)
        u, add = sb("u", [P, W, D], FP), sb("add", [P, W, D], FP)
        nth = sb("nth", [P, PAIR, W], FP)
        dot_h = sb("dot_h", [P, 2, PAIR, W], FP)
        s0, s1, s2, s3, s4, p = (sb(f"s{i}", [P, PAIR, W], FP) for i in range(6))
        y = sb("y", [P, PAIR, 4, W], FP)
        z = sb("z", [P, 4, W], FP)
        za, zb = sb("za", [P, 4, W], FP), sb("zb", [P, 4, W], FP)
        ab = sb("ab", [P, 2, W], FP)
        dot_u, c0, c1, c2, c3, gamma = (sb(f"c{i}", [P, W], FP) for i in range(6))
        fin = sb("fin", [P, 13, T], FP)
        total = sb("total", [P, T, D], FP)

        vec, maxed, counted, sized = sem("vec"), sem("maxed"), sem("counted"), sem("sized")
        squared, stored, out_done, finished = sem("squared"), sem("stored"), sem("out_done"), sem("finished")
        edges_at, edge_next, src_ready, indexed = sem("edges_at"), sem("edge_next"), sem("src_ready"), sem("indexed")
        listed = [sem(f"listed{g}") for g in range(NG)]
        owned = [sem(f"owned{g}") for g in range(NG)]
        CHUNKS = 3
        gathered = [[[sem(f"gathered{g}_{kind}{j}") for j in range(STEPS)] for kind in ("wide", "alone")] for g in range(NG)]
        freed, gammas, scaled, stepped, dotted, to_act, from_act = (
            sem(n) for n in ("freed", "gammas", "scaled", "stepped", "dotted", "to_act", "from_act"))

        def width(g, alone):
            a, b, fullest = TILE_GROUPS[g]
            return fullest if alone else b - a

        def clamped(eng, name, value, most):
            with eng.register(f"{name}_from") as reg, eng.register(name) as to:
                eng.reg_mov(reg, value)
                eng.reg_alu(reg, reg, most, ALU.min)
                eng.reg_alu(to, reg, 0, ALU.max)
                return eng.snap(to, min_val=0, max_val=most)

        numbers = itertools.count()

        def walk(eng, begin, refill, start, body, end):
            def run(g, alone, before, local, at, rest):
                start(g, alone, before, local)
                with eng.If(rest > 0):
                    with eng.Fori(0, rest) as it:
                        body(g, alone, before + it, local + it, at + it, False)
                body(g, alone, before + rest, local + rest, at + rest, True)

            eng.wait_ge(sized, 1)
            rest_of, more_of, wide_of = (
                [eng.value_load(trips[0:1, k * NG + g:k * NG + g + 1], min_val=0, max_val=E // per) for g in range(NG)]
                for k, per in enumerate((STEPS, KB, STEPS)))
            bodies, blocks = 0, 0
            for g in range(NG):
                begin(g)
                wide = clamped(eng, f"wide_{g}", wide_of[g], BLOCK - 1)
                run(g, False, bodies, 0, 0, wide)
                in_block = clamped(eng, f"in_block_{g}", rest_of[g], BLOCK - 1)
                alone = clamped(eng, f"alone_{g}", in_block - wide, BLOCK - 1)
                with eng.If(alone > 0):
                    rest = clamped(eng, f"alone_rest_{g}", alone - 1, BLOCK - 2)
                    run(g, True, bodies + (wide + 1), 0, wide + 1, rest)
                with eng.If(more_of[g] > 0):
                    with eng.Fori(0, more_of[g]) as again:
                        refill(g, blocks + (again + 1), again + 1)
                        rest = clamped(eng, f"more_{g}", rest_of[g] - (again + 1) * BLOCK, BLOCK - 1)
                        run(g, False, bodies + (again + 1) * BLOCK, wide + 1 + again * BLOCK, 0, rest)
                end(g)
                bodies, blocks = bodies + (rest_of[g] + 1), blocks + more_of[g]

        def nothing(*_):
            pass

        with nc.Block() as block:
            @block.sync
            def _(sync):
                sync.wait_ge(squared, 1)
                sync.dma_start(table[:, 0:RW].rearrange("(t p) d -> p t d", p=P), table_sb[:, :, :]).then_inc(stored, 16)
                sync.dma_start(table[:, RW:TW].rearrange("(t p) d -> p t d", p=P), x_sb[:, :, :]).then_inc(stored, 16)
                sync.wait_ge(stored, 32)

            @block.gpsimd
            def _(pool):
                pool.wait_ge(maxed, 1)
                pool.partition_all_reduce(most_all[:, :], most[:, :], P, bass.bass_isa.ReduceOp.max).then_inc(counted, 1)
                pool.wait_ge(stored, 32)

                def begin(g):
                    a, b, _ = TILE_GROUPS[g]
                    for t in range(a, b):
                        pool.indirect_dma_start(own[:, t, :], None, table, bass.IndirectOffsetOnAxis(node_o[:, t:t + 1], 0)) \
                            .then_inc(owned[g], 16)
                    if g == 0:
                        pool.wait_ge(src_ready, 1)

                def refill(g, blocks, b):
                    a, e, _ = TILE_GROUPS[g]
                    wait_apart(pool, edges_at, blocks)
                    for t in range(a, e):
                        pool.indirect_dma_start(lists[:, t, :], None, edge_code,
                                                bass.IndirectOffsetOnAxis(at_edge[:, t:t + 1], 0)).then_inc(listed[g], 16)
                    pool.wait_ge(src_ready, blocks + 1)

                def body(g, alone, count, local, it, last):
                    n, a = width(g, alone), TILE_GROUPS[g][0]
                    at = clamped(pool, f"at_{next(numbers)}", it, BLOCK - 1)
                    for j in range(STEPS):
                        pool.wait_ge(freed, count * STEPS + (j + 1))
                        pool.tensor_copy(source[:, j, 0:n], lists[:, a:a + n, bass.ds(at * STEPS + j, 1)]
                                         .rearrange("p t o -> p (t o)")).then_inc(indexed, 1)
                        wait_apart(pool, indexed, count * STEPS + (j + 1))
                        for t in range(n):
                            pool.indirect_dma_start(ring[:, j, t, :], None, table,
                                                    bass.IndirectOffsetOnAxis(source[:, j, t:t + 1], 0)) \
                                .then_inc(gathered[g][alone][j], 16)

                walk(pool, begin, refill, nothing, body, nothing)
                for g, (a, b, _) in enumerate(TILE_GROUPS):
                    pool.wait_ge(finished, g + 1)
                    for t in range(a, b):
                        pool.indirect_dma_start(A["out"], bass.IndirectOffsetOnAxis(node_o[:, t:t + 1], 0), total[:, t, :], None,
                                                bounds_check=N - 1, oob_is_err=False).then_inc(out_done, 16)
                pool.wait_ge(out_done, 16 * T)

            @block.scalar
            def _(act):
                def body(g, alone, count, local, it, last):
                    n = width(g, alone)
                    for j in range(STEPS):
                        act.wait_ge(gammas, count * STEPS + (j + 1))
                        for c in range(CHUNKS):
                            for t in range(n * c // CHUNKS, n * (c + 1) // CHUNKS):
                                one = act.activation(add[:, t, :], ring[:, j, t, 0:D], ACT.Copy, scale=gamma[:, t:t + 1])
                            one.then_inc(scaled, 1)

                def end(g):
                    a, b, _ = TILE_GROUPS[g]
                    act.wait_ge(to_act, 3 * g + 1)
                    act.activation(fin[:, 1, a:b], fin[:, 0, a:b], ACT.Sqrt).then_inc(from_act, 1)
                    act.wait_ge(to_act, 3 * g + 2)
                    act.activation(fin[:, 4, a:b], fin[:, 3, a:b], ACT.Ln).then_inc(from_act, 1)
                    act.wait_ge(to_act, 3 * g + 3)
                    act.activation(fin[:, 5, a:b], fin[:, 4, a:b], ACT.Tanh, scale=0.5).then_inc(from_act, 1)

                walk(act, nothing, nothing, nothing, body, end)

            @block.vector
            def _(dve):
                v = Tally(dve, vec)
                for g, (a, b, fullest) in enumerate(TILE_GROUPS):
                    v(dve.tensor_reduce(most[:, g:g + 1], deg[:, a:b], AX.X, ALU.max))
                    v(dve.tensor_reduce(most[:, NG + g:NG + g + 1], deg[:, a + fullest:b], AX.X, ALU.max))
                v.settle()
                dve.memset(junk[:, 0, 0, 0:1], 0.0).then_inc(maxed, 1)
                dve.wait_ge(counted, 1)
                for k, of in enumerate((0, 0, NG)):
                    v(dve.tensor_scalar(trips_f[:, k * NG:k * NG + NG], most_all[:, of:of + NG], -1.0, 0.0, ALU.add, ALU.max))
                v.settle()
                v.chain(dve.tensor_copy(trips[:, :], trips_f[:, :]))
                for k, per in enumerate((STEPS, KB, STEPS)):
                    v(dve.tensor_scalar(trips[:, k * NG:k * NG + NG], trips[:, k * NG:k * NG + NG], per.bit_length() - 1, None,
                                        ALU.logical_shift_right))
                v.settle()
                dve.memset(junk[:, 0, 0, 1:2], 0.0).then_inc(sized, 1)
                v.chain(dve.memset(table_sb[:, :, D:RW], 0.0))
                v(dve.tensor_scalar(lists[:, :, :], lists[:, :, :], TYPE_BITS, None, ALU.logical_shift_right))
                v.settle()
                dve.memset(junk[:, 0, 0, 6:7], 0.0).then_inc(src_ready, 1)
                for t in range(T):
                    last = dve.tensor_tensor_reduce(out=squares[:, t, :], in0=table_sb[:, t, 0:D], in1=table_sb[:, t, 0:D],
                                                    scale=1.0, scalar=0.0, op0=ALU.mult, op1=ALU.add,
                                                    accum_out=table_sb[:, t, D:D + 1])
                last.then_inc(squared, 1)
                dve.wait_ge(squared, 1)
                for j in range(STEPS):
                    dve.memset(junk[:, 0, 0, 2 + j:3 + j], 0.0).then_inc(freed, 1)

                def begin(g):
                    a, b, _ = TILE_GROUPS[g]
                    v(dve.memset(u[:, :, :], 0.0))
                    v(dve.memset(z[:, :, :], 0.0))
                    for j in range(PAIR):
                        v(dve.memset(nth[:, j, :], float(j)))
                    v.settle()
                    dve.wait_ge(owned[g], 16 * (b - a))

                def source_dot(g, alone, slot, t):
                    a = TILE_GROUPS[g][0]
                    one = dve.tensor_tensor_reduce(
                        out=junk_h[:, slot, t, :], in0=ring[:, slot, t, 0:D], in1=own[:, a + t, 0:D], scale=1.0,
                        scalar=0.0, op0=ALU.mult, op1=ALU.add, accum_out=dot_h[:, slot // PAIR, slot % PAIR, t:t + 1])
                    if t == width(g, alone) - 1:
                        one.then_inc(dotted, 1)

                def start(g, alone, count, local):
                    n = width(g, alone)
                    for slot in range(PAIR):
                        dve.wait_ge(gathered[g][alone][slot], local * (16 * n) + 16 * n)
                        for t in range(n):
                            source_dot(g, alone, slot, t)

                def refill(g, blocks, b):
                    a, e, _ = TILE_GROUPS[g]
                    n = e - a
                    edge = record_o[:, a:e, 2]
                    dve.tensor_scalar(edge, edge, float(KB), float(E), ALU.add, ALU.min).then_inc(edge_next, 1)
                    dve.wait_ge(edge_next, blocks)
                    dve.tensor_copy(at_edge[:, a:e], edge).then_inc(edges_at, 1)
                    dve.wait_ge(listed[g], b * (16 * n))
                    dve.tensor_scalar(lists[:, a:e, :], lists[:, a:e, :], TYPE_BITS, None, ALU.logical_shift_right).then_inc(src_ready, 1)

                def body(g, alone, count, local, it, last):
                    n = width(g, alone)
                    a, b = TILE_GROUPS[g][0], TILE_GROUPS[g][0] + n
                    w = Tally(dve, stepped, count * BODY_COUNT)
                    h_n = own[:, a:b, :]
                    S = h_n[:, :, D].unsqueeze(1).broadcast_to([P, PAIR, n])

                    def sum_dot(k, t):
                        one = dve.tensor_tensor_reduce(
                            out=junk[:, k % PAIR, t, :], in0=ring[:, k, t, 0:D], in1=u[:, t, :], scale=1.0,
                            scalar=0.0, op0=ALU.mult, op1=ALU.add, accum_out=dot_u[:, t:t + 1])
                        if t == n - 1:
                            w(one)

                    def next_dot(k, t):
                        ahead = (k + PAIR) % STEPS
                        if last and k + PAIR >= STEPS:
                            return
                        if t == 0:
                            dve.wait_ge(gathered[g][alone][ahead], (local + (k + PAIR) // STEPS) * (16 * n) + 16 * n)
                        source_dot(g, alone, ahead, t)

                    for q in range(STEPS // PAIR):
                        dve.wait_ge(dotted, count * STEPS + (q * PAIR + PAIR))
                        s = ring[:, q * PAIR:(q + 1) * PAIR, 0:n, D]
                        g_ = dot_h[:, q % 2, :, 0:n]
                        A1, sS, mask, negB, D1 = (x[:, :, 0:n] for x in (s0, s1, s2, s3, s4))
                        pp, qq = p[:, :, 0:n], y[:, :, 1, 0:n]
                        m_h, m_m = y[:, :, 0, 0:n], y[:, :, 3, 0:n]
                        gap = Gap(w, n, sum_dot, q * PAIR)
                        w(dve.tensor_scalar(A1, g_, -2.0, 1.0, ALU.mult, ALU.add))
                        w(dve.tensor_tensor(sS, s, S, ALU.mult))
                        w(dve.tensor_tensor(mask, nth[:, :, 0:n], deg[:, a:b].unsqueeze(1).broadcast_to([P, PAIR, n]), ALU.is_lt))
                        w(dve.tensor_scalar(negB, s, -1.0, None, ALU.add))
                        gap.settle()
                        w(dve.tensor_tensor(D1, A1, sS, ALU.add))
                        w(dve.tensor_scalar(nth[:, :, :], nth[:, :, :], float(PAIR), None, ALU.add))
                        gap.settle()
                        w(dve.tensor_tensor(A1, A1, S, ALU.add))
                        w(dve.tensor_scalar(D1, D1, BALL_EPS, None, ALU.max))
                        gap.settle()
                        gap.chain(dve.reciprocal(D1, D1))
                        gap.chain(dve.tensor_tensor(D1, D1, mask, ALU.mult))
                        w(dve.tensor_tensor(pp, A1, D1, ALU.mult))
                        w(dve.tensor_tensor(qq, negB, D1, ALU.mult))
                        gap.settle()
                        w(dve.tensor_tensor(s0[:, :, 0:n], pp, g_, ALU.mult))
                        w(dve.tensor_tensor(s1[:, :, 0:n], qq, S, ALU.mult))
                        w(dve.tensor_tensor(s2[:, :, 0:n], pp, s, ALU.mult))
                        w(dve.tensor_tensor(s3[:, :, 0:n], qq, g_, ALU.mult))
                        gap.settle()
                        w(dve.tensor_tensor(m_h, s0[:, :, 0:n], s1[:, :, 0:n], ALU.add))
                        w(dve.tensor_tensor(s2[:, :, 0:n], s2[:, :, 0:n], s3[:, :, 0:n], ALU.add))
                        gap.settle()
                        w(dve.tensor_tensor(s0[:, :, 0:n], m_h, qq, ALU.mult))
                        w(dve.tensor_tensor(s1[:, :, 0:n], s2[:, :, 0:n], pp, ALU.mult))
                        gap.settle()
                        w(dve.tensor_tensor(m_m, s0[:, :, 0:n], s1[:, :, 0:n], ALU.add))
                        gap.finish()

                        for j in range(PAIR):
                            k = q * PAIR + j
                            t_, w_, X, xy = (z[:, i, 0:n] for i in range(4))
                            alpha, beta = ab[:, 0, 0:n], ab[:, 1, 0:n]
                            if j > 0:
                                for t in range(n):
                                    sum_dot(k, t)
                            gap = Gap(w, n, next_dot, k)
                            w(dve.tensor_tensor(c0[:, 0:n], w_, dot_h[:, q % 2, j, 0:n], ALU.mult))
                            w(dve.tensor_scalar(beta, X, -1.0, 1.0, ALU.mult, ALU.add))
                            gap.settle()
                            w(dve.tensor_tensor(c0[:, 0:n], c0[:, 0:n], dot_u[:, 0:n], ALU.add))
                            w(dve.tensor_tensor(c1[:, 0:n], y[:, j, 1, 0:n], t_, ALU.mult))
                            gap.settle()
                            w(dve.tensor_tensor(c0[:, 0:n], c0[:, 0:n], p[:, j, 0:n], ALU.mult))
                            w(dve.tensor_tensor(c2[:, 0:n], X, y[:, j, 3, 0:n], ALU.mult))
                            gap.settle()
                            w(dve.tensor_tensor(xy, c0[:, 0:n], c1[:, 0:n], ALU.add))
                            w(dve.tensor_tensor(y[:, j, 2, 0:n], c0[:, 0:n], c1[:, 0:n], ALU.add))
                            gap.settle()
                            w(dve.scalar_tensor_tensor(c3[:, 0:n], xy, 2.0, c2[:, 0:n], ALU.mult, ALU.add))
                            w(dve.scalar_tensor_tensor(alpha, xy, 2.0, y[:, j, 3, 0:n], ALU.mult, ALU.add))
                            gap.settle()
                            w(dve.tensor_scalar(c3[:, 0:n], c3[:, 0:n], 1.0, BALL_EPS, ALU.add, ALU.max))
                            w(dve.tensor_scalar(alpha, alpha, 1.0, None, ALU.add))
                            gap.settle()
                            gap.chain(dve.reciprocal(c3[:, 0:n], c3[:, 0:n]))
                            w(dve.tensor_tensor(ab[:, :, 0:n], ab[:, :, 0:n],
                                                c3[:, 0:n].unsqueeze(1).broadcast_to([P, 2, n]), ALU.mult))
                            w.settle()
                            dve.tensor_tensor(gamma[:, 0:n], beta, p[:, j, 0:n], ALU.mult).then_inc(gammas, 1)
                            w(dve.tensor_tensor(za[:, :, 0:n], z[:, :, 0:n], alpha.unsqueeze(1).broadcast_to([P, 4, n]), ALU.mult))
                            w(dve.tensor_tensor(zb[:, :, 0:n], y[:, j, :, 0:n], beta.unsqueeze(1).broadcast_to([P, 4, n]), ALU.mult))
                            gap.settle()
                            gap.chain(dve.tensor_tensor(z[:, :, 0:n], za[:, :, 0:n], zb[:, :, 0:n], ALU.add))
                            gap.chain(dve.tensor_tensor(za[:, 0:2, 0:n], z[:, 2:4, 0:n], ab[:, :, 0:n], ALU.mult))
                            w(dve.tensor_tensor(X, za[:, 0, 0:n], za[:, 1, 0:n], ALU.add))
                            gap.finish()
                            for c in range(CHUNKS):
                                dve.wait_ge(scaled, count * (STEPS * CHUNKS) + (k * CHUNKS + c + 1))
                                for t in range(n * c // CHUNKS, n * (c + 1) // CHUNKS):
                                    one = dve.scalar_tensor_tensor(u[:, t, :], u[:, t, :], ab[:, 0, t:t + 1], add[:, t, :],
                                                                   ALU.mult, ALU.add)
                            one.then_inc(freed, 1)
                            wait_apart(dve, freed, count * STEPS + (STEPS + k + 1))
                    assert w.n == BODY_COUNT, w.n

                BODY_COUNT = (STEPS // PAIR) * 21 + STEPS * 20

                def end(g):
                    a, b, _ = TILE_GROUPS[g]
                    for t in range(b - a):
                        v(dve.scalar_tensor_tensor(total[:, a + t, :], own[:, a + t, 0:D], z[:, 1, t:t + 1], u[:, t, :],
                                                   ALU.mult, ALU.add))
                    v.settle()
                    for t in range(b - a):
                        for j, (x, to) in enumerate(((total, 0), (own, 2))):
                            v(dve.tensor_tensor_reduce(out=junk[:, j, t, :], in0=total[:, a + t, :], in1=x[:, a + t, 0:D],
                                                       scale=1.0, scalar=0.0, op0=ALU.mult, op1=ALU.add,
                                                       accum_out=fin[:, to, a + t:a + t + 1]))
                    v.settle()

                    square, norm, dot, ratio, log, tanh, zc, up, down, f, A_, B_, inside = (fin[:, i, a:b] for i in range(13))
                    S = own[:, a:b, D]
                    dve.tensor_scalar(square, square, 1e-30, None, ALU.max).then_inc(to_act, 1)
                    dve.wait_ge(from_act, 3 * g + 1)
                    v.chain(dve.tensor_scalar(zc, norm, BALL_EPS, float(np.float32(1.0 - BALL_EPS)), ALU.max, ALU.min))
                    v(dve.tensor_scalar(up, zc, 1.0, None, ALU.add))
                    v(dve.tensor_scalar(down, zc, -1.0, 1.0, ALU.mult, ALU.add))
                    v.settle()
                    v.chain(dve.reciprocal(down, down))
                    dve.tensor_tensor(ratio, up, down, ALU.mult).then_inc(to_act, 1)
                    v(dve.reciprocal(f, zc))
                    v(dve.tensor_scalar(inside, norm, BALL_EPS, None, ALU.is_gt))
                    v.settle()
                    v.chain(dve.tensor_tensor(f, f, inside, ALU.mult))
                    dve.wait_ge(from_act, 3 * g + 2)
                    dve.tensor_tensor(log, log, rdeg[:, a:b], ALU.mult).then_inc(to_act, 1)
                    dve.wait_ge(from_act, 3 * g + 3)
                    v.chain(dve.tensor_tensor(f, f, tanh, ALU.mult))
                    v(dve.tensor_tensor(dot, dot, f, ALU.mult))
                    v(dve.tensor_tensor(square, square, f, ALU.mult))
                    v.settle()
                    v.chain(dve.tensor_tensor(square, square, f, ALU.mult))
                    v(dve.tensor_scalar(dot, dot, 2.0, 1.0, ALU.mult, ALU.add))
                    v(dve.tensor_tensor(down, S, square, ALU.mult))
                    v.settle()
                    v(dve.tensor_tensor(A_, dot, square, ALU.add))
                    v(dve.tensor_tensor(down, down, dot, ALU.add))
                    v(dve.tensor_scalar(B_, S, -1.0, 1.0, ALU.mult, ALU.add))
                    v.settle()
                    v.chain(dve.tensor_scalar(down, down, BALL_EPS, None, ALU.max))
                    v.chain(dve.reciprocal(down, down))
                    v(dve.tensor_tensor(A_, A_, down, ALU.mult))
                    v(dve.tensor_tensor(B_, B_, down, ALU.mult))
                    v.settle()
                    v.chain(dve.tensor_tensor(B_, B_, f, ALU.mult))
                    for t in range(a, b):
                        v(dve.scalar_tensor_tensor(total[:, t, :], total[:, t, :], B_[:, t - a:t - a + 1], own[:, t, RW:TW], ALU.mult, ALU.add))
                    v.settle()
                    for t in range(a, b):
                        one = dve.scalar_tensor_tensor(total[:, t, :], own[:, t, 0:D], A_[:, t - a:t - a + 1], total[:, t, :],
                                                       ALU.mult, ALU.add)
                    one.then_inc(finished, 1)

                walk(dve, begin, refill, start, body, end)


_INS = ["x", "src", "dst", "edge_type_5", "L0_gnn_weights", "L0_gnn_roots", "L0_gnn_biases", "L1_gnn_W_self",
        "L1_gnn_b_self", "L1_gnn_W_neig", "L1_gnn_b_neig", "L2_gnn_W1_l", "L2_gnn_b1_l", "L2_gnn_W1_r",
        "L2_gnn_W2_l", "L2_gnn_b2_l", "L2_gnn_W2_r"]


def kernel(**inputs):
    import concourse.bacc as bacc
    from concourse.bass_utils import run_bass_kernel_spmd

    nc = bacc.Bacc("TRN2", target_bir_lowering=False, num_devices=1)
    arrays, handles = {}, {}
    for name in _INS:
        a = np.ascontiguousarray(inputs[name])
        arrays[f"in_{name}"] = a
        handles[name] = nc.dram_tensor(f"in_{name}", a.shape, mybir.dt.from_np(a.dtype), kind="ExternalInput").ap()
    handles["out"] = nc.dram_tensor("out_0", (N, D), FP, kind="ExternalOutput").ap()
    build(nc, handles)
    return run_bass_kernel_spmd(nc, [arrays], core_ids=[0]).results[0]["out_0"]
```
